# Optimizing a Trainium2 kernel written in Bass

```python
import numpy as np
import jax
import jax.numpy as jnp

def _softmax(x, axis=-1):
    return jax.nn.softmax(x, axis=axis)

def _gelu(x):
    return jax.nn.gelu(x, approximate=True)

def _silu(x):
    return jax.nn.silu(x)

def _sigmoid(x):
    return jax.nn.sigmoid(x)

def _layernorm(x, axis=-1, eps=1e-05):
    m = jnp.mean(x, axis=axis, keepdims=True)
    v = jnp.var(x, axis=axis, keepdims=True)
    return (x - m) / jnp.sqrt(v + eps)

def _scatter_add(tgt, idx, src, axis=0):
    return tgt.at[idx].add(src)

def _segment_sum(src, seg, n):
    return jax.ops.segment_sum(src, seg, n)
kernel_name = 'mk_gnn_ffn_d1_gnn_r32_db7183'

def setup_inputs(seed: int=0):
    np.random.seed(seed)
    _w = jnp.asarray

    def _rec_inputs():
        import jax
        import jax.numpy as jnp
        _gk = jax.random.key(seed)
        x = -0.0002117 + 1 * jax.random.normal(jax.random.fold_in(_gk, 1), (3125, 256), jnp.float32)
        src = jax.random.randint(jax.random.fold_in(_gk, 2), (50000,), 0, 3125, jnp.int32)
        dst = jnp.minimum((3125 * jax.random.uniform(jax.random.fold_in(_gk, 3), (50000,)) ** 2.0).astype(jnp.int32), 99999)
        _o = jnp.argsort(dst, stable=True)
        src = src[_o]
        dst = dst[_o]
        return (x, src, dst)
    x, src, dst = _rec_inputs()

    def _L0_gnn_setup():
        import jax, jax.numpy as jnp
        import numpy as np
        N = 3125
        E = 25000
        D_IN = 256
        D_H = 512

        def _gcn_prep(edge_index, n_nodes):
            loop = jnp.arange(n_nodes, dtype=edge_index.dtype)
            row = jnp.concatenate([edge_index[0], loop])
            col = jnp.concatenate([edge_index[1], loop])
            deg = jax.ops.segment_sum(jnp.ones_like(row, dtype=jnp.float32), row, num_segments=n_nodes)
            dinv = jax.lax.rsqrt(deg)
            norm = dinv[row] * dinv[col]
            return (row, col, norm)

        def _gcn_conv(x, W, b, row, col, norm, n_nodes):
            h = x @ W
            msg = h[col] * norm[:, None]
            out = jax.ops.segment_sum(msg, row, num_segments=n_nodes)
            return out + b
        key = jax.random.key(seed)
        ks = jax.random.split(key, 8)
        s_in = 1.0 / np.sqrt(D_IN)
        s_h = 1.0 / np.sqrt(D_H)
        return {'x': jax.random.normal(ks[0], (N, D_IN), jnp.float32), 'edge_index': jax.random.randint(ks[1], (2, E), 0, N, dtype=jnp.int64), 'W1': jax.random.normal(ks[2], (D_IN, D_H), jnp.float32) * s_in, 'b1': jnp.zeros((D_H,), jnp.float32), 'W2': jax.random.normal(ks[3], (D_H, D_H), jnp.float32) * s_h, 'b2': jnp.zeros((D_H,), jnp.float32), 'W3': jax.random.normal(ks[4], (D_H, D_H), jnp.float32) * s_h, 'b3': jnp.zeros((D_H,), jnp.float32), 'Wfc': jax.random.normal(ks[5], (D_H, D_IN), jnp.float32) * s_h, 'bfc': jnp.zeros((D_IN,), jnp.float32)}
    _L0_gnn_all = _L0_gnn_setup()
    _L0_gnn_in = {k: v for k, v in _L0_gnn_all.items() if k in ('W1', 'b1', 'W2', 'b2', 'W3', 'b3', 'Wfc', 'bfc')}
    del _L0_gnn_all

    def _L0_ffn_setup():
        import math
        import jax, jax.numpy as jnp
        import numpy as np
        CAPACITY_FACTOR = 1.25
        key = jax.random.key(seed)
        ks = jax.random.split(key, 5)
        B, L, D, F, E = (8, 256, 256, 1024, 8)
        h = jax.random.normal(ks[0], (B, L, D), dtype=jnp.float32)
        gate_w = jax.random.normal(ks[1], (D, E), dtype=jnp.float32) * 0.02
        gate_b = jnp.zeros((E,), dtype=jnp.float32)
        w1 = jax.random.normal(ks[2], (E, D, F), dtype=jnp.float32) * (1.0 / math.sqrt(D))
        b1 = jnp.zeros((E, F), dtype=jnp.float32)
        w2 = jax.random.normal(ks[3], (E, F, D), dtype=jnp.float32) * (1.0 / math.sqrt(F))
        b2 = jnp.zeros((E, D), dtype=jnp.float32)
        return {'h': h, 'gate_w': gate_w, 'gate_b': gate_b, 'w1': w1, 'b1': b1, 'w2': w2, 'b2': b2}
    _L0_ffn_all = _L0_ffn_setup()
    _L0_ffn_in = {k: v for k, v in _L0_ffn_all.items() if k in ('gate_w', 'gate_b', 'w1', 'b1', 'w2', 'b2')}
    del _L0_ffn_all
    return {'x': x, 'src': src, 'dst': dst, 'L0_gnn_W1': _L0_gnn_in['W1'], 'L0_gnn_b1': _L0_gnn_in['b1'], 'L0_gnn_W2': _L0_gnn_in['W2'], 'L0_gnn_b2': _L0_gnn_in['b2'], 'L0_gnn_W3': _L0_gnn_in['W3'], 'L0_gnn_b3': _L0_gnn_in['b3'], 'L0_gnn_Wfc': _L0_gnn_in['Wfc'], 'L0_gnn_bfc': _L0_gnn_in['bfc'], 'L0_ffn_gate_w': _L0_ffn_in['gate_w'], 'L0_ffn_gate_b': _L0_ffn_in['gate_b'], 'L0_ffn_w1': _L0_ffn_in['w1'], 'L0_ffn_b1': _L0_ffn_in['b1'], 'L0_ffn_w2': _L0_ffn_in['w2'], 'L0_ffn_b2': _L0_ffn_in['b2']}

def reference(x, src, dst, L0_gnn_W1, L0_gnn_b1, L0_gnn_W2, L0_gnn_b2, L0_gnn_W3, L0_gnn_b3, L0_gnn_Wfc, L0_gnn_bfc, L0_ffn_gate_w, L0_ffn_gate_b, L0_ffn_w1, L0_ffn_b1, L0_ffn_w2, L0_ffn_b2):
    import jax
    import jax.numpy as jnp

    def _L0_gnn_ref(x, edge_index, W1, b1, W2, b2, W3, b3, Wfc, bfc):
        import jax, jax.numpy as jnp
        import numpy as np
        N = 3125
        E = 25000
        D_IN = 256
        D_H = 512

        def _gcn_prep(edge_index, n_nodes):
            loop = jnp.arange(n_nodes, dtype=edge_index.dtype)
            row = jnp.concatenate([edge_index[0], loop])
            col = jnp.concatenate([edge_index[1], loop])
            deg = jax.ops.segment_sum(jnp.ones_like(row, dtype=jnp.float32), row, num_segments=n_nodes)
            dinv = jax.lax.rsqrt(deg)
            norm = dinv[row] * dinv[col]
            return (row, col, norm)

        def _gcn_conv(x, W, b, row, col, norm, n_nodes):
            h = x @ W
            msg = h[col] * norm[:, None]
            out = jax.ops.segment_sum(msg, row, num_segments=n_nodes)
            return out + b
        n = x.shape[0]
        row, col, norm = _gcn_prep(edge_index, n)
        h = jax.nn.relu(_gcn_conv(x, W1, b1, row, col, norm, n))
        h = jax.nn.relu(_gcn_conv(h, W2, b2, row, col, norm, n))
        h = jax.nn.relu(_gcn_conv(h, W3, b3, row, col, norm, n))
        return h @ Wfc + bfc

    def _L0_ffn_ref(h, gate_w, gate_b, w1, b1, w2, b2):
        import math
        import jax, jax.numpy as jnp
        import numpy as np
        CAPACITY_FACTOR = 1.25
        B, L, D = h.shape
        E = gate_w.shape[1]
        T = B * L
        C = max(1, math.ceil(CAPACITY_FACTOR * T / E))
        x = h.reshape(T, D)
        logits = x @ gate_w + gate_b
        probs = jax.nn.softmax(logits, axis=-1)
        idx = jnp.argmax(probs, axis=-1)
        prb = jnp.take_along_axis(probs, idx[:, None], axis=1)[:, 0]
        one_hot = jax.nn.one_hot(idx, E, dtype=jnp.float32)
        pos = (jnp.cumsum(one_hot, axis=0) * one_hot).sum(-1).astype(jnp.int32) - 1
        kept = pos < C
        pos_safe = jnp.where(kept, pos, C)
        buf = jnp.zeros((E, C, D), dtype=h.dtype).at[idx, pos_safe].set(x, mode='drop')
        hmid = jax.nn.relu(jnp.einsum('ecd,edf->ecf', buf, w1) + b1[:, None, :])
        ybuf = jnp.einsum('ecf,efd->ecd', hmid, w2) + b2[:, None, :]
        pos_g = jnp.minimum(pos, C - 1)
        y_tok = ybuf[idx, pos_g] * (prb * kept)[:, None]
        y = y_tok.reshape(B, L, D)
        y = jnp.nan_to_num(y, nan=0.0, posinf=10000.0, neginf=-10000.0)
        return y
    edge_index = jnp.stack([src, dst])
    x = x + _L0_gnn_ref(_layernorm(x, axis=-1), edge_index, L0_gnn_W1, L0_gnn_b1, L0_gnn_W2, L0_gnn_b2, L0_gnn_W3, L0_gnn_b3, L0_gnn_Wfc, L0_gnn_bfc)
    x = x + _L0_ffn_ref(_layernorm(x, axis=-1)[None], L0_ffn_gate_w, L0_ffn_gate_b, L0_ffn_w1, L0_ffn_b1, L0_ffn_w2, L0_ffn_b2)[0]
    return x

_drawn_inputs = setup_inputs


def setup_inputs(seed=0):
    import zlib

    import numpy as np

    out = dict(_drawn_inputs(seed))
    spreads = {'L0_gnn_b1': (0.0, 0.1),
     'L0_gnn_b2': (0.0, 0.1),
     'L0_gnn_b3': (0.0, 0.1),
     'L0_gnn_bfc': (0.0, 0.1),
     'L0_ffn_gate_b': (0.0, 0.1),
     'L0_ffn_b1': (0.0, 0.614),
     'L0_ffn_b2': (0.0, 0.435)}
    factors = {'L0_gnn_W1': 2.705}
    for name, (base, spread) in spreads.items():
        noise = np.random.default_rng([zlib.crc32(name.encode()), seed]).standard_normal(out[name].shape)
        drawn = base * np.exp(spread * noise) if base else spread * noise
        out[name] = jnp.asarray(drawn.astype(out[name].dtype))
    for name, factor in factors.items():
        out[name] = (out[name] * factor).astype(out[name].dtype)
    return out
```

```python
from contextlib import ExitStack

import numpy as np

import concourse.bass as bass
from concourse import mybir

F32 = mybir.dt.float32
F16 = mybir.dt.float16
I32 = mybir.dt.int32
U32 = mybir.dt.uint32
ALU = mybir.AluOpType
ACT = mybir.ActivationFunctionType
AX = mybir.AxisListType
RMAX = bass.bass_isa.ReduceOp.max

P = 128
N = 3125
D = 256
H = 512
NT = -(-N // P)
NP = NT * P
LAST = N - (NT - 1) * P

WD = 32
NW = NP // WD
WPT = P // WD
WCOL = NT * WD
KEYW = 1024
ETB = 4
ET = ETB * P
NOWHERE = 4095
GT = 4
HT = 2
OHW = WCOL + P
TBLK = 4
TURNS = -(-NT // TBLK)
PIECES = [range(2 * q, min(2 * q + 2, TURNS)) for q in range(WPT)]
MAXGROUPS = ET // GT
MAXSTEPS = 2 * NW * MAXGROUPS

KF = (D // P, H // P, H // P)
CH = 7
CS = [c * N // CH for c in range(CH + 1)]
GT5 = 5
NG = NT // GT5
GN = GT5 * P

NE = 8
F = 1024
FM = F // P
C = -(-5 * N // (4 * NE))
SLOTS = NE * C
ST = -(-C // P)
FMAX = float(np.finfo(np.float32).max)


def build(nc, io):
    E = io["src"].shape[0]
    EFULL = E // P
    EREST = E - EFULL * P
    with ExitStack() as ctx:
        def sb(name, shape, dt):
            return ctx.enter_context(nc.sbuf_tensor(name, shape, dt))

        def sem(name):
            return ctx.enter_context(nc.semaphore(name))

        t = {}
        t["AT"] = sb("AT", [P, NT, NP], F16)
        t["work"] = sb("work", [P, 13312], F32)
        t["ident"] = sb("ident", [P, P], F32)
        t["ident16"] = sb("ident16", [P, P], F16)
        t["ones16"] = sb("ones16", [P, 2], F16)
        t["zeros16"] = sb("zeros16", [P, 32], F16)
        for name, shape, dt in (
            ("stats", [P, NT, 6], F32), ("mean_var", [P, NT, 2], F32), ("rstd", [P, NT], F32),
            ("dinv", [P, NT], F32), ("logits", [P, NT, NE], F32), ("scale", [P, 3, 2], F32),
            ("stats2", [P, NT, 6], F32), ("mean_var2", [P, NT, 2], F32), ("var2", [P, NT], F32),
            ("root2", [P, NT], F32), ("rstd2", [P, NT], F32), ("newton2", [P, NT], F32), ("peak", [P, NT], F32),
            ("peak_1", [P, 1], F32), ("peak_all", [P, 1], F32), ("expo", [P, 3], I32),
            ("prob", [P, NT], F32), ("weight", [P, NT], F32), ("finite", [P, NE * ST], F32),
            ("finite_1", [P, 1], F32), ("bad", [P, 2], F32), ("bad_i", [P, 1], I32),
            ("scatter_idx", [P, NT], U32), ("gather_idx", [P, NT], U32),
        ):
            t[name] = sb(name, shape, dt)
        t["h_dram"] = nc.dram_tensor("h_dram", (H // P, P, NT, P), F32).ap()
        t["agg_dram"] = nc.dram_tensor("agg_dram", (H // P, P, N), F32).ap()
        t["slots_in"] = nc.dram_tensor("slots_in", (SLOTS, D), F32).ap()
        t["slots_out"] = nc.dram_tensor("slots_out", (SLOTS, D), F32).ap()
        t["w1_landed"] = [sem(f"w1_landed_{e}") for e in range(NE)]
        t["w2_landed"] = [sem("w2_landed_0"), sem("w2_landed_1")]
        t["b_landed"] = sem("b_landed")

        free_words, at = t["AT"][:, :, :].rearrange("p t n -> p (t n)").bitcast(F32), 0
        t["free"] = {}
        for name, words, pattern, sizes in (
            ("x2", NT * D, "p (t d) -> p t d", dict(t=NT)), ("xn2", NT * D, "p (t d) -> p t d", dict(t=NT)),
            ("wfc", 4 * D, "p (k n) -> p k n", dict(k=4)), ("bfc", D, None, {}),
            ("gate_w", 2 * NE, "p (k e) -> p k e", dict(k=2)), ("gate_b", NE, None, {}),
            ("h3t", 2 * 4 * P, "p (r k m) -> p r k m", dict(r=2, k=4)),
            ("xnt", 2 * 2 * P, "p (r k m) -> p r k m", dict(r=2, k=2)), ("zeros", D, None, {}), ("junk", D, None, {}),
            ("w1", NE * 2 * F, "p (e k f) -> p e k f", dict(e=NE, k=2)),
            ("w2", 2 * FM * D, "p (e k d) -> p e k d", dict(e=2, k=FM)), ("b2", NE * D, "p (e d) -> p e d", dict(e=NE)),
            ("b1_rows", P, None, {}), ("b1t", NE * FM, None, {}), ("tri", P // 2, None, {}), ("ones", P // 2, None, {}),
            ("e_less", NT * NE, "p (t e) -> p t e", dict(t=NT)), ("valid", NT * NE, "p (t e) -> p t e", dict(t=NT)),
        ):
            v = free_words[:, at:at + words]
            t["free"][name] = v.rearrange(pattern, **sizes) if pattern else v
            at += words
        assert at <= NT * NP // 2
        for name in ("tri", "ones"):
            t["free"][name] = t["free"][name].bitcast(F16)
        t["free"]["b1_rows"] = t["free"]["b1_rows"][0:NE * FM, :]

        adjacency(nc, io, t, E, EFULL, EREST)
        convolutions(nc, io, t)
        experts(nc, io, t)


def adjacency(nc, io, t, E, EFULL, EREST):
    with ExitStack() as ctx:
        def sb(name, shape, dt):
            return ctx.enter_context(nc.sbuf_tensor(name, shape, dt))

        def sem(name):
            return ctx.enter_context(nc.semaphore(name))

        AT, work, ident, ident16, ones16 = t["AT"], t["work"], t["ident"], t["ident16"], t["ones16"]
        zeros16 = t["zeros16"]
        stats, mean_var, rstd, dinv = t["stats"], t["mean_var"], t["rstd"], t["dinv"]

        counts = work[:, 0:3200].bitcast(F16).rearrange("p (r s d) -> p r s d", r=2, s=NT)
        row_sums = work[:, 3200:6400].rearrange("p (s d) -> p s d", s=NT)
        one_hots = work[:, 6400:6400 + GT * OHW // 2].bitcast(F16).rearrange("p (g c) -> p g c", g=GT)
        x_all = AT[:, :, :].rearrange("p t n -> p (t n)").bitcast(F32)[:, NT * NP // 2 - NT * D:].rearrange(
            "p (t d) -> p t d", t=NT)
        prep = AT[:, :, :].rearrange("p t n -> p (t n)").bitcast(I32)
        dst_i, src_i, key_i, low_i, tmp_i = (prep[:, n * ET:(n + 1) * ET] for n in range(5))
        prep_f = AT[:, :, :].rearrange("p t n -> p (t n)").bitcast(F32)
        key_f, low_f, win_f = (prep_f[:, n * ET:(n + 1) * ET] for n in range(5, 8))
        o = 8 * ET
        win_ids = prep_f[:, o:o + NW]
        tile_no = prep_f[:, o + NW:o + NW + 8]
        wmin = prep_f[:, o + NW + 8:o + NW + 12]
        wmax = prep_f[:, o + NW + 12:o + NW + 16]
        o += NW + 16
        from_lo = prep_f[:, o:o + NW * ETB].rearrange("p (w b) -> p w b", b=ETB)
        to_hi = prep_f[:, o + NW * ETB:o + 2 * NW * ETB].rearrange("p (w b) -> p w b", b=ETB)
        o += 2 * NW * ETB
        reach = prep_f[:, o:o + 2 * NW * ETB].rearrange("p (w b) -> p w b", b=ETB)
        reach_1 = prep_f[:, o + 2 * NW * ETB:o + 2 * NW * ETB + 2 * NW]
        reach_all = prep_f[:, o + 2 * NW * ETB + 2 * NW:o + 2 * NW * ETB + 4 * NW]
        lo_f = prep_f[:, o + 2 * NW * ETB + 4 * NW:o + 2 * NW * ETB + 5 * NW]
        n_f = prep_f[:, o + 2 * NW * ETB + 5 * NW:o + 2 * NW * ETB + 6 * NW]
        n_i = prep[:, o + 2 * NW * ETB + 6 * NW:o + 2 * NW * ETB + 7 * NW]

        edges = work[:, 8256:8256 + 2 * ET].rearrange("p (t k) -> p t k", k=2)
        iota16 = work[:, 9280:9280 + WCOL // 2].bitcast(F16)
        win_keys = sb("win_keys", [P, NW + WPT], F32)
        keys_now = sb("keys_now", [P, WPT], F32)
        ranges = sb("ranges", [P, NW, 2], I32)
        deg = sb("deg", [P, NT], F32)
        root = sb("root", [P, NT], F32)
        vroot = sb("vroot", [P, NT], F32)
        var = sb("var", [P, NT], F32)
        newton = sb("newton", [P, NT], F32)

        win_ps = ctx.enter_context(nc.psum_tensor("win_ps", [P, 2, 1024], F32))
        turn_ps = ctx.enter_context(nc.psum_tensor("turn_ps", [P, 2, TBLK * P], F32))
        prep_ps = ctx.enter_context(nc.psum_tensor("prep_ps", [P, 512], F32))

        edges_blank = sem("edges_blank")
        edges_in = sem("edges_in")
        x_blank = sem("x_blank")
        x_in = sem("x_in")
        pool_step = sem("pool_step")
        consts_set = sem("consts_set")
        dve_step = sem("dve_step")
        fields_set = sem("fields_set")
        turned = sem("turned")
        keys_set = sem("keys_set")
        reach_set = sem("reach_set")
        reach_max = sem("reach_max")
        ranges_set = sem("ranges_set")
        oh_ready = sem("oh_ready")
        oh_free = sem("oh_free")
        win_ready = sem("win_ready")
        win_out = sem("win_out")
        turn_ready = sem("turn_ready")
        turn_out = sem("turn_out")
        summed = sem("summed")
        node_set = sem("node_set")
        stats_set = sem("stats_set")
        roots_set = sem("roots_set")

        block = ctx.enter_context(nc.Block())

        @block.sync
        def _(sp):
            sp.wait_ge(edges_blank, 2)
            for name, ints in (("dst", dst_i), ("src", src_i)):
                full = EFULL // P * P
                sp.dma_start(ints[:, 0:full].rearrange("p (b e) -> p b e", e=P),
                             io[name][0:full * P].rearrange("(b p e) -> p b e", p=P, e=P)).then_inc(edges_in, 16)
                sp.dma_start(ints[0:EFULL - full, full:full + P],
                             io[name][full * P:EFULL * P].rearrange("(p e) -> p e", e=P)).then_inc(edges_in, 16)
                sp.dma_start(ints[EFULL - full:EFULL - full + 1, full:full + EREST],
                             io[name][EFULL * P:E].rearrange("(p e) -> p e", p=1)).then_inc(edges_in, 16)
            sp.wait_ge(x_blank, 1)
            sp.dma_start(x_all[:, 0:NT - 1, :],
                         io["x"][0:(NT - 1) * P, :].rearrange("(t p) d -> p t d", p=P)).then_inc(x_in, 16)
            sp.dma_start(x_all[0:LAST, NT - 1, :], io["x"][(NT - 1) * P:N, :]).then_inc(x_in, 16)

        @block.gpsimd
        def _(pool):
            pool.memset(dst_i[:, 3 * P:4 * P], NOWHERE).then_inc(edges_blank, 1)
            pool.memset(src_i[:, 3 * P:4 * P], NOWHERE).then_inc(edges_blank, 1)
            pool.memset(x_all[:, NT - 1, :], 0.0).then_inc(x_blank, 1)
            pool.memset(ident[:, :], 0.0).then_inc(pool_step, 1)
            pool.wait_ge(pool_step, 1)
            pool.affine_select(out=ident[:, :], in_=ident[:, :], compare_op=ALU.not_equal, fill=1.0, base=0,
                               pattern=[[-1, P]], channel_multiplier=1).then_inc(pool_step, 1)
            pool.wait_ge(pool_step, 2)
            pool.tensor_copy(ident16[:, :], ident[:, :]).then_inc(consts_set, 1)
            pool.iota(win_ids, [[1, NW]], base=0, channel_multiplier=0,
                      allow_small_or_imprecise_dtypes=True).then_inc(consts_set, 1)
            pool.iota(tile_no[:, 0:4], [[P, ETB]], base=1, channel_multiplier=1,
                      allow_small_or_imprecise_dtypes=True).then_inc(consts_set, 1)
            pool.iota(tile_no[:, 4:8], [[-P, ETB]], base=ET, channel_multiplier=-1,
                      allow_small_or_imprecise_dtypes=True).then_inc(consts_set, 1)
            pool.iota(iota16, [[1, WCOL]], base=0, channel_multiplier=0,
                      allow_small_or_imprecise_dtypes=True).then_inc(consts_set, 1)
            pool.iota(win_keys[:, :], [[KEYW, NW + WPT]], base=0, channel_multiplier=0,
                      allow_small_or_imprecise_dtypes=True).then_inc(consts_set, 1)
            pool.memset(zeros16[:, :], 0.0)
            pool.memset(ones16[:, :], 1.0).then_inc(consts_set, 1)
            pool.wait_ge(reach_set, 1)
            pool.partition_all_reduce(reach_all, reach_1, P, RMAX).then_inc(reach_max, 1)
            pool.sem_inc(summed, 1)
            pool.wait_ge(win_out, WPT)
            pool.tensor_copy(row_sums, counts[:, 0, :, :]).then_inc(summed, 1)
            with pool.Fori(0, NT // 2) as i:
                for half in range(2):
                    pool.wait_ge(win_out, (i * 2 + half + 2) * WPT)
                    pool.wait_ge(summed, i * 2 + half + 2)
                    pool.tensor_tensor(row_sums, row_sums, counts[:, 1 - half, :, :], ALU.add).then_inc(summed, 1)

        @block.vector
        def _(dve):
            done = [0]

            def then(ins):
                done[0] += 1
                ins.then_inc(dve_step, 1)
                dve.wait_ge(dve_step, done[0])

            dve.wait_ge(edges_in, 96)
            then(dve.tensor_scalar(key_i, dst_i, 5, 10, ALU.logical_shift_right, ALU.logical_shift_left))
            then(dve.tensor_scalar(tmp_i, src_i, 7, 5, ALU.logical_shift_right, ALU.logical_shift_left))
            then(dve.tensor_tensor(key_i, key_i, tmp_i, ALU.bitwise_or))
            then(dve.tensor_scalar(tmp_i, dst_i, WD - 1, None, ALU.bitwise_and))
            then(dve.tensor_tensor(key_i, key_i, tmp_i, ALU.bitwise_or))
            then(dve.tensor_scalar(low_i, src_i, P - 1, None, ALU.bitwise_and))
            then(dve.tensor_scalar(tmp_i, dst_i, 5, None, ALU.logical_shift_right))
            dve.tensor_copy(key_f, key_i).then_inc(fields_set, 1)
            dve.tensor_copy(low_f, low_i).then_inc(fields_set, 1)
            then(dve.tensor_copy(win_f, tmp_i))
            wins = win_f.rearrange("p (b e) -> p b e", b=ETB)
            then(dve.tensor_reduce(wmin, wins, AX.X, ALU.min))
            then(dve.tensor_reduce(wmax, wins, AX.X, ALU.max))
            dve.wait_ge(consts_set, 7)
            for b in range(ETB):
                dve.tensor_scalar(to_hi[:, :, b], win_ids, wmin[:, b:b + 1], tile_no[:, b:b + 1], ALU.is_ge, ALU.mult)
                then(dve.tensor_scalar(from_lo[:, :, b], win_ids, wmin[:, b:b + 1], tile_no[:, 4 + b:5 + b],
                                       ALU.is_ge, ALU.mult))
                dve.scalar_tensor_tensor(out=reach[:, 0:NW, b], in0=win_ids, scalar=wmax[:, b:b + 1],
                                         in1=to_hi[:, :, b], op0=ALU.is_le, op1=ALU.mult)
                then(dve.scalar_tensor_tensor(out=reach[:, NW:2 * NW, b], in0=win_ids, scalar=wmax[:, b:b + 1],
                                              in1=from_lo[:, :, b], op0=ALU.is_le, op1=ALU.mult))
            dve.tensor_reduce(reach_1, reach, AX.X, ALU.max).then_inc(reach_set, 1)
            dve.wait_ge(x_in, 32)
            for tile in range(NT):
                dve.bn_stats(stats[:, tile, :], x_all[:, tile, :]).then_inc(stats_set, 1)
            for n, (field, kept) in enumerate(((key_f, 0), (low_f, 1))):
                dve.wait_ge(turned, n + 1)
                dve.tensor_copy(edges[:, :, kept], prep_ps[:, :]).then_inc(keys_set, 1)
            dve.wait_ge(reach_max, 1)
            then(dve.tensor_scalar(lo_f, reach_all[:, NW:2 * NW], -1.0, float(ET), ALU.mult, ALU.add))
            then(dve.tensor_tensor(n_f, reach_all[:, 0:NW], lo_f, ALU.subtract))
            then(dve.tensor_scalar(n_f, n_f, 1.0, float(GT - 1), ALU.max, ALU.add))
            then(dve.tensor_copy(n_i, n_f))
            dve.tensor_scalar(ranges[:, :, 0], n_i, GT.bit_length() - 1, None, ALU.logical_shift_right).then_inc(ranges_set, 1)
            then(dve.tensor_scalar(lo_f, lo_f, float(ET - GT), None, ALU.min))
            dve.tensor_copy(ranges[:, :, 1], lo_f).then_inc(ranges_set, 1)
            dve.wait_ge(ranges_set, 2)
            dve.wait_ge(keys_set, 2)
            slot = dve.alloc_register("dve_slot")
            tile = dve.alloc_register("dve_edge_tile")
            range_regs = [dve.alloc_register(f"dve_range_{n}") for n in range(2 * WPT)]
            dve.reg_mov(slot, 0)

            dve.tensor_copy(keys_now[:, :], win_keys[:, 0:WPT]).then_inc(node_set, 1)
            with dve.Fori(0, NT) as d:
                dve.wait_ge(node_set, d + 1)
                dve.load(range_regs, ranges[0:1, bass.ds(d * WPT, WPT), :].rearrange("p w r -> p (w r)"))
                for q in range(WPT):
                    n = dve.snap(range_regs[2 * q], min_val=1, max_val=MAXGROUPS)
                    dve.reg_mov(tile, range_regs[2 * q + 1])
                    with dve.Fori(0, n):
                        c = dve.snap(slot, min_val=0, max_val=MAXSTEPS)
                        first = dve.snap(tile, min_val=0, max_val=ET - GT)
                        for g in range(GT):
                            if g % HT == 0:
                                dve.wait_ge(oh_free, c + (g // HT + 1))
                            dve.tensor_scalar(one_hots[:, g, 0:WCOL], iota16, keys_now[:, q:q + 1],
                                              edges[:, bass.ds(first + g, 1), 0], ALU.add, ALU.is_equal)
                            last = dve.tensor_scalar(one_hots[:, g, WCOL:OHW], iota16[:, 0:P],
                                                     edges[:, bass.ds(first + g, 1), 1], None, ALU.is_equal)
                            if g % HT == HT - 1:
                                last.then_inc(oh_ready, 1)
                        dve.reg_add(slot, slot, GT // HT)
                        dve.reg_add(tile, tile, GT)
                dve.wait_ge(oh_ready, dve.snap(slot, min_val=2 * WPT, max_val=MAXSTEPS))
                dve.tensor_copy(keys_now[:, :], win_keys[:, bass.ds(d * WPT + WPT, WPT)]).then_inc(node_set, 1)
            dve.wait_ge(stats_set, NT)
            for tile in range(NT):
                last = dve.bn_aggr(mean_var[:, tile, :], stats[:, tile, :])
            then(last)
            then(dve.tensor_scalar(var[:, :], mean_var[:, :, 1], 1e-5, None, ALU.add))
            dve.wait_ge(summed, NT + 1)
            dve.tensor_reduce(deg[:, :], row_sums, AX.X, ALU.add).then_inc(roots_set, 1)
            dve.wait_ge(roots_set, 3)
            for value, r in ((var, rstd), (deg, dinv)):
                then(dve.reciprocal(r[:, :], (vroot if r is rstd else root)[:, :]))
                then(dve.tensor_tensor(newton[:, :], r[:, :], r[:, :], ALU.mult))
                then(dve.scalar_tensor_tensor(out=newton[:, :], in0=newton[:, :], scalar=-0.5, in1=value[:, :],
                                              op0=ALU.mult, op1=ALU.mult))
                then(dve.scalar_tensor_tensor(out=r[:, :], in0=newton[:, :], scalar=1.5, in1=r[:, :],
                                              op0=ALU.add, op1=ALU.mult))

        @block.scalar
        def _(act):
            act.sem_inc(turn_out, 1)

            def window_out(d, half, q):
                act.wait_ge(win_ready, d * WPT + q + 1)
                if not isinstance(d, int) and q == 0:
                    act.wait_ge(summed, d)
                act.activation(counts[:, half, :, q * WD:(q + 1) * WD],
                               win_ps[:, q % 2, 0:WCOL].rearrange("p (s d) -> p s d", d=WD),
                               ACT.Copy).then_inc(win_out, 1)

            def turned_out(d, i):
                k = min(TBLK, NT - i * TBLK)
                act.wait_ge(turn_ready, d * TURNS + i + 1)
                into = AT[:, d:d + 1, :] if isinstance(d, int) else AT[:, bass.ds(d, 1), :]
                act.activation(into[:, :, i * TBLK * P:(i * TBLK + k) * P].rearrange("p a n -> p (a n)"),
                               turn_ps[:, i % 2, 0:k * P], ACT.Copy).then_inc(turn_out, 1)

            def destinations(d, half):
                for q in range(WPT):
                    window_out(d, half, q)
                    for i in PIECES[q]:
                        turned_out(d - 1, i)

            for q in range(WPT):
                window_out(0, 0, q)
            with act.Fori(0, NT // 2) as pair:
                for half in range(2):
                    destinations(pair * 2 + (half + 1), 1 - half)
            for i in range(TURNS):
                turned_out(NT - 1, i)
            act.wait_ge(roots_set, 1)
            act.activation(root[:, :], deg[:, :], ACT.Sqrt).then_inc(roots_set, 1)
            act.activation(vroot[:, :], var[:, :], ACT.Sqrt).then_inc(roots_set, 1)

        @block.tensor
        def _(pe):
            pe.wait_ge(consts_set, 7)
            for n, field in enumerate((key_f, low_f)):
                pe.wait_ge(fields_set, n + 1)
                if n:
                    pe.wait_ge(keys_set, n)
                for b in range(ETB):
                    mm = pe.transpose(prep_ps[:, b * P:(b + 1) * P], field[:, b * P:(b + 1) * P], ident[:, :])
                mm.then_inc(turned, 1)
            pe.wait_ge(ranges_set, 2)
            pe.sem_inc(oh_free, GT // HT)
            slot = pe.alloc_register("pe_slot")
            range_regs = [pe.alloc_register(f"pe_range_{n}") for n in range(2 * WPT)]
            pe.reg_mov(slot, 0)

            def group(q, first):
                c = pe.snap(slot, min_val=0, max_val=MAXSTEPS)
                for g in range(GT):
                    if g % HT == 0:
                        pe.wait_ge(oh_ready, c + (g // HT + 1))
                    for a, b in ((0, 512), (512, WCOL)):
                        mm = pe.matmul(win_ps[:, q % 2, a:b], one_hots[:, g, WCOL:OHW], one_hots[:, g, a:b],
                                       start=(first and g == 0), stop=False, skip_group_check=True)
                    if g % HT == HT - 1:
                        mm.then_inc(oh_free, 1)
                pe.reg_add(slot, slot, GT // HT)

            def window(d, q, n):
                if not (isinstance(d, int) and q < 2):
                    pe.wait_ge(win_out, d * WPT + q - 1)
                group(q, True)
                with pe.If(n > 1):
                    with pe.Fori(1, n):
                        group(q, False)
                into = win_ps[:, q % 2, 0:WD] if isinstance(d, int) else win_ps[:, q % 2, bass.ds(d * WD, WD)]
                pe.matmul(into, ident16[:, :], ident16[:, q * WD:(q + 1) * WD], start=False, stop=True,
                          skip_group_check=True).then_inc(win_ready, 1)

            def turn(d, half, i):
                if i == 0:
                    pe.wait_ge(win_out, (d + 1) * WPT)
                pe.wait_ge(turn_out, d * TURNS + max(i - 1, 0) + 1)
                for k in range(min(TBLK, NT - i * TBLK)):
                    mm = pe.matmul(turn_ps[:, i % 2, k * P:(k + 1) * P], counts[:, half, i * TBLK + k, :],
                                   ident16[:, :], start=True, stop=True)
                mm.then_inc(turn_ready, 1)

            def destinations(d, half):
                pe.load(range_regs, ranges[0:1, bass.ds(d * WPT, WPT), :].rearrange("p w r -> p (w r)"))
                n_of = [pe.snap(range_regs[2 * q], min_val=1, max_val=MAXGROUPS) for q in range(WPT)]
                for q in range(WPT):
                    window(d, q, n_of[q])
                    if not isinstance(d, int):
                        for i in PIECES[q]:
                            turn(d - 1, 1 - half, i)

            destinations(0, 0)
            with pe.Fori(0, NT // 2) as pair:
                for half in range(2):
                    destinations(pair * 2 + (half + 1), 1 - half)
            for i in range(TURNS):
                turn(NT - 1, 0, i)


def convolutions(nc, io, t):
    with ExitStack() as ctx:
        def sem(name):
            return ctx.enter_context(nc.semaphore(name))

        AT, work, ident, ident16 = t["AT"], t["work"], t["ident"], t["ident16"]
        mean_var, rstd, dinv, logits = t["mean_var"], t["rstd"], t["dinv"], t["logits"]
        scale, stats2, mean_var2, var2, root2, rstd2, newton2 = (
            t[name] for name in ("scale", "stats2", "mean_var2", "var2", "root2", "rstd2", "newton2"))
        h_dram, agg_dram = t["h_dram"], t["agg_dram"]

        h_in = work[:, 0:3200].rearrange("p (t f) -> p t f", t=NT)
        parts = [work[:, a:a + 3200].bitcast(F16).rearrange("p (c t f) -> p c t f", c=2, t=NT)
                 for a in (3200, 6400)]
        agg_st = work[:, 9600:9600 + N]
        w_sb = work[:, 3200:3200 + 4 * H].rearrange("p (k n) -> p k n", k=4)
        bias = work[:, 3200 + 4 * H:3200 + 5 * H]
        agg_in = [work[:, a:a + 4 * GN].rearrange("p (k n) -> p k n", k=4) for a in (0, 6400)]
        y_ring = work[:, 9600:9600 + 3 * H].rearrange("p (r n) -> p r n", r=3)
        h_ring = work[:, 9600 + 3 * H:9600 + 6 * H].rearrange("p (r n) -> p r n", r=3)
        z = t["free"]
        x2, xn2, wfc, bfc, gate_w, gate_b = z["x2"], z["xn2"], z["wfc"], z["bfc"], z["gate_w"], z["gate_b"]
        h3t, xnt, zeros = z["h3t"], z["xnt"], z["zeros"]

        peak, peak_1, peak_all, expo = t["peak"], t["peak_1"], t["peak_all"], t["expo"]

        banks = ctx.enter_context(nc.psum_tensor("banks", [P, 8, 512], F32))

        pads_set, pads_out = sem("pads_set"), sem("pads_out")
        h_landed, hi_set, parts_set = sem("h_landed"), sem("hi_set"), sem("parts_set")
        norm_set = sem("norm_set")
        agg_ready, agg_out_act, agg_out_dve = sem("agg_ready"), sem("agg_out_act"), sem("agg_out_dve")
        agg_stored = sem("agg_stored")
        w_landed = sem("w_landed")
        group_landed = [sem("group_landed_0"), sem("group_landed_1")]
        z_ready, z_out, relu_out, peak_set = sem("z_ready"), sem("z_out"), sem("relu_out"), sem("peak_set")
        h_stored = [sem(f"h_stored_{i}") for i in range(3)]
        peak_row, peak_found, scale_set = sem("peak_row"), sem("peak_found"), sem("scale_set")
        conv_step = sem("conv_step")
        x2_landed, xb_set, heads_landed = sem("x2_landed"), sem("xb_set"), sem("heads_landed")
        h3_turned, h3t_set = sem("h3_turned"), sem("h3t_set")
        o_ready, x2_set = sem("o_ready"), sem("x2_set")
        var_set, root_set, xn_set = sem("var_set"), sem("root_set"), sem("xn_set")
        xn_turned, xnt_set, logit_ready = sem("xn_turned"), sem("xnt_set"), sem("logit_ready")
        slots_blank = sem("slots_blank")
        zeros_set = sem("zeros_set")

        blocks = [(layer, j) for layer, k in enumerate(KF) for j in range(k)]
        first = [sum(KF[:layer]) for layer in range(4)]
        weights = [(io[f"L0_gnn_W{n}"], io[f"L0_gnn_b{n}"]) for n in (1, 2, 3)]
        nact, ndve = (CH + 1) // 2, CH // 2

        def rows(tile):
            return P if tile < NT - 1 else LAST

        block = ctx.enter_context(nc.Block())

        @block.sync
        def _(sp):
            sp.wait_ge(pads_set, 2)
            sp.dma_start(h_dram[:, LAST:P, NT - 1, :].rearrange("k p f -> p k f"),
                         y_ring[LAST:P, 0, :].rearrange("p (k f) -> p k f", k=4)).then_inc(pads_out, 16)
            stored = 0
            for layer, k in enumerate(KF):
                for j in range(k):
                    n = first[layer] + j
                    if n:
                        sp.wait_ge(parts_set, n)
                    if layer == 0:
                        sp.dma_start(h_in[:, 0:NT - 1, :], io["x"][0:(NT - 1) * P, j * P:(j + 1) * P]
                                     .rearrange("(t p) f -> p t f", p=P)).then_inc(h_landed, 16)
                        sp.dma_start(h_in[0:LAST, NT - 1, :],
                                     io["x"][(NT - 1) * P:N, j * P:(j + 1) * P]).then_inc(h_landed, 16)
                    else:
                        if j == 0:
                            for i in range(3):
                                sp.wait_ge(h_stored[i], 16 * len(range(i, layer * NT, 3)))
                            sp.wait_ge(pads_out, 16)
                        sp.dma_start(h_in, h_dram[j]).then_inc(h_landed, 32)
                for j in range(k):
                    n = first[layer] + j
                    if n == first[layer] + k - 1:
                        sp.wait_ge(agg_ready, CH * n)
                        sp.dma_start(w_sb[:, 0:k, :],
                                     weights[layer][0].rearrange("(k p) n -> p k n", p=P)).then_inc(w_landed, 16)
                        sp.dma_start(bias, weights[layer][1].rearrange("(o n) -> o n", o=1)
                                     .to_broadcast([P, H])).then_inc(w_landed, 16)
                    for c in range(CH):
                        if c % 2:
                            sp.wait_ge(agg_out_dve, n * ndve + c // 2 + 1)
                        else:
                            sp.wait_ge(agg_out_act, n * nact + c // 2 + 1)
                        sp.dma_start(agg_dram[j, :, CS[c]:CS[c + 1]],
                                     agg_st[:, CS[c]:CS[c + 1]]).then_inc(agg_stored, 16)
                sp.wait_ge(agg_stored, 16 * CH * first[layer + 1])
                if layer == 2:
                    sp.wait_ge(zeros_set, 1)
                    full = SLOTS // P * P
                    sp.dma_start(t["slots_in"][0:full, :].rearrange("(a p) d -> p a d", p=P),
                                 zeros.rearrange("p (a d) -> p a d", a=1).to_broadcast([P, SLOTS // P, D])
                                 ).then_inc(slots_blank, 16)
                    sp.dma_start(t["slots_in"][full:SLOTS, :], zeros[0:SLOTS - full, :]).then_inc(slots_blank, 16)
                for g in range(NG + 1):
                    if g < NG:
                        if g >= 2:
                            sp.wait_ge(z_ready, layer * NT + (g - 1) * GT5)
                        a, b = g * GN, min(N, (g + 1) * GN)
                        sp.dma_start(agg_in[g % 2][:, 0:k, 0:b - a],
                                     agg_dram[0:k, :, a:b].rearrange("k p n -> p k n")).then_inc(group_landed[g % 2], 16)
                    if layer == 2 and g == 1:
                        sp.dma_start(x2[:, 0:NT - 1, :],
                                       io["x"][0:(NT - 1) * P, :].rearrange("(t p) d -> p t d", p=P)).then_inc(x2_landed, 16)
                        sp.dma_start(x2[0:LAST, NT - 1, :], io["x"][(NT - 1) * P:N, :]).then_inc(x2_landed, 16)
                        sp.dma_start(wfc, io["L0_gnn_Wfc"].rearrange("(k p) n -> p k n", p=P)).then_inc(heads_landed, 16)
                        sp.dma_start(bfc, io["L0_gnn_bfc"].rearrange("(o n) -> o n", o=1)
                                       .to_broadcast([P, D])).then_inc(heads_landed, 16)
                        sp.dma_start(gate_w, io["L0_ffn_gate_w"].rearrange("(k p) e -> p k e", p=P)).then_inc(heads_landed, 16)
                        sp.dma_start(gate_b, io["L0_ffn_gate_b"].rearrange("(o e) -> o e", o=1)
                                       .to_broadcast([P, NE])).then_inc(heads_landed, 16)
                        for e in range(NE):
                            sp.dma_start(z["w1"][:, e, :, :],
                                           io["L0_ffn_w1"][e].rearrange("(k p) f -> p k f", p=P)).then_inc(t["w1_landed"][e], 16)
                            if e < 2:
                                sp.dma_start(z["w2"][:, e, :, :], io["L0_ffn_w2"][e].rearrange("(k p) d -> p k d", p=P)
                                               ).then_inc(t["w2_landed"][e], 16)
                        sp.dma_start(z["b2"], io["L0_ffn_b2"].rearrange("(o e) d -> o (e d)", o=1)
                                       .to_broadcast([P, NE * D])).then_inc(t["b_landed"], 16)
                        sp.dma_start(z["b1_rows"], io["L0_ffn_b1"].rearrange("e (m f) -> (e m) f", f=P)).then_inc(t["b_landed"], 16)
                    if g and layer < 2:
                        for tile in range((g - 1) * GT5, g * GT5):
                            m = rows(tile)
                            sp.wait_ge(relu_out, layer * NT + tile + 1)
                            sp.dma_start(h_dram[:, 0:m, tile, :].rearrange("k p f -> p k f"),
                                         h_ring[0:m, stored % 3, :].rearrange("p (k f) -> p k f", k=4)
                                         ).then_inc(h_stored[stored % 3], 16)
                            stored += 1
            sp.wait_ge(slots_blank, 32)

        @block.gpsimd
        def _(pool):
            pool.memset(h_in[:, NT - 1, :], 0.0).then_inc(pads_set, 1)
            pool.memset(y_ring[:, 0, :], 0.0).then_inc(pads_set, 1)
            pool.memset(scale[:, 0, 0:1], 1024.0).then_inc(pads_set, 1)
            pool.memset(scale[:, 0, 1:2], 1.0 / 1024.0).then_inc(pads_set, 1)
            pool.memset(peak[:, :], 0.0).then_inc(pads_set, 1)
            for layer in range(2):
                pool.wait_ge(peak_row, layer + 1)
                pool.partition_all_reduce(peak_all[:, :], peak_1[:, :], P, RMAX).then_inc(peak_found, 1)
            pool.wait_ge(agg_ready, CH * len(blocks))
            pool.memset(zeros, 0.0).then_inc(zeros_set, 1)
            pool.memset(logits[:, :, :], 0.0).then_inc(zeros_set, 1)
            pool.wait_ge(x2_landed, 32)
            pool.wait_ge(heads_landed, 64)
            for tile in range(NT):
                m = rows(tile)
                pool.tensor_tensor(x2[0:m, tile, :], x2[0:m, tile, :], bfc[0:m, :], ALU.add).then_inc(xb_set, 1)

        @block.vector
        def _(dve):
            done = [0]

            def then(ins):
                done[0] += 1
                ins.then_inc(conv_step, 1)
                dve.wait_ge(conv_step, done[0])

            def aggregate_out(n, layer):
                for c in range(1, CH, 2):
                    dve.wait_ge(agg_ready, CH * n + c + 1)
                    if n:
                        dve.wait_ge(agg_stored, 16 * CH * n)
                    dve.tensor_scalar(agg_st[:, CS[c]:CS[c + 1]], banks[:, c, 0:CS[c + 1] - CS[c]],
                                      scale[:, layer, 1:2], None, ALU.mult).then_inc(agg_out_dve, 1)

            def residual(tile):
                m = rows(tile)
                dve.wait_ge(xb_set, tile + 1)
                dve.wait_ge(o_ready, tile + 1)
                dve.tensor_tensor(x2[0:m, tile, :], banks[0:m, 4 + tile % 2, 0:D], x2[0:m, tile, :],
                                  ALU.add).then_inc(x2_set, 1)
                dve.wait_ge(x2_set, tile + 1)
                then(dve.bn_stats(stats2[0:m, tile, :], x2[0:m, tile, :]))
                then(dve.bn_aggr(mean_var2[0:m, tile, :], stats2[0:m, tile, :]))
                dve.tensor_scalar(var2[0:m, tile:tile + 1], mean_var2[0:m, tile, 1:2], 1e-5, None,
                                  ALU.add).then_inc(var_set, 1)

            def normed(tile):
                m = rows(tile)
                v, root, r, a = (arr[0:m, tile:tile + 1] for arr in (var2, root2, rstd2, newton2))
                dve.wait_ge(root_set, tile + 1)
                then(dve.reciprocal(r, root))
                then(dve.tensor_tensor(a, r, r, ALU.mult))
                then(dve.scalar_tensor_tensor(out=a, in0=a, scalar=-0.5, in1=v, op0=ALU.mult, op1=ALU.mult))
                then(dve.scalar_tensor_tensor(out=r, in0=a, scalar=1.5, in1=r, op0=ALU.add, op1=ALU.mult))
                dve.tensor_scalar(xn2[0:m, tile, :], x2[0:m, tile, :], mean_var2[0:m, tile, 0:1], r,
                                  ALU.subtract, ALU.mult).then_inc(xn_set, 1)

            then(dve.tensor_tensor(rstd[:, :], rstd[:, :], dinv[:, :], ALU.mult))
            dve.wait_ge(pads_set, 5)
            for layer, k in enumerate(KF):
                for j in range(k):
                    n = first[layer] + j
                    dve.wait_ge(h_landed, 32 * (n + 1))
                    if layer == 0:
                        for tile in range(NT):
                            last = dve.tensor_scalar(h_in[:, tile, :], h_in[:, tile, :], mean_var[:, tile, 0:1],
                                                     rstd[:, tile:tile + 1], ALU.subtract, ALU.mult)
                        last.then_inc(norm_set, 1)
                    dve.wait_ge(hi_set, n + 1)
                    flat = parts[n % 2].rearrange("p c t f -> p c (t f)")
                    dve.scalar_tensor_tensor(out=flat[:, 1, :], in0=h_in.rearrange("p t f -> p (t f)"),
                                             scalar=scale[:, layer, 0:1], in1=flat[:, 0, :],
                                             op0=ALU.mult, op1=ALU.subtract).then_inc(parts_set, 1)
                    if j:
                        aggregate_out(n - 1, layer)
                aggregate_out(first[layer + 1] - 1, layer)
                dve.wait_ge(w_landed, 32 * (layer + 1))
                for tile in range(NT + 4):
                    if tile < NT:
                        m = rows(tile)
                        at = layer * NT + tile
                        dve.wait_ge(z_ready, at + 1)
                        if at >= 3:
                            dve.wait_ge(relu_out, at - 2)
                        if tile < 3:
                            dve.wait_ge(agg_stored, 16 * CH * first[layer + 1])
                        dve.scalar_tensor_tensor(out=y_ring[0:m, at % 3, :], in0=banks[0:m, tile % 2, :],
                                                 scalar=dinv[0:m, tile:tile + 1], in1=bias[0:m, :],
                                                 op0=ALU.mult, op1=ALU.add).then_inc(z_out, 1)
                    if layer < 2 and 1 <= tile <= NT:
                        m = rows(tile - 1)
                        at = layer * NT + tile - 1
                        dve.wait_ge(relu_out, at + 1)
                        dve.tensor_reduce(peak[0:m, tile - 1:tile], h_ring[0:m, at % 3, :], AX.X,
                                          ALU.max).then_inc(peak_set, 1)
                    if layer == 2 and 0 <= tile - 2 < NT:
                        residual(tile - 2)
                    if layer == 2 and 0 <= tile - 3 < NT:
                        normed(tile - 3)
                if layer < 2:
                    dve.wait_ge(peak_set, (layer + 1) * NT)
                    dve.tensor_reduce(peak_1[:, :], peak[:, :], AX.X, ALU.max).then_inc(peak_row, 1)
                    dve.wait_ge(peak_found, layer + 1)
                    then(dve.tensor_scalar(expo[:, 0:1], peak_all[:, :].bitcast(I32), 23, None,
                                           ALU.logical_shift_right))
                    then(dve.tensor_scalar(expo[:, 1:2], expo[:, 0:1], -1.0, 268.0, ALU.mult, ALU.add))
                    then(dve.tensor_scalar(expo[:, 1:2], expo[:, 1:2], 253.0, None, ALU.min))
                    then(dve.tensor_scalar(expo[:, 2:3], expo[:, 1:2], -1.0, 254.0, ALU.mult, ALU.add))
                    dve.tensor_scalar(scale[:, layer + 1, :].bitcast(I32), expo[:, 1:3], 23, None,
                                      ALU.logical_shift_left).then_inc(scale_set, 1)
            dve.wait_ge(zeros_set, 2)
            for a, b, m in ((0, NT - 1, P), (NT - 1, NT, LAST)):
                dve.wait_ge(logit_ready, NT)
                dve.tensor_tensor(logits[0:m, a:b, :],
                                  banks[0:m, 7, a * NE:b * NE].rearrange("p (t e) -> p t e", e=NE),
                                  gate_b[0:m, :].rearrange("p (o e) -> p o e", o=1).to_broadcast([m, b - a, NE]),
                                  ALU.add).then_inc(conv_step, 1)

        @block.scalar
        def _(act):
            def aggregate_out(n, layer):
                for c in range(0, CH, 2):
                    act.wait_ge(agg_ready, CH * n + c + 1)
                    if n:
                        act.wait_ge(agg_stored, 16 * CH * n)
                    else:
                        act.wait_ge(pads_out, 16)
                    act.activation(agg_st[:, CS[c]:CS[c + 1]], banks[:, c, 0:CS[c + 1] - CS[c]], ACT.Copy,
                                   scale=scale[:, layer, 1:2]).then_inc(agg_out_act, 1)

            def turned_out(tile):
                m = rows(tile)
                act.wait_ge(h3_turned, tile + 1)
                if tile >= 2:
                    act.wait_ge(o_ready, tile - 1)
                act.activation(h3t[:, tile % 2, :, 0:m],
                               banks[:, 2 + tile % 2, :].rearrange("p (k m) -> p k m", k=4)[:, :, 0:m],
                               ACT.Copy).then_inc(h3t_set, 1)

            def root(tile):
                m = rows(tile)
                act.wait_ge(var_set, tile + 1)
                act.activation(root2[0:m, tile:tile + 1], var2[0:m, tile:tile + 1], ACT.Sqrt).then_inc(root_set, 1)

            def xn_out(tile):
                m = rows(tile)
                act.wait_ge(xn_turned, tile + 1)
                if tile >= 2:
                    act.wait_ge(logit_ready, tile - 1)
                act.activation(xnt[:, tile % 2, :, 0:m],
                               banks[:, 6, :].rearrange("p (r k m) -> p r k m", r=2, k=2)[:, tile % 2, :, 0:m],
                               ACT.Copy).then_inc(xnt_set, 1)

            act.wait_ge(pads_set, 5)
            for layer, k in enumerate(KF):
                if layer:
                    act.wait_ge(scale_set, layer)
                for j in range(k):
                    n = first[layer] + j
                    act.wait_ge(h_landed, 32 * (n + 1))
                    if layer == 0:
                        act.wait_ge(norm_set, n + 1)
                    if n >= 2:
                        act.wait_ge(agg_ready, CH * (n - 1))
                    act.activation(parts[n % 2][:, 0, :, :], h_in[:, :, :], ACT.Copy,
                                   scale=scale[:, layer, 0:1]).then_inc(hi_set, 1)
                    if j:
                        aggregate_out(n - 1, layer)
                aggregate_out(first[layer + 1] - 1, layer)
                for tile in range(NT + 5):
                    m = rows(tile)
                    at = layer * NT + tile
                    if tile < NT:
                        act.wait_ge(z_out, at + 1)
                    if tile >= NT:
                        pass
                    elif layer < 2:
                        if at >= 3:
                            act.wait_ge(h_stored[at % 3], 16 * (at // 3))
                            act.wait_ge(peak_set, at - 2)
                        act.activation(h_ring[0:m, at % 3, :], y_ring[0:m, at % 3, :], ACT.Relu,
                                       scale=dinv[0:m, tile:tile + 1]).then_inc(relu_out, 1)
                    else:
                        if tile >= 3:
                            act.wait_ge(h3_turned, tile - 2)
                        else:
                            act.wait_ge(h_stored[at % 3], 16 * (at // 3))
                            act.wait_ge(peak_set, 2 * NT)
                        act.activation(h_ring[0:m, at % 3, :], y_ring[0:m, at % 3, :],
                                       ACT.Relu).then_inc(relu_out, 1)
                    if layer == 2:
                        if 0 <= tile - 1 < NT:
                            turned_out(tile - 1)
                        if 0 <= tile - 3 < NT:
                            root(tile - 3)
                        if 0 <= tile - 4 < NT:
                            xn_out(tile - 4)

        @block.tensor
        def _(pe):
            def turn_h3(tile):
                m = rows(tile)
                pe.wait_ge(relu_out, 2 * NT + tile + 1)
                if tile >= 2:
                    pe.wait_ge(h3t_set, tile - 1)
                for kk in range(4):
                    mm = pe.transpose(banks[:, 2 + tile % 2, kk * P:kk * P + m],
                                      h_ring[0:m, (2 * NT + tile) % 3, kk * P:(kk + 1) * P], ident[0:m, 0:m])
                mm.then_inc(h3_turned, 1)

            def head(tile):
                m = rows(tile)
                if tile == 0:
                    pe.wait_ge(heads_landed, 64)
                pe.wait_ge(h3t_set, tile + 1)
                if tile >= 2:
                    pe.wait_ge(x2_set, tile - 1)
                for kk in range(4):
                    mm = pe.matmul(banks[0:m, 4 + tile % 2, 0:D], h3t[:, tile % 2, kk, 0:m], wfc[:, kk, :],
                                   start=(kk == 0), stop=(kk == 3))
                mm.then_inc(o_ready, 1)

            def turn_xn(tile):
                m = rows(tile)
                pe.wait_ge(xn_set, tile + 1)
                if tile:
                    pe.wait_ge(xnt_set, tile)
                for kk in range(2):
                    mm = pe.transpose(banks[:, 6, (tile % 2) * 2 * P + kk * P:(tile % 2) * 2 * P + kk * P + m],
                                      xn2[0:m, tile, kk * P:(kk + 1) * P], ident[0:m, 0:m])
                mm.then_inc(xn_turned, 1)

            def gate(tile):
                m = rows(tile)
                pe.wait_ge(xnt_set, tile + 1)
                for kk in range(2):
                    mm = pe.matmul(banks[0:m, 7, tile * NE:(tile + 1) * NE], xnt[:, tile % 2, kk, 0:m],
                                   gate_w[:, kk, :], start=(kk == 0), stop=(kk == 1))
                mm.then_inc(logit_ready, 1)

            for layer, k in enumerate(KF):
                for j in range(k):
                    n = first[layer] + j
                    pe.wait_ge(parts_set, n + 1)
                    for c in range(CH):
                        if n:
                            pe.wait_ge(agg_out_dve if c % 2 else agg_out_act,
                                       (n - 1) * (ndve if c % 2 else nact) + c // 2 + 1)
                        for part in range(2):
                            pe.matmul(banks[:, c, 0:CS[c + 1] - CS[c]], parts[n % 2][:, part, 0, :],
                                      AT[:, 0, CS[c]:CS[c + 1]], start=(part == 0), stop=False)
                    with pe.Fori(1, NT - 1) as d:
                        for part in range(2):
                            for c in range(CH):
                                pe.matmul(banks[:, c, 0:CS[c + 1] - CS[c]],
                                          parts[n % 2][:, part, bass.ds(d, 1), :].rearrange("p a f -> p (a f)"),
                                          AT[:, bass.ds(d, 1), CS[c]:CS[c + 1]].rearrange("p a n -> p (a n)"),
                                          start=False, stop=False)
                    for c in range(CH):
                        for part in range(2):
                            mm = pe.matmul(banks[:, c, 0:CS[c + 1] - CS[c]], parts[n % 2][:, part, NT - 1, :],
                                           AT[:, NT - 1, CS[c]:CS[c + 1]], start=False, stop=(part == 1))
                        mm.then_inc(agg_ready, 1)
                pe.wait_ge(agg_out_act, first[layer + 1] * nact)
                pe.wait_ge(agg_out_dve, first[layer + 1] * ndve)
                pe.wait_ge(w_landed, 32 * (layer + 1))
                for tile in range(NT if layer < 2 else NT + 5):
                    if tile < NT:
                        m = rows(tile)
                        at = layer * NT + tile
                        g = tile // GT5
                        if tile % GT5 == 0:
                            pe.wait_ge(group_landed[g % 2], 16 * (layer * len(range(g % 2, NG, 2)) + g // 2 + 1))
                        if tile >= 2:
                            pe.wait_ge(z_out, at - 1)
                        a = (tile - g * GT5) * P
                        for kk in range(k):
                            mm = pe.matmul(banks[0:m, tile % 2, :], agg_in[g % 2][:, kk, a:a + m], w_sb[:, kk, :],
                                           start=(kk == 0), stop=(kk == k - 1))
                        mm.then_inc(z_ready, 1)
                    if layer == 2:
                        for stage, lag in ((turn_h3, 1), (head, 2), (turn_xn, 4), (gate, 5)):
                            if 0 <= tile - lag < NT:
                                stage(tile - lag)


def experts(nc, io, t):
    with ExitStack() as ctx:
        def sem(name):
            return ctx.enter_context(nc.semaphore(name))

        work, ident, logits, z = t["work"], t["ident"], t["logits"], t["free"]
        slots_in, slots_out = t["slots_in"], t["slots_out"]
        x2, xn2, w1, w2, b2, b1_rows, b1t = (z[n] for n in ("x2", "xn2", "w1", "w2", "b2", "b1_rows", "b1t"))
        tri, ones, e_less, valid = z["tri"], z["ones"], z["e_less"], z["valid"]
        back = xn2

        hid = [work[:, a:a + FM * C].rearrange("p (m c) -> p m c", m=FM) for a in (0, FM * C)]
        a = 2 * FM * C
        xs = [work[:, a + n * 1024:a + (n + 1) * 1024].rearrange("p (s d) -> p s d", s=ST) for n in range(2)]
        xst = [work[:, a + 2048 + n * 1024:a + 2048 + (n + 1) * 1024].rearrange("p (k c) -> p k c", k=2)
               for n in range(2)]
        y_st = work[:, a + 4096:a + 4096 + 1024].rearrange("p (s d) -> p s d", s=ST)
        gate_words = [FM * C]

        def small(*shape, dt=F32):
            n = int(np.prod(shape))
            lo = gate_words[0]
            gate_words[0] += n
            v = work[:, lo:lo + n]
            v = v if dt is F32 else v.bitcast(dt)
            return v if len(shape) == 1 else v.rearrange("p (t e) -> p t e", e=shape[1])

        less, ex, pr, eq, cand, hot, tot, run_a, run_b, cum = (small(NT, NE) for _ in range(10))
        top, total, inv, idx8, pos, kept, place, token, target = (small(NT) for _ in range(9))
        hot16 = small(NT * NE // 2).bitcast(F16)
        scatter_idx, gather_idx = t["scatter_idx"], t["gather_idx"]
        prob, weight, finite, finite_1, bad = (t[n] for n in ("prob", "weight", "finite", "finite_1", "bad"))

        banks = ctx.enter_context(nc.psum_tensor("expert_banks", [P, 8, 512], F32))

        consts_set, pool_step, gate_step = sem("ffn_consts_set"), sem("ffn_pool_step"), sem("gate_step")
        less_set, ex_set, hot_set, counted = sem("less_set"), sem("ex_set"), sem("hot_set"), sem("counted")
        target_set, scattered = sem("target_set"), sem("scattered")
        b1_turned, b1_set = sem("b1_turned"), sem("b1_set")
        xs_landed = [sem("xs_landed_0"), sem("xs_landed_1")]
        xs_turned, xst_act, xst_dve = sem("xs_turned"), sem("xst_act"), sem("xst_dve")
        hid_ready, hid_act, hid_dve = sem("hid_ready"), sem("hid_act"), sem("hid_dve")
        y_ready, y_out, y_stored = sem("y_ready"), sem("y_out"), sem("y_stored")
        finite_set, bad_row, bad_found, bad_set = sem("finite_set"), sem("bad_row"), sem("bad_found"), sem("bad_set")
        gathered = [sem(f"gathered_{i}") for i in range(NT)]
        sum_set, out_stored, guard_step = sem("sum_set"), sem("out_stored"), sem("guard_step")

        def rows(tile):
            return P if tile < NT - 1 else LAST

        def slot_rows(s):
            return min(P, C - s * P)

        def whole(dram, e, tiles, to_sbuf):
            if tiles == "full":
                return dram[e * C:e * C + (ST - 1) * P, :].rearrange("(s p) d -> p s d", p=P)
            return dram[e * C + (ST - 1) * P:(e + 1) * C, :]

        block = ctx.enter_context(nc.Block())

        @block.sync
        def _(sp):
            def load_slots(e):
                if e >= 2:
                    sp.wait_ge(xs_turned, 2 * (e - 1))
                sp.dma_start(xs[e % 2][:, 0:ST - 1, :], whole(slots_in, e, "full", True)).then_inc(xs_landed[e % 2], 16)
                sp.dma_start(xs[e % 2][0:slot_rows(ST - 1), ST - 1, :],
                             whole(slots_in, e, "rest", True)).then_inc(xs_landed[e % 2], 16)

            sp.wait_ge(scattered, 16 * NT)
            load_slots(0)
            load_slots(1)
            for e in range(NE):
                sp.wait_ge(y_out, ST * (e + 1))
                sp.dma_start(whole(slots_out, e, "full", False), y_st[:, 0:ST - 1, :]).then_inc(y_stored, 16)
                sp.dma_start(whole(slots_out, e, "rest", False),
                             y_st[0:slot_rows(ST - 1), ST - 1, :]).then_inc(y_stored, 16)
                if e + 2 < NE:
                    sp.wait_ge(y_ready, ST * (e + 1))
                    sp.dma_start(w2[:, e % 2, :, :], io["L0_ffn_w2"][e + 2].rearrange("(k p) d -> p k d", p=P)
                                 ).then_inc(t["w2_landed"][e % 2], 16)
                    load_slots(e + 2)
            for tile in range(NT):
                m = rows(tile)
                sp.wait_ge(sum_set, tile + 1)
                sp.dma_start(io["out"][tile * P:tile * P + m, :], x2[0:m, tile, :]).then_inc(out_stored, 16)
            sp.wait_ge(out_stored, 16 * NT)

        @block.gpsimd
        def _(pool):
            pool.iota(e_less, [[0, NT], [1, NE]], base=-NE, channel_multiplier=0,
                      allow_small_or_imprecise_dtypes=True).then_inc(consts_set, 1)
            pool.iota(token, [[P, NT]], base=SLOTS, channel_multiplier=1,
                      allow_small_or_imprecise_dtypes=True).then_inc(consts_set, 1)
            pool.memset(finite[:, :], 0.0).then_inc(consts_set, 1)
            pool.memset(valid, 1.0).then_inc(pool_step, 1)
            pool.memset(tri, 1.0).then_inc(pool_step, 1)
            pool.memset(ones, 1.0).then_inc(consts_set, 1)
            pool.wait_ge(pool_step, 2)
            pool.affine_select(out=valid[:, NT - 1, :], in_=valid[:, NT - 1, :], compare_op=ALU.is_ge, fill=0.0,
                               base=LAST - 1, pattern=[[0, NE]], channel_multiplier=-1).then_inc(consts_set, 1)
            pool.affine_select(out=tri, in_=tri, compare_op=ALU.is_ge, fill=0.0, base=0, pattern=[[1, P]],
                               channel_multiplier=-1).then_inc(consts_set, 1)
            pool.wait_ge(target_set, 2)
            for tile in range(NT):
                m = rows(tile)
                pool.indirect_dma_start(
                    out=slots_in[:, :], out_offset=bass.IndirectOffsetOnAxis(ap=scatter_idx[0:m, tile:tile + 1], axis=0),
                    in_=xn2[0:m, tile, :], in_offset=None, bounds_check=SLOTS - 1, oob_is_err=False,
                ).then_inc(scattered, 16)
            pool.wait_ge(bad_row, 1)
            pool.partition_all_reduce(bad[:, 1:2], bad[:, 0:1], P, RMAX).then_inc(bad_found, 1)
            pool.wait_ge(y_stored, 32 * NE)
            for tile in range(NT):
                m = rows(tile)
                pool.indirect_dma_start(
                    out=back[0:m, tile, :], out_offset=None, in_=slots_out[:, :],
                    in_offset=bass.IndirectOffsetOnAxis(ap=gather_idx[0:m, tile:tile + 1], axis=0),
                ).then_inc(gathered[tile], 16)

        @block.vector
        def _(dve):
            done = [0]

            def then(ins):
                done[0] += 1
                ins.then_inc(gate_step, 1)
                dve.wait_ge(gate_step, done[0])

            def by_expert(v):
                return v.rearrange("p (t o) -> p t o", o=1).to_broadcast([P, NT, NE])

            then(dve.tensor_reduce(top, logits[:, :, :], AX.X, ALU.max))
            dve.tensor_tensor(less, logits[:, :, :], by_expert(top), ALU.subtract).then_inc(less_set, 1)
            dve.wait_ge(ex_set, 1)
            then(dve.tensor_reduce(total, ex, AX.X, ALU.add))
            then(dve.reciprocal(inv, total))
            then(dve.tensor_tensor(pr, ex, by_expert(inv), ALU.mult))
            then(dve.tensor_reduce(prob[:, :], pr, AX.X, ALU.max))
            then(dve.tensor_tensor(eq, pr, by_expert(prob[:, :]), ALU.is_equal))
            dve.wait_ge(consts_set, 6)
            then(dve.tensor_tensor(cand, eq, e_less, ALU.mult))
            then(dve.tensor_reduce(idx8, cand, AX.X, ALU.min))
            then(dve.tensor_tensor(hot, e_less, by_expert(idx8), ALU.is_equal))
            then(dve.tensor_tensor(hot, hot, valid, ALU.mult))
            dve.tensor_copy(hot16, hot.rearrange("p t e -> p (t e)")).then_inc(hot_set, 1)
            dve.wait_ge(counted, 1)
            dve.tensor_copy(cum.rearrange("p t e -> p (t e)"), banks[:, 7, 0:NT * NE])
            dve.tensor_copy(tot.rearrange("p t e -> p (t e)"), banks[:, 7, NT * NE:2 * NT * NE])
            then(dve.tensor_copy(run_a.rearrange("p t e -> p (t e)"), banks[:, 7, NT * NE:2 * NT * NE]))
            src, dst, width = run_a, run_b, 1
            while width < NT:
                dve.tensor_copy(dst[:, 0:width, :], src[:, 0:width, :])
                then(dve.tensor_tensor(dst[:, width:NT, :], src[:, width:NT, :], src[:, 0:NT - width, :], ALU.add))
                src, dst, width = dst, src, 2 * width
            then(dve.tensor_tensor(src, src, tot, ALU.subtract))
            then(dve.tensor_tensor(src, src, cum, ALU.add))
            then(dve.tensor_tensor(src, src, hot, ALU.mult))
            then(dve.tensor_reduce(pos, src, AX.X, ALU.add))
            then(dve.tensor_scalar(kept, pos, float(C), None, ALU.is_le))
            dve.tensor_tensor(weight[:, :], prob[:, :], kept, ALU.mult)
            then(dve.tensor_scalar(pos, pos, float(C), 1.0, ALU.min, ALU.max))
            then(dve.tensor_scalar(place, idx8, float(C), float(SLOTS - 1), ALU.mult, ALU.add))
            then(dve.tensor_tensor(place, place, pos, ALU.add))
            then(dve.tensor_tensor(target, place, token, ALU.subtract))
            then(dve.tensor_tensor(target, target, kept, ALU.mult))
            then(dve.tensor_tensor(target, target, token, ALU.add))
            dve.tensor_copy(gather_idx[:, :], place).then_inc(target_set, 1)
            dve.tensor_copy(scatter_idx[:, :], target).then_inc(target_set, 1)
            dve.wait_ge(b1_turned, 1)
            dve.tensor_copy(b1t, banks[:, 5, 0:NE * FM]).then_inc(b1_set, 1)

            def xst_out(e):
                dve.wait_ge(xs_turned, 2 * e + 2)
                dve.tensor_copy(xst[e % 2][:, 1, 0:C], banks[:, 1, 0:C]).then_inc(xst_dve, 1)

            xst_out(0)
            dve.wait_ge(b1_set, 1)
            for e in range(NE):
                for m in range(1, FM, 2):
                    g = e * FM + m
                    dve.wait_ge(hid_ready, g + 1)
                    dve.tensor_scalar(hid[e % 2][:, m, :], banks[:, 2 + g % 3, 0:C], b1t[:, g:g + 1], 0.0,
                                      ALU.add, ALU.max).then_inc(hid_dve, 1)
                if e + 1 < NE:
                    xst_out(e + 1)
                if e == 0:
                    dve.wait_ge(t["b_landed"], 32)
                if e:
                    dve.wait_ge(y_stored, 32 * e)
                for s in range(ST):
                    m = slot_rows(s)
                    dve.wait_ge(y_ready, e * ST + s + 1)
                    dve.tensor_tensor(y_st[0:m, s, :], banks[0:m, 5 + s % 2, 0:D], b2[0:m, e, :],
                                      ALU.add).then_inc(y_out, 1)
                    dve.wait_ge(y_out, e * ST + s + 1)
                    dve.tensor_tensor_reduce(out=z["junk"][0:m, :], in0=y_st[0:m, s, :], in1=z["zeros"][0:m, :],
                                             scale=1.0, scalar=0.0, op0=ALU.mult, op1=ALU.add,
                                             accum_out=finite[0:m, e * ST + s:e * ST + s + 1]).then_inc(finite_set, 1)
            dve.wait_ge(finite_set, NE * ST)
            then(dve.tensor_scalar(finite[:, :], finite[:, :], 0.0, None, ALU.is_equal))
            then(dve.tensor_reduce(finite_1[:, :], finite[:, :], AX.X, ALU.min))
            dve.tensor_scalar(bad[:, 0:1], finite_1[:, :], -1.0, 1.0, ALU.mult, ALU.add).then_inc(bad_row, 1)
            dve.wait_ge(bad_found, 1)
            dve.tensor_copy(t["bad_i"][:, :], bad[:, 1:2]).then_inc(bad_set, 1)
            dve.wait_ge(bad_set, 1)
            flag = dve.value_load(t["bad_i"][0:1, 0:1], min_val=0, max_val=1)
            with dve.If(flag > 0):
                lim = hid[0][:, 0, 0:D]
                mask = hid[0][:, 1, 0:D].bitcast(I32)
                value = hid[0][:, 2, 0:D]
                steps = [0]

                def after(ins):
                    steps[0] += 1
                    ins.then_inc(guard_step, 1)
                    dve.wait_ge(guard_step, steps[0])

                for tile in range(NT):
                    m = rows(tile)
                    dve.wait_ge(gathered[tile], 16)
                    after(dve.tensor_scalar(lim[0:m, :], back[0:m, tile, :], weight[0:m, tile:tile + 1], None, ALU.mult))
                    for op, bound, fill in ((ALU.is_gt, FMAX, 1e4), (ALU.is_lt, -FMAX, -1e4)):
                        dve.memset(value[0:m, :], fill)
                        after(dve.tensor_scalar(mask[0:m, :], lim[0:m, :], bound, None, op))
                        after(dve.copy_predicated(lim[0:m, :], mask[0:m, :], value[0:m, :]))
                    after(dve.tensor_tensor(value[0:m, :], lim[0:m, :], lim[0:m, :], ALU.is_equal))
                    after(dve.tensor_scalar(mask[0:m, :], value[0:m, :], 0.5, None, ALU.is_lt))
                    after(dve.memset(value[0:m, :], 0.0))
                    after(dve.copy_predicated(lim[0:m, :], mask[0:m, :], value[0:m, :]))
                    after(dve.tensor_tensor(x2[0:m, tile, :], lim[0:m, :], x2[0:m, tile, :], ALU.add))
                    dve.sem_inc(sum_set, 1)
            with dve.Else():
                for tile in range(NT):
                    m = rows(tile)
                    dve.wait_ge(gathered[tile], 16)
                    dve.scalar_tensor_tensor(out=x2[0:m, tile, :], in0=back[0:m, tile, :],
                                             scalar=weight[0:m, tile:tile + 1], in1=x2[0:m, tile, :],
                                             op0=ALU.mult, op1=ALU.add).then_inc(sum_set, 1)

        @block.scalar
        def _(act):
            act.wait_ge(less_set, 1)
            act.activation(ex, less, ACT.Exp).then_inc(ex_set, 1)

            def xst_out(e):
                act.wait_ge(xs_turned, 2 * e + 1)
                act.activation(xst[e % 2][:, 0, 0:C], banks[:, 0, 0:C], ACT.Copy).then_inc(xst_act, 1)

            xst_out(0)
            act.wait_ge(b1_set, 1)
            for e in range(NE):
                for m in range(0, FM, 2):
                    g = e * FM + m
                    act.wait_ge(hid_ready, g + 1)
                    act.activation(hid[e % 2][:, m, :], banks[:, 2 + g % 3, 0:C], ACT.Relu,
                                   bias=b1t[:, g:g + 1]).then_inc(hid_act, 1)
                if e + 1 < NE:
                    xst_out(e + 1)

        @block.tensor
        def _(pe):
            pe.wait_ge(t["b_landed"], 32)
            pe.transpose(banks[:, 5, 0:NE * FM], b1_rows, ident[0:NE * FM, 0:NE * FM]).then_inc(b1_turned, 1)
            pe.wait_ge(consts_set, 6)
            pe.wait_ge(hot_set, 1)
            pe.matmul(banks[:, 7, 0:NT * NE], tri, hot16, start=True, stop=True)
            pe.matmul(banks[:, 7, NT * NE:2 * NT * NE], ones, hot16, start=True, stop=True).then_inc(counted, 1)

            def turn_slots(e):
                pe.wait_ge(xs_landed[e % 2], 32 * (e // 2 + 1))
                for k in range(2):
                    if e:
                        pe.wait_ge(xst_dve if k else xst_act, e)
                    for s in range(ST):
                        m = slot_rows(s)
                        mm = pe.transpose(banks[:, k, s * P:s * P + m], xs[e % 2][0:m, s, k * P:(k + 1) * P],
                                          ident[0:m, 0:m])
                    mm.then_inc(xs_turned, 1)

            turn_slots(0)
            for e in range(NE):
                pe.wait_ge(t["w1_landed"][e], 16)
                pe.wait_ge(xst_act, e + 1)
                pe.wait_ge(xst_dve, e + 1)
                for m in range(FM):
                    g = e * FM + m
                    if g >= 3:
                        pe.wait_ge(hid_dve if (g - 3) % 2 else hid_act, (g - 3) // 2 + 1)
                    for k in range(2):
                        mm = pe.matmul(banks[:, 2 + g % 3, 0:C], w1[:, e, k, m * P:(m + 1) * P],
                                       xst[e % 2][:, k, 0:C], start=(k == 0), stop=(k == 1))
                    mm.then_inc(hid_ready, 1)
                if e + 1 < NE:
                    turn_slots(e + 1)
                pe.wait_ge(hid_act, (e + 1) * FM // 2)
                pe.wait_ge(hid_dve, (e + 1) * FM // 2)
                pe.wait_ge(t["w2_landed"][e % 2], 16 * (e // 2 + 1))
                if e == 0:
                    pe.wait_ge(b1_set, 1)
                for s in range(ST):
                    m = slot_rows(s)
                    g = e * ST + s
                    if g >= 2:
                        pe.wait_ge(y_out, g - 1)
                    for k in range(FM):
                        mm = pe.matmul(banks[0:m, 5 + s % 2, 0:D], hid[e % 2][:, k, s * P:s * P + m],
                                       w2[:, e % 2, k, :], start=(k == 0), stop=(k == FM - 1))
                    mm.then_inc(y_ready, 1)


_INS = ["x", "src", "dst", "L0_gnn_W1", "L0_gnn_b1", "L0_gnn_W2", "L0_gnn_b2", "L0_gnn_W3", "L0_gnn_b3",
        "L0_gnn_Wfc", "L0_gnn_bfc", "L0_ffn_gate_w", "L0_ffn_gate_b", "L0_ffn_w1", "L0_ffn_b1", "L0_ffn_w2",
        "L0_ffn_b2"]


def kernel(**inputs):
    import concourse.bacc as bacc
    from concourse.bass_utils import run_bass_kernel_spmd

    nc = bacc.Bacc("TRN2", target_bir_lowering=False, num_devices=1, dynamic_dma_scratch_size=4096)
    arrays, io = {}, {}
    for name in _INS:
        a = np.ascontiguousarray(inputs[name])
        arrays[f"in_{name}"] = a
        io[name] = nc.dram_tensor(f"in_{name}", a.shape, mybir.dt.from_np(a.dtype), kind="ExternalInput").ap()
    io["out"] = nc.dram_tensor("out", (N, D), F32, kind="ExternalOutput").ap()
    build(nc, io)
    r = run_bass_kernel_spmd(nc, [arrays], core_ids=[0])
    return r.results[0]["out"]
```

```python
from contextlib import ExitStack

import numpy as np

import concourse.bass as bass
from concourse import mybir

F32 = mybir.dt.float32
F32R = mybir.dt.float32r
F16 = mybir.dt.float16
I32 = mybir.dt.int32
U32 = mybir.dt.uint32
ALU = mybir.AluOpType
ACT = mybir.ActivationFunctionType
AX = mybir.AxisListType
RMAX = bass.bass_isa.ReduceOp.max

P = 128
N = 3125
D = 256
H = 512
NT = -(-N // P)
NP = NT * P
LAST = N - (NT - 1) * P

WD = 32
NW = NP // WD
WPT = P // WD
WCOL = NT * WD
KEYW = 1024
ETB = 4
ET = ETB * P
NOWHERE = 4095
GT = 4
HT = 2
OHW = WCOL + P
TBLK = 4
TURNS = -(-NT // TBLK)
PIECES = [range(2 * q, min(2 * q + 2, TURNS)) for q in range(WPT)]
MAXGROUPS = ET // GT
MAXSTEPS = 2 * NW * MAXGROUPS

KF = (D // P, H // P, H // P)
CH = 7
CS = [c * N // CH for c in range(CH + 1)]
CUTS = (0, 3, 10, NT)
NPIECE = len(CUTS) - 1
LT = 2
NG = -(-NT // LT)
GN = LT * P

NE = 8
F = 1024
FM = F // P
C = -(-5 * N // (4 * NE))
CE = C + C % 2
SLOTS = NE * C
ST = -(-C // P)
FMAX = float(np.finfo(np.float32).max)


def build(nc, io):
    E = io["src"].shape[0]
    EFULL = E // P
    EREST = E - EFULL * P
    with ExitStack() as ctx:
        def sb(name, shape, dt):
            return ctx.enter_context(nc.sbuf_tensor(name, shape, dt))

        def sem(name):
            return ctx.enter_context(nc.semaphore(name))

        t = {}
        at_at = -(-nc.sbuf_base // 32) * 32
        t["AT"] = sb("AT", [P, NT, NP], F16)
        work_at = -(-nc.sbuf_base // 32) * 32
        t["work"] = sb("work", [P, 13312], F32)

        def over_work(name, word, shape):
            return nc.alloc_sbuf_tensor_at(name, [P] + shape, F32R, offset=work_at + 4 * word)

        t["w_parts"] = [over_work(name, n * 4 * H, [4, H]) for n, name in enumerate(("w_hi", "w_lo"))]
        t["agg_parts"] = [[over_work(f"agg_{name}_{slot}", word + n * 4 * P, [4, P])
                           for n, name in enumerate(("hi", "lo"))] for slot, word in enumerate((12288, 4608, 8704))]
        t["ident"] = sb("ident", [P, P], F32)
        t["ident16"] = sb("ident16", [P, P], F16)
        t["ones16"] = sb("ones16", [P, 2], F16)
        t["zeros16"] = sb("zeros16", [P, 32], F16)
        for name, shape, dt in (
            ("stats", [P, NT, 6], F32), ("mean_var", [P, NT, 2], F32), ("rstd", [P, NT], F32),
            ("dinv", [P, NT], F32), ("logits", [P, NT, NE], F32), ("scale", [P, 3, 2], F32),
            ("stats2", [P, NT, 6], F32), ("mean_var2", [P, NT, 2], F32), ("var2", [P, NT], F32),
            ("root2", [P, NT], F32), ("rstd2", [P, NT], F32), ("newton2", [P, NT], F32), ("peak", [P, NT], F32),
            ("peak_1", [P, 1], F32), ("peak_all", [P, 1], F32), ("expo", [P, 3], I32),
            ("prob", [P, NT], F32), ("weight", [P, NT], F32), ("finite", [P, NE * ST], F32),
            ("finite_1", [P, 1], F32), ("bad", [P, 2], F32), ("bad_i", [P, 1], I32),
            ("scatter_idx", [P, NT], U32), ("gather_idx", [P, NT], U32),
        ):
            t[name] = sb(name, shape, dt)
        t["xst_parts"] = over_work("xst_parts", 2 * FM * CE, [2, 2, CE])
        t["hid_parts"] = [over_work(f"hid_{name}", n * FM * CE, [FM, CE]) for n, name in enumerate(("hi", "lo"))]
        t["h_dram"] = nc.dram_tensor("h_dram", (H // P, P, NT, P), F32).ap()
        t["agg_dram"] = nc.dram_tensor("agg_dram", (H // P, P, N), F32).ap()
        t["slots_in"] = nc.dram_tensor("slots_in", (SLOTS, D), F32).ap()
        t["slots_out"] = nc.dram_tensor("slots_out", (SLOTS, D), F32).ap()
        t["w1_landed"] = [sem("w1_landed_0"), sem("w1_landed_1")]
        t["w2_landed"] = sem("w2_landed")
        t["b_landed"] = sem("b_landed")

        free_words, at = t["AT"][:, :, :].rearrange("p t n -> p (t n)").bitcast(F32), 0
        t["free"] = {}
        for name, words, pattern, sizes in (
            ("x2", NT * D, "p (t d) -> p t d", dict(t=NT)), ("xn2", NT * D, "p (t d) -> p t d", dict(t=NT)),
            ("wfc", 4 * D, "p (k n) -> p k n", dict(k=4)), ("bfc", D, None, {}),
            ("gate_w", 2 * NE, "p (k e) -> p k e", dict(k=2)), ("gate_b", NE, None, {}),
            ("h3t", 2 * 4 * P, "p (r k m) -> p r k m", dict(r=2, k=4)),
            ("xnt", 2 * 2 * P, "p (r k m) -> p r k m", dict(r=2, k=2)), ("zeros", D, None, {}), ("junk", D, None, {}),
            ("w1_in", 2 * 2 * F, "p (r k f) -> p r k f", dict(r=2, k=2)), ("w2_in", FM * D, "p (k d) -> p k d", dict(k=FM)),
            ("w1_hi_0", 2 * F, "r", [2, F]), ("w1_lo_0", 2 * F, "r", [2, F]), ("w1_hi_1", 2 * F, "r", [2, F]),
            ("w1_lo_1", 2 * F, "r", [2, F]), ("w2_hi", FM * D, "r", [FM, D]), ("w2_lo", FM * D, "r", [FM, D]),
            ("hid_full", 3 * CE, "p (r c) -> p r c", dict(r=3)), ("y_st", ST * D, "p (s d) -> p s d", dict(s=ST)),
            ("b2", NE * D, "p (e d) -> p e d", dict(e=NE)),
            ("b1_rows", P, None, {}), ("b1t", NE * FM, None, {}), ("tri", P // 2, None, {}), ("ones", P // 2, None, {}),
            ("e_less", NT * NE, "p (t e) -> p t e", dict(t=NT)), ("valid", NT * NE, "p (t e) -> p t e", dict(t=NT)),
        ):
            v = free_words[:, at:at + words]
            if pattern == "r":
                t["free"][name] = nc.alloc_sbuf_tensor_at(name, [P] + sizes, F32R, offset=at_at + 4 * at)
            else:
                t["free"][name] = v.rearrange(pattern, **sizes) if pattern else v
            at += words
        assert at <= NT * NP // 2
        for name in ("tri", "ones"):
            t["free"][name] = t["free"][name].bitcast(F16)
        t["free"]["b1_rows"] = t["free"]["b1_rows"][0:NE * FM, :]

        adjacency(nc, io, t, E, EFULL, EREST)
        convolutions(nc, io, t)
        experts(nc, io, t)


def adjacency(nc, io, t, E, EFULL, EREST):
    with ExitStack() as ctx:
        def sb(name, shape, dt):
            return ctx.enter_context(nc.sbuf_tensor(name, shape, dt))

        def sem(name):
            return ctx.enter_context(nc.semaphore(name))

        AT, work, ident, ident16, ones16 = t["AT"], t["work"], t["ident"], t["ident16"], t["ones16"]
        zeros16 = t["zeros16"]
        stats, mean_var, rstd, dinv = t["stats"], t["mean_var"], t["rstd"], t["dinv"]

        counts = work[:, 0:3200].bitcast(F16).rearrange("p (r s d) -> p r s d", r=2, s=NT)
        row_sums = work[:, 3200:6400].rearrange("p (s d) -> p s d", s=NT)
        one_hots = work[:, 6400:6400 + GT * OHW // 2].bitcast(F16).rearrange("p (g c) -> p g c", g=GT)
        x_all = AT[:, :, :].rearrange("p t n -> p (t n)").bitcast(F32)[:, NT * NP // 2 - NT * D:].rearrange(
            "p (t d) -> p t d", t=NT)
        prep = AT[:, :, :].rearrange("p t n -> p (t n)").bitcast(I32)
        dst_i, src_i, key_i, low_i, tmp_i = (prep[:, n * ET:(n + 1) * ET] for n in range(5))
        prep_f = AT[:, :, :].rearrange("p t n -> p (t n)").bitcast(F32)
        key_f, low_f, win_f = (prep_f[:, n * ET:(n + 1) * ET] for n in range(5, 8))
        o = 8 * ET
        win_ids = prep_f[:, o:o + NW]
        tile_no = prep_f[:, o + NW:o + NW + 8]
        wmin = prep_f[:, o + NW + 8:o + NW + 12]
        wmax = prep_f[:, o + NW + 12:o + NW + 16]
        o += NW + 16
        from_lo = prep_f[:, o:o + NW * ETB].rearrange("p (w b) -> p w b", b=ETB)
        to_hi = prep_f[:, o + NW * ETB:o + 2 * NW * ETB].rearrange("p (w b) -> p w b", b=ETB)
        o += 2 * NW * ETB
        reach = prep_f[:, o:o + 2 * NW * ETB].rearrange("p (w b) -> p w b", b=ETB)
        reach_1 = prep_f[:, o + 2 * NW * ETB:o + 2 * NW * ETB + 2 * NW]
        reach_all = prep_f[:, o + 2 * NW * ETB + 2 * NW:o + 2 * NW * ETB + 4 * NW]
        lo_f = prep_f[:, o + 2 * NW * ETB + 4 * NW:o + 2 * NW * ETB + 5 * NW]
        n_f = prep_f[:, o + 2 * NW * ETB + 5 * NW:o + 2 * NW * ETB + 6 * NW]
        n_i = prep[:, o + 2 * NW * ETB + 6 * NW:o + 2 * NW * ETB + 7 * NW]

        edges = work[:, 8256:8256 + 2 * ET].rearrange("p (t k) -> p t k", k=2)
        iota16 = work[:, 9280:9280 + WCOL // 2].bitcast(F16)
        win_keys = sb("win_keys", [P, NW + WPT], F32)
        keys_now = sb("keys_now", [P, WPT], F32)
        ranges = sb("ranges", [P, NW, 2], I32)
        deg = sb("deg", [P, NT], F32)
        root = sb("root", [P, NT], F32)
        vroot = sb("vroot", [P, NT], F32)
        var = sb("var", [P, NT], F32)
        newton = sb("newton", [P, NT], F32)

        win_ps = ctx.enter_context(nc.psum_tensor("win_ps", [P, 2, 1024], F32))
        turn_ps = ctx.enter_context(nc.psum_tensor("turn_ps", [P, 2, TBLK * P], F32))
        prep_ps = ctx.enter_context(nc.psum_tensor("prep_ps", [P, 512], F32))

        edges_blank = sem("edges_blank")
        edges_in = sem("edges_in")
        x_blank = sem("x_blank")
        x_in = sem("x_in")
        pool_step = sem("pool_step")
        consts_set = sem("consts_set")
        dve_step = sem("dve_step")
        fields_set = sem("fields_set")
        turned = sem("turned")
        keys_set = sem("keys_set")
        reach_set = sem("reach_set")
        reach_max = sem("reach_max")
        ranges_set = sem("ranges_set")
        oh_ready = sem("oh_ready")
        oh_free = sem("oh_free")
        win_ready = sem("win_ready")
        win_out = sem("win_out")
        turn_ready = sem("turn_ready")
        turn_out = sem("turn_out")
        summed = sem("summed")
        node_set = sem("node_set")
        stats_set = sem("stats_set")
        roots_set = sem("roots_set")

        block = ctx.enter_context(nc.Block())

        @block.sync
        def _(sp):
            sp.wait_ge(edges_blank, 2)
            for name, ints in (("dst", dst_i), ("src", src_i)):
                full = EFULL // P * P
                sp.dma_start(ints[:, 0:full].rearrange("p (b e) -> p b e", e=P),
                             io[name][0:full * P].rearrange("(b p e) -> p b e", p=P, e=P)).then_inc(edges_in, 16)
                sp.dma_start(ints[0:EFULL - full, full:full + P],
                             io[name][full * P:EFULL * P].rearrange("(p e) -> p e", e=P)).then_inc(edges_in, 16)
                sp.dma_start(ints[EFULL - full:EFULL - full + 1, full:full + EREST],
                             io[name][EFULL * P:E].rearrange("(p e) -> p e", p=1)).then_inc(edges_in, 16)
            sp.wait_ge(x_blank, 1)
            sp.dma_start(x_all[:, 0:NT - 1, :],
                         io["x"][0:(NT - 1) * P, :].rearrange("(t p) d -> p t d", p=P)).then_inc(x_in, 16)
            sp.dma_start(x_all[0:LAST, NT - 1, :], io["x"][(NT - 1) * P:N, :]).then_inc(x_in, 16)

        @block.gpsimd
        def _(pool):
            pool.memset(dst_i[:, 3 * P:4 * P], NOWHERE).then_inc(edges_blank, 1)
            pool.memset(src_i[:, 3 * P:4 * P], NOWHERE).then_inc(edges_blank, 1)
            pool.memset(x_all[:, NT - 1, :], 0.0).then_inc(x_blank, 1)
            pool.memset(ident[:, :], 0.0).then_inc(pool_step, 1)
            pool.wait_ge(pool_step, 1)
            pool.affine_select(out=ident[:, :], in_=ident[:, :], compare_op=ALU.not_equal, fill=1.0, base=0,
                               pattern=[[-1, P]], channel_multiplier=1).then_inc(pool_step, 1)
            pool.wait_ge(pool_step, 2)
            pool.tensor_copy(ident16[:, :], ident[:, :]).then_inc(consts_set, 1)
            pool.iota(win_ids, [[1, NW]], base=0, channel_multiplier=0,
                      allow_small_or_imprecise_dtypes=True).then_inc(consts_set, 1)
            pool.iota(tile_no[:, 0:4], [[P, ETB]], base=1, channel_multiplier=1,
                      allow_small_or_imprecise_dtypes=True).then_inc(consts_set, 1)
            pool.iota(tile_no[:, 4:8], [[-P, ETB]], base=ET, channel_multiplier=-1,
                      allow_small_or_imprecise_dtypes=True).then_inc(consts_set, 1)
            pool.iota(iota16, [[1, WCOL]], base=0, channel_multiplier=0,
                      allow_small_or_imprecise_dtypes=True).then_inc(consts_set, 1)
            pool.iota(win_keys[:, :], [[KEYW, NW + WPT]], base=0, channel_multiplier=0,
                      allow_small_or_imprecise_dtypes=True).then_inc(consts_set, 1)
            pool.memset(zeros16[:, :], 0.0)
            pool.memset(ones16[:, :], 1.0).then_inc(consts_set, 1)
            pool.wait_ge(reach_set, 1)
            pool.partition_all_reduce(reach_all, reach_1, P, RMAX).then_inc(reach_max, 1)
            pool.sem_inc(summed, 1)
            pool.wait_ge(win_out, WPT)
            pool.tensor_copy(row_sums, counts[:, 0, :, :]).then_inc(summed, 1)
            with pool.Fori(0, NT // 2) as i:
                for half in range(2):
                    pool.wait_ge(win_out, (i * 2 + half + 2) * WPT)
                    pool.wait_ge(summed, i * 2 + half + 2)
                    pool.tensor_tensor(row_sums, row_sums, counts[:, 1 - half, :, :], ALU.add).then_inc(summed, 1)

        @block.vector
        def _(dve):
            done = [0]

            def then(ins):
                done[0] += 1
                ins.then_inc(dve_step, 1)
                dve.wait_ge(dve_step, done[0])

            dve.wait_ge(edges_in, 96)
            then(dve.tensor_scalar(key_i, dst_i, 5, 10, ALU.logical_shift_right, ALU.logical_shift_left))
            then(dve.tensor_scalar(tmp_i, src_i, 7, 5, ALU.logical_shift_right, ALU.logical_shift_left))
            then(dve.tensor_tensor(key_i, key_i, tmp_i, ALU.bitwise_or))
            then(dve.tensor_scalar(tmp_i, dst_i, WD - 1, None, ALU.bitwise_and))
            then(dve.tensor_tensor(key_i, key_i, tmp_i, ALU.bitwise_or))
            then(dve.tensor_scalar(low_i, src_i, P - 1, None, ALU.bitwise_and))
            then(dve.tensor_scalar(tmp_i, dst_i, 5, None, ALU.logical_shift_right))
            dve.tensor_copy(key_f, key_i).then_inc(fields_set, 1)
            dve.tensor_copy(low_f, low_i).then_inc(fields_set, 1)
            then(dve.tensor_copy(win_f, tmp_i))
            wins = win_f.rearrange("p (b e) -> p b e", b=ETB)
            then(dve.tensor_reduce(wmin, wins, AX.X, ALU.min))
            then(dve.tensor_reduce(wmax, wins, AX.X, ALU.max))
            dve.wait_ge(consts_set, 7)
            for b in range(ETB):
                dve.tensor_scalar(to_hi[:, :, b], win_ids, wmin[:, b:b + 1], tile_no[:, b:b + 1], ALU.is_ge, ALU.mult)
                then(dve.tensor_scalar(from_lo[:, :, b], win_ids, wmin[:, b:b + 1], tile_no[:, 4 + b:5 + b],
                                       ALU.is_ge, ALU.mult))
                dve.scalar_tensor_tensor(out=reach[:, 0:NW, b], in0=win_ids, scalar=wmax[:, b:b + 1],
                                         in1=to_hi[:, :, b], op0=ALU.is_le, op1=ALU.mult)
                then(dve.scalar_tensor_tensor(out=reach[:, NW:2 * NW, b], in0=win_ids, scalar=wmax[:, b:b + 1],
                                              in1=from_lo[:, :, b], op0=ALU.is_le, op1=ALU.mult))
            dve.tensor_reduce(reach_1, reach, AX.X, ALU.max).then_inc(reach_set, 1)
            dve.wait_ge(x_in, 32)
            for tile in range(NT):
                dve.bn_stats(stats[:, tile, :], x_all[:, tile, :]).then_inc(stats_set, 1)
            for n, (field, kept) in enumerate(((key_f, 0), (low_f, 1))):
                dve.wait_ge(turned, n + 1)
                dve.tensor_copy(edges[:, :, kept], prep_ps[:, :]).then_inc(keys_set, 1)
            dve.wait_ge(reach_max, 1)
            then(dve.tensor_scalar(lo_f, reach_all[:, NW:2 * NW], -1.0, float(ET), ALU.mult, ALU.add))
            then(dve.tensor_tensor(n_f, reach_all[:, 0:NW], lo_f, ALU.subtract))
            then(dve.tensor_scalar(n_f, n_f, 1.0, float(GT - 1), ALU.max, ALU.add))
            then(dve.tensor_copy(n_i, n_f))
            dve.tensor_scalar(ranges[:, :, 0], n_i, GT.bit_length() - 1, None, ALU.logical_shift_right).then_inc(ranges_set, 1)
            then(dve.tensor_scalar(lo_f, lo_f, float(ET - GT), None, ALU.min))
            dve.tensor_copy(ranges[:, :, 1], lo_f).then_inc(ranges_set, 1)
            dve.wait_ge(ranges_set, 2)
            dve.wait_ge(keys_set, 2)
            slot = dve.alloc_register("dve_slot")
            tile = dve.alloc_register("dve_edge_tile")
            range_regs = [dve.alloc_register(f"dve_range_{n}") for n in range(2 * WPT)]
            dve.reg_mov(slot, 0)

            dve.tensor_copy(keys_now[:, :], win_keys[:, 0:WPT]).then_inc(node_set, 1)
            with dve.Fori(0, NT) as d:
                dve.wait_ge(node_set, d + 1)
                dve.load(range_regs, ranges[0:1, bass.ds(d * WPT, WPT), :].rearrange("p w r -> p (w r)"))
                for q in range(WPT):
                    n = dve.snap(range_regs[2 * q], min_val=1, max_val=MAXGROUPS)
                    dve.reg_mov(tile, range_regs[2 * q + 1])
                    with dve.Fori(0, n):
                        c = dve.snap(slot, min_val=0, max_val=MAXSTEPS)
                        first = dve.snap(tile, min_val=0, max_val=ET - GT)
                        for g in range(GT):
                            if g % HT == 0:
                                dve.wait_ge(oh_free, c + (g // HT + 1))
                            dve.tensor_scalar(one_hots[:, g, 0:WCOL], iota16, keys_now[:, q:q + 1],
                                              edges[:, bass.ds(first + g, 1), 0], ALU.add, ALU.is_equal)
                            last = dve.tensor_scalar(one_hots[:, g, WCOL:OHW], iota16[:, 0:P],
                                                     edges[:, bass.ds(first + g, 1), 1], None, ALU.is_equal)
                            if g % HT == HT - 1:
                                last.then_inc(oh_ready, 1)
                        dve.reg_add(slot, slot, GT // HT)
                        dve.reg_add(tile, tile, GT)
                dve.wait_ge(oh_ready, dve.snap(slot, min_val=2 * WPT, max_val=MAXSTEPS))
                dve.tensor_copy(keys_now[:, :], win_keys[:, bass.ds(d * WPT + WPT, WPT)]).then_inc(node_set, 1)
            dve.wait_ge(stats_set, NT)
            for tile in range(NT):
                last = dve.bn_aggr(mean_var[:, tile, :], stats[:, tile, :])
            then(last)
            then(dve.tensor_scalar(var[:, :], mean_var[:, :, 1], 1e-5, None, ALU.add))
            dve.wait_ge(summed, NT + 1)
            dve.tensor_reduce(deg[:, :], row_sums, AX.X, ALU.add).then_inc(roots_set, 1)
            dve.wait_ge(roots_set, 3)
            for value, r in ((var, rstd), (deg, dinv)):
                then(dve.reciprocal(r[:, :], (vroot if r is rstd else root)[:, :]))
                then(dve.tensor_tensor(newton[:, :], r[:, :], r[:, :], ALU.mult))
                then(dve.scalar_tensor_tensor(out=newton[:, :], in0=newton[:, :], scalar=-0.5, in1=value[:, :],
                                              op0=ALU.mult, op1=ALU.mult))
                then(dve.scalar_tensor_tensor(out=r[:, :], in0=newton[:, :], scalar=1.5, in1=r[:, :],
                                              op0=ALU.add, op1=ALU.mult))

        @block.scalar
        def _(act):
            act.sem_inc(turn_out, 1)

            def window_out(d, half, q):
                act.wait_ge(win_ready, d * WPT + q + 1)
                if not isinstance(d, int) and q == 0:
                    act.wait_ge(summed, d)
                act.activation(counts[:, half, :, q * WD:(q + 1) * WD],
                               win_ps[:, q % 2, 0:WCOL].rearrange("p (s d) -> p s d", d=WD),
                               ACT.Copy).then_inc(win_out, 1)

            def turned_out(d, i):
                k = min(TBLK, NT - i * TBLK)
                act.wait_ge(turn_ready, d * TURNS + i + 1)
                into = AT[:, d:d + 1, :] if isinstance(d, int) else AT[:, bass.ds(d, 1), :]
                act.activation(into[:, :, i * TBLK * P:(i * TBLK + k) * P].rearrange("p a n -> p (a n)"),
                               turn_ps[:, i % 2, 0:k * P], ACT.Copy).then_inc(turn_out, 1)

            def destinations(d, half):
                for q in range(WPT):
                    window_out(d, half, q)
                    for i in PIECES[q]:
                        turned_out(d - 1, i)

            for q in range(WPT):
                window_out(0, 0, q)
            with act.Fori(0, NT // 2) as pair:
                for half in range(2):
                    destinations(pair * 2 + (half + 1), 1 - half)
            for i in range(TURNS):
                turned_out(NT - 1, i)
            act.wait_ge(roots_set, 1)
            act.activation(root[:, :], deg[:, :], ACT.Sqrt).then_inc(roots_set, 1)
            act.activation(vroot[:, :], var[:, :], ACT.Sqrt).then_inc(roots_set, 1)

        @block.tensor
        def _(pe):
            pe.wait_ge(consts_set, 7)
            for n, field in enumerate((key_f, low_f)):
                pe.wait_ge(fields_set, n + 1)
                if n:
                    pe.wait_ge(keys_set, n)
                for b in range(ETB):
                    mm = pe.transpose(prep_ps[:, b * P:(b + 1) * P], field[:, b * P:(b + 1) * P], ident[:, :])
                mm.then_inc(turned, 1)
            pe.wait_ge(ranges_set, 2)
            pe.sem_inc(oh_free, GT // HT)
            slot = pe.alloc_register("pe_slot")
            range_regs = [pe.alloc_register(f"pe_range_{n}") for n in range(2 * WPT)]
            pe.reg_mov(slot, 0)

            def group(q, first):
                c = pe.snap(slot, min_val=0, max_val=MAXSTEPS)
                for g in range(GT):
                    if g % HT == 0:
                        pe.wait_ge(oh_ready, c + (g // HT + 1))
                    for a, b in ((0, 512), (512, WCOL)):
                        mm = pe.matmul(win_ps[:, q % 2, a:b], one_hots[:, g, WCOL:OHW], one_hots[:, g, a:b],
                                       start=(first and g == 0), stop=False, skip_group_check=True)
                    if g % HT == HT - 1:
                        mm.then_inc(oh_free, 1)
                pe.reg_add(slot, slot, GT // HT)

            def window(d, q, n):
                if not (isinstance(d, int) and q < 2):
                    pe.wait_ge(win_out, d * WPT + q - 1)
                group(q, True)
                with pe.If(n > 1):
                    with pe.Fori(1, n):
                        group(q, False)
                into = win_ps[:, q % 2, 0:WD] if isinstance(d, int) else win_ps[:, q % 2, bass.ds(d * WD, WD)]
                pe.matmul(into, ident16[:, :], ident16[:, q * WD:(q + 1) * WD], start=False, stop=True,
                          skip_group_check=True).then_inc(win_ready, 1)

            def turn(d, half, i):
                if i == 0:
                    pe.wait_ge(win_out, (d + 1) * WPT)
                pe.wait_ge(turn_out, d * TURNS + max(i - 1, 0) + 1)
                for k in range(min(TBLK, NT - i * TBLK)):
                    mm = pe.matmul(turn_ps[:, i % 2, k * P:(k + 1) * P], counts[:, half, i * TBLK + k, :],
                                   ident16[:, :], start=True, stop=True)
                mm.then_inc(turn_ready, 1)

            def destinations(d, half):
                pe.load(range_regs, ranges[0:1, bass.ds(d * WPT, WPT), :].rearrange("p w r -> p (w r)"))
                n_of = [pe.snap(range_regs[2 * q], min_val=1, max_val=MAXGROUPS) for q in range(WPT)]
                for q in range(WPT):
                    window(d, q, n_of[q])
                    if not isinstance(d, int):
                        for i in PIECES[q]:
                            turn(d - 1, 1 - half, i)

            destinations(0, 0)
            with pe.Fori(0, NT // 2) as pair:
                for half in range(2):
                    destinations(pair * 2 + (half + 1), 1 - half)
            for i in range(TURNS):
                turn(NT - 1, 0, i)


def convolutions(nc, io, t):
    with ExitStack() as ctx:
        def sem(name):
            return ctx.enter_context(nc.semaphore(name))

        AT, work, ident, ident16 = t["AT"], t["work"], t["ident"], t["ident16"]
        mean_var, rstd, dinv, logits = t["mean_var"], t["rstd"], t["dinv"], t["logits"]
        scale, stats2, mean_var2, var2, root2, rstd2, newton2 = (
            t[name] for name in ("scale", "stats2", "mean_var2", "var2", "root2", "rstd2", "newton2"))
        h_dram, agg_dram = t["h_dram"], t["agg_dram"]

        h_in = work[:, 0:3200].rearrange("p (t f) -> p t f", t=NT)
        parts = [work[:, a:a + 3200].bitcast(F16).rearrange("p (c t f) -> p c t f", c=2, t=NT)
                 for a in (3200, 6400)]
        agg_st = work[:, 9600:9600 + N]
        w_hi, w_lo = t["w_parts"]
        agg_parts = t["agg_parts"]
        bias = work[:, 4096:4096 + H]
        w_in = work[:, 4608:4608 + 2 * H].rearrange("p (k n) -> p k n", k=2)
        agg_in = [work[:, a:a + 4 * GN].rearrange("p (k n) -> p k n", k=4) for a in range(5632, 5632 + 3 * 4 * GN, 4 * GN)]
        y_ring = work[:, 9728:9728 + 2 * H].rearrange("p (r n) -> p r n", r=2)
        h_ring = work[:, 9728 + 2 * H:9728 + 5 * H].rearrange("p (r n) -> p r n", r=3)
        z = t["free"]
        x2, xn2, wfc, bfc, gate_w, gate_b = z["x2"], z["xn2"], z["wfc"], z["bfc"], z["gate_w"], z["gate_b"]
        h3t, xnt, zeros = z["h3t"], z["xnt"], z["zeros"]

        peak, peak_1, peak_all, expo = t["peak"], t["peak_1"], t["peak_all"], t["expo"]

        banks = ctx.enter_context(nc.psum_tensor("banks", [P, 8, 512], F32))

        pads_set, pads_out = sem("pads_set"), sem("pads_out")
        h_landed = [sem(f"h_landed_{i}") for i in range(NPIECE)]
        hi_set, parts_set = sem("hi_set"), sem("parts_set")
        norm_set = sem("norm_set")
        agg_ready, agg_out_act, agg_out_dve = sem("agg_ready"), sem("agg_out_act"), sem("agg_out_dve")
        agg_stored = sem("agg_stored")
        w_landed, bias_landed = sem("w_landed"), sem("bias_landed")
        w_hi_set, w_lo_set = sem("w_hi_set"), sem("w_lo_set")
        agg_hi_set, agg_lo_set = sem("agg_hi_set"), sem("agg_lo_set")
        group_landed = [sem(f"group_landed_{i}") for i in range(3)]
        z_ready, z_out, relu_out, peak_set = sem("z_ready"), sem("z_out"), sem("relu_out"), sem("peak_set")
        h_stored = [sem(f"h_stored_{i}") for i in range(3)]
        peak_row, peak_found, scale_set = sem("peak_row"), sem("peak_found"), sem("scale_set")
        conv_step = sem("conv_step")
        xb_set, heads_landed = sem("xb_set"), sem("heads_landed")
        h3_turned, h3t_set = sem("h3_turned"), sem("h3t_set")
        o_ready, x2_set = sem("o_ready"), sem("x2_set")
        var_set, root_set, xn_set = sem("var_set"), sem("root_set"), sem("xn_set")
        xn_turned, xnt_set, logit_ready = sem("xn_turned"), sem("xnt_set"), sem("logit_ready")
        slots_blank = sem("slots_blank")
        zeros_set = sem("zeros_set")

        blocks = [(layer, j) for layer, k in enumerate(KF) for j in range(k)]
        first = [sum(KF[:layer]) for layer in range(4)]
        weights = [(io[f"L0_gnn_W{n}"], io[f"L0_gnn_b{n}"]) for n in (1, 2, 3)]
        nact, ndve = (CH + 1) // 2, CH // 2

        def rows(tile):
            return P if tile < NT - 1 else LAST

        def landed(n, i):
            return 16 * (n + 1 + (min(n + 1, KF[0]) if i == NPIECE - 1 else 0))

        block = ctx.enter_context(nc.Block())

        @block.sync
        def _(sp):
            sp.wait_ge(pads_set, 2)
            sp.dma_start(h_dram[:, LAST:P, NT - 1, :].rearrange("k p f -> p k f"),
                         y_ring[LAST:P, 0, :].rearrange("p (k f) -> p k f", k=4)).then_inc(pads_out, 16)
            stored = 0
            for layer, k in enumerate(KF):
                for j in range(k):
                    n = first[layer] + j
                    if n:
                        sp.wait_ge(parts_set, NPIECE * n)
                    if layer == 0:
                        for i, (a, b) in enumerate(zip(CUTS, CUTS[1:])):
                            full = min(b, NT - 1)
                            sp.dma_start(h_in[:, a:full, :], io["x"][a * P:full * P, j * P:(j + 1) * P]
                                         .rearrange("(t p) f -> p t f", p=P)).then_inc(h_landed[i], 16)
                        sp.dma_start(h_in[0:LAST, NT - 1, :],
                                     io["x"][(NT - 1) * P:N, j * P:(j + 1) * P]).then_inc(h_landed[NPIECE - 1], 16)
                    else:
                        if j == 0:
                            for i in range(3):
                                sp.wait_ge(h_stored[i], 16 * len(range(i, layer * NT, 3)))
                            sp.wait_ge(pads_out, 16)
                        for i, (a, b) in enumerate(zip(CUTS, CUTS[1:])):
                            sp.dma_start(h_in[:, a:b, :], h_dram[j, :, a:b, :]).then_inc(h_landed[i], 16)
                for j in range(k):
                    n = first[layer] + j
                    if n == first[layer] + k - 1:
                        sp.wait_ge(agg_ready, CH * n)
                        sp.dma_start(bias, weights[layer][1].rearrange("(o n) -> o n", o=1)
                                     .to_broadcast([P, H])).then_inc(bias_landed, 16)
                        for half in range(k // 2):
                            halves = first[layer] // 2 + half
                            if half:
                                sp.wait_ge(w_lo_set, halves)
                            sp.dma_start(w_in, weights[layer][0].rearrange("(k p) n -> p k n", p=P)
                                         [:, 2 * half:2 * half + 2, :]).then_inc(w_landed, 16)
                    for c in range(CH):
                        if c % 2:
                            sp.wait_ge(agg_out_dve, n * ndve + c // 2 + 1)
                        else:
                            sp.wait_ge(agg_out_act, n * nact + c // 2 + 1)
                        sp.dma_start(agg_dram[j, :, CS[c]:CS[c + 1]],
                                     agg_st[:, CS[c]:CS[c + 1]]).then_inc(agg_stored, 16)
                sp.wait_ge(agg_stored, 16 * CH * first[layer + 1])
                if layer == 2:
                    sp.wait_ge(zeros_set, 1)
                    full = SLOTS // P * P
                    sp.dma_start(t["slots_in"][0:full, :].rearrange("(a p) d -> p a d", p=P),
                                 zeros.rearrange("p (a d) -> p a d", a=1).to_broadcast([P, SLOTS // P, D])
                                 ).then_inc(slots_blank, 16)
                    sp.dma_start(t["slots_in"][full:SLOTS, :], zeros[0:SLOTS - full, :]).then_inc(slots_blank, 16)
                for g in range(NG + 3):
                    if g < NG:
                        if g >= 3:
                            sp.wait_ge(agg_lo_set, layer * NT + (g - 2) * LT)
                        a, b = g * GN, min(N, (g + 1) * GN)
                        sp.dma_start(agg_in[g % 3][:, 0:k, 0:b - a],
                                     agg_dram[0:k, :, a:b].rearrange("k p n -> p k n")).then_inc(group_landed[g % 3], 16)
                    if layer == 2 and g < NG:
                        tiles = range(g * LT, min(NT, (g + 1) * LT))
                        if tiles[-1] == NT - 1:
                            assert len(tiles) == 1
                            sp.dma_start(x2[0:LAST, NT - 1, :], io["x"][(NT - 1) * P:N, :]).then_inc(group_landed[g % 3], 16)
                        else:
                            sp.dma_start(x2[:, tiles[0]:tiles[-1] + 1, :], io["x"][tiles[0] * P:(tiles[-1] + 1) * P, :]
                                         .rearrange("(t p) d -> p t d", p=P)).then_inc(group_landed[g % 3], 16)
                    if layer == 2 and g == 0:
                        sp.dma_start(wfc, io["L0_gnn_Wfc"].rearrange("(k p) n -> p k n", p=P)).then_inc(heads_landed, 16)
                        sp.dma_start(bfc, io["L0_gnn_bfc"].rearrange("(o n) -> o n", o=1)
                                     .to_broadcast([P, D])).then_inc(heads_landed, 16)
                        sp.dma_start(gate_w, io["L0_ffn_gate_w"].rearrange("(k p) e -> p k e", p=P)).then_inc(heads_landed, 16)
                        sp.dma_start(gate_b, io["L0_ffn_gate_b"].rearrange("(o e) -> o e", o=1)
                                     .to_broadcast([P, NE])).then_inc(heads_landed, 16)
                    if layer == 2 and 3 <= g < 5:
                        e = g - 3
                        sp.dma_start(z["w1_in"][:, e, :, :],
                                     io["L0_ffn_w1"][e].rearrange("(k p) f -> p k f", p=P)).then_inc(t["w1_landed"][e], 16)
                    if layer == 2 and g == 5:
                        sp.dma_start(z["b2"], io["L0_ffn_b2"].rearrange("(o e) d -> o (e d)", o=1)
                                     .to_broadcast([P, NE * D])).then_inc(t["b_landed"], 16)
                        sp.dma_start(z["b1_rows"],
                                     io["L0_ffn_b1"].rearrange("e (m f) -> (e m) f", f=P)).then_inc(t["b_landed"], 16)
                        sp.dma_start(z["w2_in"], io["L0_ffn_w2"][0].rearrange("(k p) d -> p k d", p=P)
                                     ).then_inc(t["w2_landed"], 16)
                    if g >= 3 and layer < 2:
                        for tile in range((g - 3) * LT, min(NT, (g - 2) * LT)):
                            m = rows(tile)
                            sp.wait_ge(relu_out, layer * NT + tile + 1)
                            sp.dma_start(h_dram[:, 0:m, tile, :].rearrange("k p f -> p k f"),
                                         h_ring[0:m, stored % 3, :].rearrange("p (k f) -> p k f", k=4)
                                         ).then_inc(h_stored[stored % 3], 16)
                            stored += 1
            sp.wait_ge(slots_blank, 32)

        @block.gpsimd
        def _(pool):
            pool.memset(h_in[:, NT - 1, :], 0.0).then_inc(pads_set, 1)
            pool.memset(y_ring[:, 0, :], 0.0).then_inc(pads_set, 1)
            pool.memset(scale[:, 0, 0:1], 1024.0).then_inc(pads_set, 1)
            pool.memset(scale[:, 0, 1:2], 1.0 / 1024.0).then_inc(pads_set, 1)
            pool.memset(peak[:, :], 0.0).then_inc(pads_set, 1)
            for layer, k in enumerate(KF):
                if layer == 2:
                    pool.wait_ge(agg_ready, CH * len(blocks))
                    pool.memset(zeros, 0.0).then_inc(zeros_set, 1)
                    pool.memset(logits[:, :, :], 0.0).then_inc(zeros_set, 1)
                for tile in range(NT if layer < 2 else NT + 3):
                    if tile < NT:
                        m = rows(tile)
                        at = layer * NT + tile
                        a = tile % LT * P
                        pool.wait_ge(agg_hi_set, at + 1)
                        if at >= 3:
                            pool.wait_ge(z_ready, at - 2)
                        hi, lo = agg_parts[at % 3]
                        pool.tensor_tensor(lo[:, 0:k, 0:m], agg_in[tile // LT % 3][:, 0:k, a:a + m],
                                           hi[:, 0:k, 0:m].bitcast(F32), ALU.subtract).then_inc(agg_lo_set, 1)
                    if layer == 2 and tile >= 3:
                        m = rows(tile - 3)
                        if tile == 3:
                            pool.wait_ge(heads_landed, 64)
                        pool.tensor_tensor(x2[0:m, tile - 3, :], x2[0:m, tile - 3, :], bfc[0:m, :],
                                           ALU.add).then_inc(xb_set, 1)
                if layer < 2:
                    pool.wait_ge(peak_row, layer + 1)
                    pool.partition_all_reduce(peak_all[:, :], peak_1[:, :], P, RMAX).then_inc(peak_found, 1)

        @block.vector
        def _(dve):
            done = [0]

            def then(ins):
                done[0] += 1
                ins.then_inc(conv_step, 1)
                dve.wait_ge(conv_step, done[0])

            def aggregate_out(n, layer):
                for c in range(1, CH, 2):
                    dve.wait_ge(agg_ready, CH * n + c + 1)
                    if n:
                        dve.wait_ge(agg_stored, 16 * CH * n)
                    dve.tensor_scalar(agg_st[:, CS[c]:CS[c + 1]], banks[:, c, 0:CS[c + 1] - CS[c]],
                                      scale[:, layer, 1:2], None, ALU.mult).then_inc(agg_out_dve, 1)

            def residual(tile):
                m = rows(tile)
                dve.wait_ge(xb_set, tile + 1)
                dve.wait_ge(o_ready, tile + 1)
                dve.tensor_tensor(x2[0:m, tile, :], banks[0:m, 4 + tile % 2, 0:D], x2[0:m, tile, :],
                                  ALU.add).then_inc(x2_set, 1)
                dve.wait_ge(x2_set, tile + 1)
                then(dve.bn_stats(stats2[0:m, tile, :], x2[0:m, tile, :]))
                then(dve.bn_aggr(mean_var2[0:m, tile, :], stats2[0:m, tile, :]))
                dve.tensor_scalar(var2[0:m, tile:tile + 1], mean_var2[0:m, tile, 1:2], 1e-5, None,
                                  ALU.add).then_inc(var_set, 1)

            def normed(tile):
                m = rows(tile)
                v, root, r, a = (arr[0:m, tile:tile + 1] for arr in (var2, root2, rstd2, newton2))
                dve.wait_ge(root_set, tile + 1)
                then(dve.reciprocal(r, root))
                then(dve.tensor_tensor(a, r, r, ALU.mult))
                then(dve.scalar_tensor_tensor(out=a, in0=a, scalar=-0.5, in1=v, op0=ALU.mult, op1=ALU.mult))
                then(dve.scalar_tensor_tensor(out=r, in0=a, scalar=1.5, in1=r, op0=ALU.add, op1=ALU.mult))
                dve.tensor_scalar(xn2[0:m, tile, :], x2[0:m, tile, :], mean_var2[0:m, tile, 0:1], r,
                                  ALU.subtract, ALU.mult).then_inc(xn_set, 1)

            then(dve.tensor_tensor(rstd[:, :], rstd[:, :], dinv[:, :], ALU.mult))
            dve.wait_ge(pads_set, 5)
            for layer, k in enumerate(KF):
                for j in range(k):
                    n = first[layer] + j
                    for i, (a, b) in enumerate(zip(CUTS, CUTS[1:])):
                        dve.wait_ge(h_landed[i], landed(n, i))
                        if layer == 0:
                            for tile in range(a, b):
                                last = dve.tensor_scalar(h_in[:, tile, :], h_in[:, tile, :], mean_var[:, tile, 0:1],
                                                         rstd[:, tile:tile + 1], ALU.subtract, ALU.mult)
                            last.then_inc(norm_set, 1)
                        dve.wait_ge(hi_set, NPIECE * n + i + 1)
                        dve.scalar_tensor_tensor(out=parts[n % 2][:, 1, a:b, :], in0=h_in[:, a:b, :],
                                                 scalar=scale[:, layer, 0:1], in1=parts[n % 2][:, 0, a:b, :],
                                                 op0=ALU.mult, op1=ALU.subtract).then_inc(parts_set, 1)
                    if j:
                        aggregate_out(n - 1, layer)
                for half in range(k // 2):
                    halves = first[layer] // 2 + half + 1
                    dve.wait_ge(w_hi_set, halves)
                    dve.tensor_tensor(w_lo[:, 2 * half:2 * half + 2, :], w_in,
                                      w_hi[:, 2 * half:2 * half + 2, :].bitcast(F32), ALU.subtract).then_inc(w_lo_set, 1)
                aggregate_out(first[layer + 1] - 1, layer)
                dve.wait_ge(bias_landed, 16 * (layer + 1))
                for tile in range(NT + 4):
                    if tile < NT:
                        m = rows(tile)
                        at = layer * NT + tile
                        dve.wait_ge(z_ready, at + 1)
                        if at >= 2:
                            dve.wait_ge(relu_out, at - 1)
                        if tile < 2:
                            dve.wait_ge(agg_stored, 16 * CH * first[layer + 1])
                        dve.scalar_tensor_tensor(out=y_ring[0:m, at % 2, :], in0=banks[0:m, tile % 2, :],
                                                 scalar=dinv[0:m, tile:tile + 1], in1=bias[0:m, :],
                                                 op0=ALU.mult, op1=ALU.add).then_inc(z_out, 1)
                    if layer < 2 and 1 <= tile <= NT:
                        m = rows(tile - 1)
                        at = layer * NT + tile - 1
                        dve.wait_ge(relu_out, at + 1)
                        dve.tensor_reduce(peak[0:m, tile - 1:tile], h_ring[0:m, at % 3, :], AX.X,
                                          ALU.max).then_inc(peak_set, 1)
                    if layer == 2 and 0 <= tile - 2 < NT:
                        residual(tile - 2)
                    if layer == 2 and 0 <= tile - 3 < NT:
                        normed(tile - 3)
                if layer < 2:
                    dve.wait_ge(peak_set, (layer + 1) * NT)
                    dve.tensor_reduce(peak_1[:, :], peak[:, :], AX.X, ALU.max).then_inc(peak_row, 1)
                    dve.wait_ge(peak_found, layer + 1)
                    then(dve.tensor_scalar(expo[:, 0:1], peak_all[:, :].bitcast(I32), 23, None,
                                           ALU.logical_shift_right))
                    then(dve.tensor_scalar(expo[:, 1:2], expo[:, 0:1], -1.0, 268.0, ALU.mult, ALU.add))
                    then(dve.tensor_scalar(expo[:, 1:2], expo[:, 1:2], 253.0, None, ALU.min))
                    then(dve.tensor_scalar(expo[:, 2:3], expo[:, 1:2], -1.0, 254.0, ALU.mult, ALU.add))
                    dve.tensor_scalar(scale[:, layer + 1, :].bitcast(I32), expo[:, 1:3], 23, None,
                                      ALU.logical_shift_left).then_inc(scale_set, 1)
            dve.wait_ge(zeros_set, 2)
            for a, b, m in ((0, NT - 1, P), (NT - 1, NT, LAST)):
                dve.wait_ge(logit_ready, NT)
                dve.tensor_tensor(logits[0:m, a:b, :],
                                  banks[0:m, 7, a * NE:b * NE].rearrange("p (t e) -> p t e", e=NE),
                                  gate_b[0:m, :].rearrange("p (o e) -> p o e", o=1).to_broadcast([m, b - a, NE]),
                                  ALU.add).then_inc(conv_step, 1)

        @block.scalar
        def _(act):
            def aggregate_out(n, layer):
                for c in range(0, CH, 2):
                    act.wait_ge(agg_ready, CH * n + c + 1)
                    if n:
                        act.wait_ge(agg_stored, 16 * CH * n)
                    else:
                        act.wait_ge(pads_out, 16)
                    act.activation(agg_st[:, CS[c]:CS[c + 1]], banks[:, c, 0:CS[c + 1] - CS[c]], ACT.Copy,
                                   scale=scale[:, layer, 1:2]).then_inc(agg_out_act, 1)

            def agg_high(layer, tile):
                m = rows(tile)
                at = layer * NT + tile
                g = tile // LT
                a = tile % LT * P
                act.wait_ge(group_landed[g % 3], 16 * (layer * len(range(g % 3, NG, 3)) + (g // 3 + 1) * (1 + layer // 2)))
                if at >= 3:
                    act.wait_ge(z_ready, at - 2)
                act.activation(agg_parts[at % 3][0][:, 0:KF[layer], 0:m], agg_in[g % 3][:, 0:KF[layer], a:a + m],
                               ACT.Copy).then_inc(agg_hi_set, 1)

            def turned_out(tile):
                m = rows(tile)
                act.wait_ge(h3_turned, tile + 1)
                if tile >= 2:
                    act.wait_ge(o_ready, tile - 1)
                act.activation(h3t[:, tile % 2, :, 0:m],
                               banks[:, 2 + tile % 2, :].rearrange("p (k m) -> p k m", k=4)[:, :, 0:m],
                               ACT.Copy).then_inc(h3t_set, 1)

            def root(tile):
                m = rows(tile)
                act.wait_ge(var_set, tile + 1)
                act.activation(root2[0:m, tile:tile + 1], var2[0:m, tile:tile + 1], ACT.Sqrt).then_inc(root_set, 1)

            def xn_out(tile):
                m = rows(tile)
                act.wait_ge(xn_turned, tile + 1)
                if tile >= 2:
                    act.wait_ge(logit_ready, tile - 1)
                act.activation(xnt[:, tile % 2, :, 0:m],
                               banks[:, 6, :].rearrange("p (r k m) -> p r k m", r=2, k=2)[:, tile % 2, :, 0:m],
                               ACT.Copy).then_inc(xnt_set, 1)

            act.wait_ge(pads_set, 5)
            for layer, k in enumerate(KF):
                if layer:
                    act.wait_ge(scale_set, layer)
                for j in range(k):
                    n = first[layer] + j
                    for i, (a, b) in enumerate(zip(CUTS, CUTS[1:])):
                        act.wait_ge(h_landed[i], landed(n, i))
                        if layer == 0:
                            act.wait_ge(norm_set, NPIECE * n + i + 1)
                        if n >= 2:
                            act.wait_ge(agg_ready, CH * (n - 1))
                        act.activation(parts[n % 2][:, 0, a:b, :], h_in[:, a:b, :], ACT.Copy,
                                       scale=scale[:, layer, 0:1]).then_inc(hi_set, 1)
                    if j:
                        aggregate_out(n - 1, layer)
                act.wait_ge(parts_set, NPIECE * first[layer + 1])
                for half in range(k // 2):
                    act.wait_ge(w_landed, 16 * (first[layer] // 2 + half + 1))
                    act.activation(w_hi[:, 2 * half:2 * half + 2, :], w_in, ACT.Copy).then_inc(w_hi_set, 1)
                aggregate_out(first[layer + 1] - 1, layer)
                act.wait_ge(agg_stored, 16 * CH * first[layer + 1])
                agg_high(layer, 0)
                agg_high(layer, 1)
                for tile in range(NT + 5):
                    m = rows(tile)
                    at = layer * NT + tile
                    if tile + 2 < NT:
                        agg_high(layer, tile + 2)
                    if tile < NT:
                        act.wait_ge(z_out, at + 1)
                    if tile >= NT:
                        pass
                    elif layer < 2:
                        if at >= 3:
                            act.wait_ge(h_stored[at % 3], 16 * (at // 3))
                            act.wait_ge(peak_set, at - 2)
                        act.activation(h_ring[0:m, at % 3, :], y_ring[0:m, at % 2, :], ACT.Relu,
                                       scale=dinv[0:m, tile:tile + 1]).then_inc(relu_out, 1)
                    else:
                        if tile >= 3:
                            act.wait_ge(h3_turned, tile - 2)
                        else:
                            act.wait_ge(h_stored[at % 3], 16 * (at // 3))
                            act.wait_ge(peak_set, 2 * NT)
                        act.activation(h_ring[0:m, at % 3, :], y_ring[0:m, at % 2, :],
                                       ACT.Relu).then_inc(relu_out, 1)
                    if layer == 2:
                        if 0 <= tile - 1 < NT:
                            turned_out(tile - 1)
                        if 0 <= tile - 3 < NT:
                            root(tile - 3)
                        if 0 <= tile - 4 < NT:
                            xn_out(tile - 4)

        @block.tensor
        def _(pe):
            def turn_h3(tile):
                m = rows(tile)
                pe.wait_ge(relu_out, 2 * NT + tile + 1)
                if tile >= 2:
                    pe.wait_ge(h3t_set, tile - 1)
                for kk in range(4):
                    mm = pe.transpose(banks[:, 2 + tile % 2, kk * P:kk * P + m],
                                      h_ring[0:m, (2 * NT + tile) % 3, kk * P:(kk + 1) * P], ident[0:m, 0:m])
                mm.then_inc(h3_turned, 1)

            def head(tile):
                m = rows(tile)
                if tile == 0:
                    pe.wait_ge(heads_landed, 64)
                pe.wait_ge(h3t_set, tile + 1)
                if tile >= 2:
                    pe.wait_ge(x2_set, tile - 1)
                for kk in range(4):
                    mm = pe.matmul(banks[0:m, 4 + tile % 2, 0:D], h3t[:, tile % 2, kk, 0:m], wfc[:, kk, :],
                                   start=(kk == 0), stop=(kk == 3))
                mm.then_inc(o_ready, 1)

            def turn_xn(tile):
                m = rows(tile)
                pe.wait_ge(xn_set, tile + 1)
                if tile:
                    pe.wait_ge(xnt_set, tile)
                for kk in range(2):
                    mm = pe.transpose(banks[:, 6, (tile % 2) * 2 * P + kk * P:(tile % 2) * 2 * P + kk * P + m],
                                      xn2[0:m, tile, kk * P:(kk + 1) * P], ident[0:m, 0:m])
                mm.then_inc(xn_turned, 1)

            def gate(tile):
                m = rows(tile)
                pe.wait_ge(xnt_set, tile + 1)
                for kk in range(2):
                    mm = pe.matmul(banks[0:m, 7, tile * NE:(tile + 1) * NE], xnt[:, tile % 2, kk, 0:m],
                                   gate_w[:, kk, :], start=(kk == 0), stop=(kk == 1))
                mm.then_inc(logit_ready, 1)

            for layer, k in enumerate(KF):
                for j in range(k):
                    n = first[layer] + j
                    pe.wait_ge(parts_set, NPIECE * n + 1)
                    for c in range(CH):
                        if n:
                            pe.wait_ge(agg_out_dve if c % 2 else agg_out_act,
                                       (n - 1) * (ndve if c % 2 else nact) + c // 2 + 1)
                        for part in range(2):
                            pe.matmul(banks[:, c, 0:CS[c + 1] - CS[c]], parts[n % 2][:, part, 0, :],
                                      AT[:, 0, CS[c]:CS[c + 1]], start=(part == 0), stop=False)
                    for i in range(NPIECE):
                        if i:
                            pe.wait_ge(parts_set, NPIECE * n + i + 1)
                        with pe.Fori(max(1, CUTS[i]), min(NT - 1, CUTS[i + 1])) as d:
                            for part in range(2):
                                for c in range(CH):
                                    pe.matmul(banks[:, c, 0:CS[c + 1] - CS[c]],
                                              parts[n % 2][:, part, bass.ds(d, 1), :].rearrange("p a f -> p (a f)"),
                                              AT[:, bass.ds(d, 1), CS[c]:CS[c + 1]].rearrange("p a n -> p (a n)"),
                                              start=False, stop=False)
                    for c in range(CH):
                        for part in range(2):
                            mm = pe.matmul(banks[:, c, 0:CS[c + 1] - CS[c]], parts[n % 2][:, part, NT - 1, :],
                                           AT[:, NT - 1, CS[c]:CS[c + 1]], start=False, stop=(part == 1))
                        mm.then_inc(agg_ready, 1)
                pe.wait_ge(agg_out_act, first[layer + 1] * nact)
                pe.wait_ge(agg_out_dve, first[layer + 1] * ndve)
                pe.wait_ge(w_lo_set, first[layer + 1] // 2)
                for tile in range(NT if layer < 2 else NT + 5):
                    if tile < NT:
                        m = rows(tile)
                        at = layer * NT + tile
                        pe.wait_ge(agg_lo_set, at + 1)
                        if tile >= 2:
                            pe.wait_ge(z_out, at - 1)
                        hi, lo = agg_parts[at % 3]
                        for kk in range(k):
                            for a, b in ((hi, w_hi), (hi, w_lo), (lo, w_hi)):
                                mm = pe.matmul(banks[0:m, tile % 2, :], a[:, kk, 0:m], b[:, kk, :],
                                               start=(kk == 0 and b is w_hi and a is hi),
                                               stop=(kk == k - 1 and a is lo))
                        mm.then_inc(z_ready, 1)
                    if layer == 2:
                        for stage, lag in ((turn_h3, 1), (head, 2), (turn_xn, 4), (gate, 5)):
                            if 0 <= tile - lag < NT:
                                stage(tile - lag)


def experts(nc, io, t):
    with ExitStack() as ctx:
        def sem(name):
            return ctx.enter_context(nc.semaphore(name))

        work, ident, logits, z = t["work"], t["ident"], t["logits"], t["free"]
        slots_in, slots_out = t["slots_in"], t["slots_out"]
        x2, xn2, w1_in, w2_in, b2, b1_rows, b1t = (z[n] for n in ("x2", "xn2", "w1_in", "w2_in", "b2", "b1_rows", "b1t"))
        w1_parts = [[z["w1_hi_0"], z["w1_lo_0"]], [z["w1_hi_1"], z["w1_lo_1"]]]
        w2_hi, w2_lo = z["w2_hi"], z["w2_lo"]
        xst_hi, xst_lo = (t["xst_parts"][:, n] for n in range(2))
        hid_hi, hid_lo = t["hid_parts"]
        hid_full, y_st = z["hid_full"], z["y_st"]
        tri, ones, e_less, valid = z["tri"], z["ones"], z["e_less"], z["valid"]
        back = xn2

        a = 2 * FM * CE + 4 * CE
        xs = [work[:, a + n * 1024:a + (n + 1) * 1024].rearrange("p (s d) -> p s d", s=ST) for n in range(2)]
        gate_words = [0]

        def small(*shape, dt=F32):
            n = int(np.prod(shape))
            lo = gate_words[0]
            gate_words[0] += n
            v = work[:, lo:lo + n]
            v = v if dt is F32 else v.bitcast(dt)
            return v if len(shape) == 1 else v.rearrange("p (t e) -> p t e", e=shape[1])

        less, ex, pr, eq, cand, hot, tot, run_a, run_b, cum = (small(NT, NE) for _ in range(10))
        top, total, inv, idx8, pos, kept, place, token, target = (small(NT) for _ in range(9))
        hot16 = small(NT * NE // 2).bitcast(F16)
        scatter_idx, gather_idx = t["scatter_idx"], t["gather_idx"]
        prob, weight, finite, finite_1, bad = (t[n] for n in ("prob", "weight", "finite", "finite_1", "bad"))

        banks = ctx.enter_context(nc.psum_tensor("expert_banks", [P, 8, 512], F32))

        consts_set, pool_step, gate_step = sem("ffn_consts_set"), sem("ffn_pool_step"), sem("gate_step")
        less_set, ex_set, hot_set, counted = sem("less_set"), sem("ex_set"), sem("hot_set"), sem("counted")
        target_set, scattered = sem("target_set"), sem("scattered")
        b1_turned, b1_set = sem("b1_turned"), sem("b1_set")
        xs_landed = [sem("xs_landed_0"), sem("xs_landed_1")]
        xs_turned, xst_pad = sem("xs_turned"), sem("xst_pad")
        xst_hi_set, xst_lo_set = sem("xst_hi_set"), sem("xst_lo_set")
        w1_hi_set, w1_lo_set, w2_hi_set, w2_lo_set = (sem(f"ffn_{n}_set") for n in ("w1_hi", "w1_lo", "w2_hi", "w2_lo"))
        hid_ready, hid_full_set = sem("hid_ready"), sem("hid_full_set")
        hid_hi_set, hid_lo_set = sem("hid_hi_set"), sem("hid_lo_set")
        y_ready, y_out, y_stored = sem("y_ready"), sem("y_out"), sem("y_stored")
        finite_set, bad_row, bad_found, bad_set = sem("finite_set"), sem("bad_row"), sem("bad_found"), sem("bad_set")
        gathered = [sem(f"gathered_{i}") for i in range(NT)]
        sum_set, out_stored, guard_step = sem("sum_set"), sem("out_stored"), sem("guard_step")

        def rows(tile):
            return P if tile < NT - 1 else LAST

        def slot_rows(s):
            return min(P, C - s * P)

        def whole(dram, e, tiles, to_sbuf):
            if tiles == "full":
                return dram[e * C:e * C + (ST - 1) * P, :].rearrange("(s p) d -> p s d", p=P)
            return dram[e * C + (ST - 1) * P:(e + 1) * C, :]

        block = ctx.enter_context(nc.Block())

        @block.sync
        def _(sp):
            def load_slots(e):
                if e >= 2:
                    sp.wait_ge(xs_turned, 2 * (e - 1))
                sp.dma_start(xs[e % 2][:, 0:ST - 1, :], whole(slots_in, e, "full", True)).then_inc(xs_landed[e % 2], 16)
                sp.dma_start(xs[e % 2][0:slot_rows(ST - 1), ST - 1, :],
                             whole(slots_in, e, "rest", True)).then_inc(xs_landed[e % 2], 16)

            sp.wait_ge(scattered, 16 * NT)
            load_slots(0)
            load_slots(1)
            for e in range(NE):
                if e + 2 < NE:
                    sp.wait_ge(w1_lo_set, e + 1)
                    sp.dma_start(w1_in[:, e % 2, :, :], io["L0_ffn_w1"][e + 2].rearrange("(k p) f -> p k f", p=P)
                                 ).then_inc(t["w1_landed"][e % 2], 16)
                    load_slots(e + 2)
                if e + 1 < NE:
                    sp.wait_ge(w2_lo_set, 2 * (e + 1))
                    sp.dma_start(w2_in, io["L0_ffn_w2"][e + 1].rearrange("(k p) d -> p k d", p=P)
                                 ).then_inc(t["w2_landed"], 16)
                sp.wait_ge(y_out, ST * (e + 1))
                sp.dma_start(whole(slots_out, e, "full", False), y_st[:, 0:ST - 1, :]).then_inc(y_stored, 16)
                sp.dma_start(whole(slots_out, e, "rest", False),
                             y_st[0:slot_rows(ST - 1), ST - 1, :]).then_inc(y_stored, 16)
            for tile in range(NT):
                m = rows(tile)
                sp.wait_ge(sum_set, tile + 1)
                sp.dma_start(io["out"][tile * P:tile * P + m, :], x2[0:m, tile, :]).then_inc(out_stored, 16)
            sp.wait_ge(out_stored, 16 * NT)

        @block.gpsimd
        def _(pool):
            if CE > C:
                for part in (xst_hi, xst_lo):
                    pool.memset(part[:, :, C:CE].bitcast(F32), 0.0).then_inc(xst_pad, 1)
            pool.iota(e_less, [[0, NT], [1, NE]], base=-NE, channel_multiplier=0,
                      allow_small_or_imprecise_dtypes=True).then_inc(consts_set, 1)
            pool.iota(token, [[P, NT]], base=SLOTS, channel_multiplier=1,
                      allow_small_or_imprecise_dtypes=True).then_inc(consts_set, 1)
            pool.memset(finite[:, :], 0.0).then_inc(consts_set, 1)
            pool.memset(valid, 1.0).then_inc(pool_step, 1)
            pool.memset(tri, 1.0).then_inc(pool_step, 1)
            pool.memset(ones, 1.0).then_inc(consts_set, 1)
            pool.wait_ge(pool_step, 2)
            pool.affine_select(out=valid[:, NT - 1, :], in_=valid[:, NT - 1, :], compare_op=ALU.is_ge, fill=0.0,
                               base=LAST - 1, pattern=[[0, NE]], channel_multiplier=-1).then_inc(consts_set, 1)
            pool.affine_select(out=tri, in_=tri, compare_op=ALU.is_ge, fill=0.0, base=0, pattern=[[1, P]],
                               channel_multiplier=-1).then_inc(consts_set, 1)
            pool.wait_ge(target_set, 2)
            for tile in range(NT):
                m = rows(tile)
                pool.indirect_dma_start(
                    out=slots_in[:, :], out_offset=bass.IndirectOffsetOnAxis(ap=scatter_idx[0:m, tile:tile + 1], axis=0),
                    in_=xn2[0:m, tile, :], in_offset=None, bounds_check=SLOTS - 1, oob_is_err=False,
                ).then_inc(scattered, 16)
            pool.wait_ge(bad_row, 1)
            pool.partition_all_reduce(bad[:, 1:2], bad[:, 0:1], P, RMAX).then_inc(bad_found, 1)
            pool.wait_ge(y_stored, 32 * NE)
            for tile in range(NT):
                m = rows(tile)
                pool.indirect_dma_start(
                    out=back[0:m, tile, :], out_offset=None, in_=slots_out[:, :],
                    in_offset=bass.IndirectOffsetOnAxis(ap=gather_idx[0:m, tile:tile + 1], axis=0),
                ).then_inc(gathered[tile], 16)

        @block.vector
        def _(dve):
            done = [0]

            def then(ins):
                done[0] += 1
                ins.then_inc(gate_step, 1)
                dve.wait_ge(gate_step, done[0])

            def by_expert(v):
                return v.rearrange("p (t o) -> p t o", o=1).to_broadcast([P, NT, NE])

            then(dve.tensor_reduce(top, logits[:, :, :], AX.X, ALU.max))
            dve.tensor_tensor(less, logits[:, :, :], by_expert(top), ALU.subtract).then_inc(less_set, 1)
            dve.wait_ge(ex_set, 1)
            then(dve.tensor_reduce(total, ex, AX.X, ALU.add))
            then(dve.reciprocal(inv, total))
            then(dve.tensor_tensor(pr, ex, by_expert(inv), ALU.mult))
            then(dve.tensor_reduce(prob[:, :], pr, AX.X, ALU.max))
            then(dve.tensor_tensor(eq, pr, by_expert(prob[:, :]), ALU.is_equal))
            dve.wait_ge(consts_set, 6)
            then(dve.tensor_tensor(cand, eq, e_less, ALU.mult))
            then(dve.tensor_reduce(idx8, cand, AX.X, ALU.min))
            then(dve.tensor_tensor(hot, e_less, by_expert(idx8), ALU.is_equal))
            then(dve.tensor_tensor(hot, hot, valid, ALU.mult))
            dve.tensor_copy(hot16, hot.rearrange("p t e -> p (t e)")).then_inc(hot_set, 1)
            dve.wait_ge(counted, 1)
            dve.tensor_copy(cum.rearrange("p t e -> p (t e)"), banks[:, 7, 0:NT * NE])
            dve.tensor_copy(tot.rearrange("p t e -> p (t e)"), banks[:, 7, NT * NE:2 * NT * NE])
            then(dve.tensor_copy(run_a.rearrange("p t e -> p (t e)"), banks[:, 7, NT * NE:2 * NT * NE]))
            src, dst, width = run_a, run_b, 1
            while width < NT:
                dve.tensor_copy(dst[:, 0:width, :], src[:, 0:width, :])
                then(dve.tensor_tensor(dst[:, width:NT, :], src[:, width:NT, :], src[:, 0:NT - width, :], ALU.add))
                src, dst, width = dst, src, 2 * width
            then(dve.tensor_tensor(src, src, tot, ALU.subtract))
            then(dve.tensor_tensor(src, src, cum, ALU.add))
            then(dve.tensor_tensor(src, src, hot, ALU.mult))
            then(dve.tensor_reduce(pos, src, AX.X, ALU.add))
            then(dve.tensor_scalar(kept, pos, float(C), None, ALU.is_le))
            dve.tensor_tensor(weight[:, :], prob[:, :], kept, ALU.mult)
            then(dve.tensor_scalar(pos, pos, float(C), 1.0, ALU.min, ALU.max))
            then(dve.tensor_scalar(place, idx8, float(C), float(SLOTS - 1), ALU.mult, ALU.add))
            then(dve.tensor_tensor(place, place, pos, ALU.add))
            then(dve.tensor_tensor(target, place, token, ALU.subtract))
            then(dve.tensor_tensor(target, target, kept, ALU.mult))
            then(dve.tensor_tensor(target, target, token, ALU.add))
            dve.tensor_copy(gather_idx[:, :], place).then_inc(target_set, 1)
            dve.tensor_copy(scatter_idx[:, :], target).then_inc(target_set, 1)
            dve.wait_ge(b1_turned, 1)
            dve.tensor_copy(b1t, banks[:, 5, 0:NE * FM]).then_inc(b1_set, 1)

            def xst_low(e):
                for k in range(2):
                    dve.wait_ge(xst_hi_set, 2 * e + k + 1)
                    dve.tensor_tensor(xst_lo[:, k, 0:C], banks[:, k, 0:C], xst_hi[:, k, 0:C].bitcast(F32),
                                      ALU.subtract).then_inc(xst_lo_set, 1)

            def w1_low(e):
                dve.wait_ge(w1_hi_set, e + 1)
                dve.tensor_tensor(w1_parts[e % 2][1][:, :, :], w1_in[:, e % 2, :, :],
                                  w1_parts[e % 2][0][:, :, :].bitcast(F32), ALU.subtract).then_inc(w1_lo_set, 1)

            w1_low(0)
            xst_low(0)
            for e in range(NE):
                for m in range(FM):
                    g = e * FM + m
                    dve.wait_ge(hid_hi_set, g + 1)
                    dve.tensor_tensor(hid_lo[:, m, 0:C], hid_full[:, g % 3, 0:C], hid_hi[:, m, 0:C].bitcast(F32),
                                      ALU.subtract).then_inc(hid_lo_set, 1)
                    if m < 4:
                        half = slice(m // 2 * FM // 2, (m // 2 + 1) * FM // 2)
                        if m == 0:
                            dve.wait_ge(t["w2_landed"], 16 * (e + 1))
                        if m % 2 == 0:
                            dve.tensor_copy(w2_hi[:, half, :], w2_in[:, half, :]).then_inc(w2_hi_set, 1)
                        else:
                            dve.wait_ge(w2_hi_set, 2 * e + m // 2 + 1)
                            dve.tensor_tensor(w2_lo[:, half, :], w2_in[:, half, :], w2_hi[:, half, :].bitcast(F32),
                                              ALU.subtract).then_inc(w2_lo_set, 1)
                if e + 1 < NE:
                    xst_low(e + 1)
                    w1_low(e + 1)
                if e == 0:
                    dve.wait_ge(t["b_landed"], 32)
                if e:
                    dve.wait_ge(y_stored, 32 * e)
                for s in range(ST):
                    m = slot_rows(s)
                    dve.wait_ge(y_ready, e * ST + s + 1)
                    dve.tensor_tensor(y_st[0:m, s, :], banks[0:m, 5 + s % 2, 0:D], b2[0:m, e, :],
                                      ALU.add).then_inc(y_out, 1)
                    dve.wait_ge(y_out, e * ST + s + 1)
                    dve.tensor_tensor_reduce(out=z["junk"][0:m, :], in0=y_st[0:m, s, :], in1=z["zeros"][0:m, :],
                                             scale=1.0, scalar=0.0, op0=ALU.mult, op1=ALU.add,
                                             accum_out=finite[0:m, e * ST + s:e * ST + s + 1]).then_inc(finite_set, 1)
            dve.wait_ge(finite_set, NE * ST)
            then(dve.tensor_scalar(finite[:, :], finite[:, :], 0.0, None, ALU.is_equal))
            then(dve.tensor_reduce(finite_1[:, :], finite[:, :], AX.X, ALU.min))
            dve.tensor_scalar(bad[:, 0:1], finite_1[:, :], -1.0, 1.0, ALU.mult, ALU.add).then_inc(bad_row, 1)
            dve.wait_ge(bad_found, 1)
            dve.tensor_copy(t["bad_i"][:, :], bad[:, 1:2]).then_inc(bad_set, 1)
            dve.wait_ge(bad_set, 1)
            flag = dve.value_load(t["bad_i"][0:1, 0:1], min_val=0, max_val=1)
            with dve.If(flag > 0):
                lim = xs[0][:, 0, :]
                mask = xs[0][:, 1, :].bitcast(I32)
                value = xs[0][:, 2, :]
                steps = [0]

                def after(ins):
                    steps[0] += 1
                    ins.then_inc(guard_step, 1)
                    dve.wait_ge(guard_step, steps[0])

                for tile in range(NT):
                    m = rows(tile)
                    dve.wait_ge(gathered[tile], 16)
                    after(dve.tensor_scalar(lim[0:m, :], back[0:m, tile, :], weight[0:m, tile:tile + 1], None, ALU.mult))
                    for op, bound, fill in ((ALU.is_gt, FMAX, 1e4), (ALU.is_lt, -FMAX, -1e4)):
                        dve.memset(value[0:m, :], fill)
                        after(dve.tensor_scalar(mask[0:m, :], lim[0:m, :], bound, None, op))
                        after(dve.copy_predicated(lim[0:m, :], mask[0:m, :], value[0:m, :]))
                    after(dve.tensor_tensor(value[0:m, :], lim[0:m, :], lim[0:m, :], ALU.is_equal))
                    after(dve.tensor_scalar(mask[0:m, :], value[0:m, :], 0.5, None, ALU.is_lt))
                    after(dve.memset(value[0:m, :], 0.0))
                    after(dve.copy_predicated(lim[0:m, :], mask[0:m, :], value[0:m, :]))
                    after(dve.tensor_tensor(x2[0:m, tile, :], lim[0:m, :], x2[0:m, tile, :], ALU.add))
                    dve.sem_inc(sum_set, 1)
            with dve.Else():
                for tile in range(NT):
                    m = rows(tile)
                    dve.wait_ge(gathered[tile], 16)
                    dve.scalar_tensor_tensor(out=x2[0:m, tile, :], in0=back[0:m, tile, :],
                                             scalar=weight[0:m, tile:tile + 1], in1=x2[0:m, tile, :],
                                             op0=ALU.mult, op1=ALU.add).then_inc(sum_set, 1)

        @block.scalar
        def _(act):
            act.wait_ge(less_set, 1)
            act.activation(ex, less, ACT.Exp).then_inc(ex_set, 1)

            def xst_high(e):
                for k in range(2):
                    act.wait_ge(xs_turned, 2 * e + k + 1)
                    act.activation(xst_hi[:, k, 0:C], banks[:, k, 0:C], ACT.Copy).then_inc(xst_hi_set, 1)

            def w1_high(e):
                act.wait_ge(t["w1_landed"][e % 2], 16 * (e // 2 + 1))
                act.activation(w1_parts[e % 2][0][:, :, :], w1_in[:, e % 2, :, :], ACT.Copy).then_inc(w1_hi_set, 1)

            def hid_high(g):
                act.wait_ge(hid_full_set, g + 1)
                act.activation(hid_hi[:, g % FM, 0:C], hid_full[:, g % 3, 0:C], ACT.Copy).then_inc(hid_hi_set, 1)

            w1_high(0)
            xst_high(0)
            act.wait_ge(b1_set, 1)
            for e in range(NE):
                for m in range(FM):
                    g = e * FM + m
                    act.wait_ge(hid_ready, g + 1)
                    if g >= 3:
                        act.wait_ge(hid_lo_set, g - 2)
                    act.activation(hid_full[:, g % 3, 0:C], banks[:, 2 + g % 3, 0:C], ACT.Relu,
                                   bias=b1t[:, g:g + 1]).then_inc(hid_full_set, 1)
                    if m:
                        hid_high(g - 1)
                hid_high(g)
                if e + 1 < NE:
                    xst_high(e + 1)
                    w1_high(e + 1)

        @block.tensor
        def _(pe):
            pe.wait_ge(t["b_landed"], 32)
            pe.transpose(banks[:, 5, 0:NE * FM], b1_rows, ident[0:NE * FM, 0:NE * FM]).then_inc(b1_turned, 1)
            pe.wait_ge(consts_set, 6)
            pe.wait_ge(hot_set, 1)
            pe.matmul(banks[:, 7, 0:NT * NE], tri, hot16, start=True, stop=True)
            pe.matmul(banks[:, 7, NT * NE:2 * NT * NE], ones, hot16, start=True, stop=True).then_inc(counted, 1)

            def turn_slots(e):
                pe.wait_ge(xs_landed[e % 2], 32 * (e // 2 + 1))
                for k in range(2):
                    if e:
                        pe.wait_ge(xst_lo_set, 2 * (e - 1) + k + 1)
                    for s in range(ST):
                        m = slot_rows(s)
                        mm = pe.transpose(banks[:, k, s * P:s * P + m], xs[e % 2][0:m, s, k * P:(k + 1) * P],
                                          ident[0:m, 0:m])
                    mm.then_inc(xs_turned, 1)

            turn_slots(0)
            for e in range(NE):
                pe.wait_ge(w1_lo_set, e + 1)
                pe.wait_ge(xst_lo_set, 2 * e + 2)
                if e == 0 and CE > C:
                    pe.wait_ge(xst_pad, 2)
                w1_hi, w1_lo = w1_parts[e % 2]
                for m in range(FM):
                    g = e * FM + m
                    if g >= 3:
                        pe.wait_ge(hid_full_set, g - 2)
                    for k in range(2):
                        for a, b in ((w1_hi, xst_hi), (w1_hi, xst_lo), (w1_lo, xst_hi)):
                            mm = pe.matmul(banks[:, 2 + g % 3, 0:CE], a[:, k, m * P:(m + 1) * P], b[:, k, :],
                                           start=(k == 0 and a is w1_hi and b is xst_hi),
                                           stop=(k == 1 and a is w1_lo))
                    mm.then_inc(hid_ready, 1)
                if e + 1 < NE:
                    turn_slots(e + 1)
                pe.wait_ge(w2_lo_set, 2 * (e + 1))
                if e == 0:
                    pe.wait_ge(b1_set, 1)
                for s in range(ST):
                    m = slot_rows(s)
                    g = e * ST + s
                    if g >= 2:
                        pe.wait_ge(y_out, g - 1)
                    for k in range(FM):
                        if s == 0:
                            pe.wait_ge(hid_lo_set, e * FM + k + 1)
                        for a, b in ((hid_hi, w2_hi), (hid_hi, w2_lo), (hid_lo, w2_hi)):
                            mm = pe.matmul(banks[0:m, 5 + s % 2, 0:D], a[:, k, s * P:s * P + m], b[:, k, :],
                                           start=(k == 0 and a is hid_hi and b is w2_hi),
                                           stop=(k == FM - 1 and a is hid_lo))
                    mm.then_inc(y_ready, 1)


_INS = ["x", "src", "dst", "L0_gnn_W1", "L0_gnn_b1", "L0_gnn_W2", "L0_gnn_b2", "L0_gnn_W3", "L0_gnn_b3",
        "L0_gnn_Wfc", "L0_gnn_bfc", "L0_ffn_gate_w", "L0_ffn_gate_b", "L0_ffn_w1", "L0_ffn_b1", "L0_ffn_w2",
        "L0_ffn_b2"]


def kernel(**inputs):
    import concourse.bacc as bacc
    from concourse.bass_utils import run_bass_kernel_spmd

    nc = bacc.Bacc("TRN2", target_bir_lowering=False, num_devices=1, dynamic_dma_scratch_size=4096)
    arrays, io = {}, {}
    for name in _INS:
        a = np.ascontiguousarray(inputs[name])
        arrays[f"in_{name}"] = a
        io[name] = nc.dram_tensor(f"in_{name}", a.shape, mybir.dt.from_np(a.dtype), kind="ExternalInput").ap()
    io["out"] = nc.dram_tensor("out", (N, D), F32, kind="ExternalOutput").ap()
    build(nc, io)
    r = run_bass_kernel_spmd(nc, [arrays], core_ids=[0])
    return r.results[0]["out"]
```

```python
from contextlib import ExitStack

import numpy as np

import concourse.bass as bass
from concourse import mybir

F32 = mybir.dt.float32
F32R = mybir.dt.float32r
F16 = mybir.dt.float16
I32 = mybir.dt.int32
U32 = mybir.dt.uint32
ALU = mybir.AluOpType
ACT = mybir.ActivationFunctionType
AX = mybir.AxisListType
RMAX = bass.bass_isa.ReduceOp.max

P = 128
N = 3125
D = 256
H = 512
NT = -(-N // P)
assert NT % 2 == 1
NP = NT * P
LAST = N - (NT - 1) * P

WD = 32
NW = NP // WD
WPT = P // WD
WCOL = NT * WD
KEYW = 1024
ETB = 4
ET = ETB * P
NOWHERE = 4095
GT = 4
HT = 2
OHW = WCOL + P
TBLK = 4
TURNS = -(-NT // TBLK)
PIECES = [range(2 * q, min(2 * q + 2, TURNS)) for q in range(WPT)]
MAXGROUPS = ET // GT
MAXSTEPS = 2 * NW * MAXGROUPS

KF = (D // P, H // P, H // P)
CH = 7
CS = [c * N // CH for c in range(CH + 1)]
CUTS = (0, 2, 8, NT)
NPIECE = len(CUTS) - 1
LT = 2
NG = -(-NT // LT)
GN = LT * P

NE = 8
F = 1024
FM = F // P
C = -(-5 * N // (4 * NE))
CE = C + C % 2
SLOTS = NE * C
ROW = D + 2
ST = -(-C // P)
FMAX = float(np.finfo(np.float32).max)


def build(nc, io):
    E = io["src"].shape[0]
    EFULL = E // P
    EREST = E - EFULL * P
    with ExitStack() as ctx:
        def sb(name, shape, dt):
            return ctx.enter_context(nc.sbuf_tensor(name, shape, dt))

        def sem(name):
            return ctx.enter_context(nc.semaphore(name))

        t = {}
        at_at = -(-nc.sbuf_base // 32) * 32
        t["AT"] = sb("AT", [P, NT, NP], F16)
        work_at = -(-nc.sbuf_base // 32) * 32
        t["work"] = sb("work", [P, 13312], F32)

        def over_work(name, word, shape):
            return nc.alloc_sbuf_tensor_at(name, [P] + shape, F32R, offset=work_at + 4 * word)

        t["w_parts"] = [over_work(name, n * 4 * H, [4, H]) for n, name in enumerate(("w_hi", "w_lo"))]
        t["agg_parts"] = [[over_work(f"agg_{name}_{slot}", word + n * 4 * P, [4, P])
                           for n, name in enumerate(("hi", "lo"))] for slot, word in enumerate((12288, 4608, 8704))]
        t["ident"] = sb("ident", [P, P], F32)
        t["ident16"] = sb("ident16", [P, P], F16)
        for name, shape, dt in (
            ("stats", [P, NT, 6], F32), ("mean_var", [P, NT, 2], F32), ("rstd", [P, NT], F32),
            ("dinv", [P, NT], F32), ("logits", [P, NT, NE], F32), ("scale", [P, 3, 2], F32),
            ("stats2", [P, NT, 6], F32), ("mean_var2", [P, NT, 2], F32), ("var2", [P, NT], F32),
            ("root2", [P, NT], F32), ("rstd2", [P, NT], F32), ("newton2", [P, NT], F32), ("peak", [P, NT], F32),
            ("peak_1", [P, 1], F32), ("peak_all", [P, 1], F32), ("expo", [P, 3], I32),
            ("prob", [P, NT], F32), ("weight", [P, NT], F32), ("finite", [P, NE * ST], F32),
            ("finite_1", [P, 1], F32), ("bad", [P, 2], F32), ("bad_i", [P, 1], I32),
            ("scatter_idx", [P, NT], U32), ("gather_idx", [P, NT], U32),
            ("nobody", [P, ST], F32), ("filled", [P, ST], F32), ("slot_token", [P, ST], F32),
            ("token_idx", [P, 2, ST], U32),
        ):
            t[name] = sb(name, shape, dt)
        t["xst_parts"] = over_work("xst_parts", 2 * FM * CE, [2, 2, CE])
        t["hid_parts"] = [over_work(f"hid_{name}", n * FM * CE, [FM, CE]) for n, name in enumerate(("hi", "lo"))]
        t["h_dram"] = nc.dram_tensor("h_dram", (H // P, P, NT, P), F32).ap()
        t["agg_dram"] = nc.dram_tensor("agg_dram", (H // P, P, N), F32).ap()
        t["slots_in"] = nc.dram_tensor("slots_in", (SLOTS, ROW), F32).ap()
        t["x2_dram"] = nc.dram_tensor("x2_dram", (N, D), F32).ap()
        t["slots_out"] = nc.dram_tensor("slots_out", (SLOTS, D), F32).ap()
        t["w1_landed"] = [sem("w1_landed_0"), sem("w1_landed_1")]
        t["w2_landed"] = sem("w2_landed")
        t["b_landed"] = sem("b_landed")

        free_words, at = t["AT"][:, :, :].rearrange("p t n -> p (t n)").bitcast(F32), 0
        t["free"] = {}
        for name, words, pattern, sizes in (
            ("x2", NT * D, "p (t d) -> p t d", dict(t=NT)),
            ("wfc", 4 * D, "p (k n) -> p k n", dict(k=4)), ("bfc", D, None, {}),
            ("gate_w", 2 * NE, "p (k e) -> p k e", dict(k=2)), ("gate_b", NE, None, {}),
            ("xnt", 2 * 2 * P, "p (r k m) -> p r k m", dict(r=2, k=2)), ("junk", D, None, {}),
            ("w1_in", 2 * 2 * F, "p (r k f) -> p r k f", dict(r=2, k=2)), ("w2_in", FM * D, "p (k d) -> p k d", dict(k=FM)),
            ("w1_hi_0", 2 * F, "r", [2, F]), ("w1_lo_0", 2 * F, "r", [2, F]), ("w1_hi_1", 2 * F, "r", [2, F]),
            ("w1_lo_1", 2 * F, "r", [2, F]), ("w2_hi", FM * D, "r", [FM, D]), ("w2_lo", FM * D, "r", [FM, D]),
            ("hid_full", 3 * CE, "p (r c) -> p r c", dict(r=3)), ("y_st", ST * D, "p (s d) -> p s d", dict(s=ST)),
            ("b2", NE * D, "p (e d) -> p e d", dict(e=NE)),
            ("b1_rows", P, None, {}), ("b1t", NE * FM, None, {}), ("tri", P // 2, None, {}), ("ones", P // 2, None, {}),
            ("e_less", NT * NE, "p (t e) -> p t e", dict(t=NT)), ("e_valid", NT * NE, "p (t e) -> p t e", dict(t=NT)),
            ("xn2", NT * ROW, "p (t d) -> p t d", dict(t=NT)), ("zeros", ROW, None, {}),
        ):
            if name == "w2_hi":
                w2_word = at
            v = free_words[:, at:at + words]
            if pattern == "r":
                t["free"][name] = nc.alloc_sbuf_tensor_at(name, [P] + sizes, F32R, offset=at_at + 4 * at)
            else:
                t["free"][name] = v.rearrange(pattern, **sizes) if pattern else v
            at += words
        assert at <= NT * NP // 2
        w2_at = at_at + 4 * w2_word
        t["wfc_parts"] = [nc.alloc_sbuf_tensor_at(f"wfc_{name}", [P, 4, D], F32R, offset=w2_at + n * 16 * D)
                          for n, name in enumerate(("hi", "lo"))]
        t["h3t_parts"] = [[nc.alloc_sbuf_tensor_at(f"h3t_{name}_{slot}", [P, 4, P], F32R,
                                                   offset=w2_at + 32 * D + (2 * slot + n) * 16 * P)
                           for n, name in enumerate(("hi", "lo"))] for slot in range(2)]
        assert 8 * D + 16 * P <= 2 * FM * D
        for name in ("tri", "ones"):
            t["free"][name] = t["free"][name].bitcast(F16)
        t["free"]["b1_rows"] = t["free"]["b1_rows"][0:NE * FM, :]

        adjacency(nc, io, t, E, EFULL, EREST)
        convolutions(nc, io, t)
        experts(nc, io, t)


def adjacency(nc, io, t, E, EFULL, EREST):
    with ExitStack() as ctx:
        def sb(name, shape, dt):
            return ctx.enter_context(nc.sbuf_tensor(name, shape, dt))

        def sem(name):
            return ctx.enter_context(nc.semaphore(name))

        AT, work, ident, ident16 = t["AT"], t["work"], t["ident"], t["ident16"]
        stats, mean_var, rstd, dinv = t["stats"], t["mean_var"], t["rstd"], t["dinv"]

        counts = work[:, 0:3200].bitcast(F16).rearrange("p (r s d) -> p r s d", r=2, s=NT)
        row_sums = work[:, 3200:6400].rearrange("p (s d) -> p s d", s=NT)
        one_hots = work[:, 6400:6400 + GT * OHW // 2].bitcast(F16).rearrange("p (g c) -> p g c", g=GT)
        x_all = AT[:, :, :].rearrange("p t n -> p (t n)").bitcast(F32)[:, NT * NP // 2 - NT * D:].rearrange(
            "p (t d) -> p t d", t=NT)
        prep = AT[:, :, :].rearrange("p t n -> p (t n)").bitcast(I32)
        dst_i, src_i, key_i, low_i, tmp_i = (prep[:, n * ET:(n + 1) * ET] for n in range(5))
        prep_f = AT[:, :, :].rearrange("p t n -> p (t n)").bitcast(F32)
        key_f, low_f, win_f = (prep_f[:, n * ET:(n + 1) * ET] for n in range(5, 8))
        o = 8 * ET
        win_ids = prep_f[:, o:o + NW]
        tile_no = prep_f[:, o + NW:o + NW + 8]
        wmin = prep_f[:, o + NW + 8:o + NW + 12]
        wmax = prep_f[:, o + NW + 12:o + NW + 16]
        o += NW + 16
        from_lo = prep_f[:, o:o + NW * ETB].rearrange("p (w b) -> p w b", b=ETB)
        to_hi = prep_f[:, o + NW * ETB:o + 2 * NW * ETB].rearrange("p (w b) -> p w b", b=ETB)
        o += 2 * NW * ETB
        reach = prep_f[:, o:o + 2 * NW * ETB].rearrange("p (w b) -> p w b", b=ETB)
        reach_1 = prep_f[:, o + 2 * NW * ETB:o + 2 * NW * ETB + 2 * NW]
        reach_all = prep_f[:, o + 2 * NW * ETB + 2 * NW:o + 2 * NW * ETB + 4 * NW]
        lo_f = prep_f[:, o + 2 * NW * ETB + 4 * NW:o + 2 * NW * ETB + 5 * NW]
        n_f = prep_f[:, o + 2 * NW * ETB + 5 * NW:o + 2 * NW * ETB + 6 * NW]
        n_i = prep[:, o + 2 * NW * ETB + 6 * NW:o + 2 * NW * ETB + 7 * NW]

        edges = work[:, 8256:8256 + 2 * ET].rearrange("p (t k) -> p t k", k=2)
        iota16 = work[:, 9280:9280 + WCOL // 2].bitcast(F16)
        win_keys = sb("win_keys", [P, NW], F32)
        ranges = sb("ranges", [P, NW, 2], I32)
        deg = sb("deg", [P, NT], F32)
        root = sb("root", [P, NT], F32)
        vroot = sb("vroot", [P, NT], F32)
        var = sb("var", [P, NT], F32)
        newton = sb("newton", [P, NT], F32)

        win_ps = ctx.enter_context(nc.psum_tensor("win_ps", [P, 2, 1024], F32))
        turn_ps = ctx.enter_context(nc.psum_tensor("turn_ps", [P, 2, TBLK * P], F32))
        prep_ps = ctx.enter_context(nc.psum_tensor("prep_ps", [P, 512], F32))

        edges_blank = sem("edges_blank")
        edges_in = sem("edges_in")
        x_blank = sem("x_blank")
        x_in = sem("x_in")
        pool_step = sem("pool_step")
        consts_set = sem("consts_set")
        dve_step = sem("dve_step")
        fields_set = sem("fields_set")
        turned = sem("turned")
        keys_set = sem("keys_set")
        reach_set = sem("reach_set")
        reach_max = sem("reach_max")
        ranges_set = sem("ranges_set")
        oh_ready = sem("oh_ready")
        oh_free = sem("oh_free")
        win_ready = sem("win_ready")
        win_out = sem("win_out")
        turn_ready = sem("turn_ready")
        turn_out = sem("turn_out")
        summed = sem("summed")
        stats_set = sem("stats_set")
        roots_set = sem("roots_set")

        block = ctx.enter_context(nc.Block())

        @block.sync
        def _(sp):
            sp.wait_ge(edges_blank, 2)
            for name, ints in (("dst", dst_i), ("src", src_i)):
                full = EFULL // P * P
                sp.dma_start(ints[:, 0:full].rearrange("p (b e) -> p b e", e=P),
                             io[name][0:full * P].rearrange("(b p e) -> p b e", p=P, e=P)).then_inc(edges_in, 16)
                sp.dma_start(ints[0:EFULL - full, full:full + P],
                             io[name][full * P:EFULL * P].rearrange("(p e) -> p e", e=P)).then_inc(edges_in, 16)
                sp.dma_start(ints[EFULL - full:EFULL - full + 1, full:full + EREST],
                             io[name][EFULL * P:E].rearrange("(p e) -> p e", p=1)).then_inc(edges_in, 16)
            sp.wait_ge(x_blank, 1)
            sp.dma_start(x_all[:, 0:NT - 1, :],
                         io["x"][0:(NT - 1) * P, :].rearrange("(t p) d -> p t d", p=P)).then_inc(x_in, 16)
            sp.dma_start(x_all[0:LAST, NT - 1, :], io["x"][(NT - 1) * P:N, :]).then_inc(x_in, 16)

        @block.gpsimd
        def _(pool):
            pool.memset(dst_i[:, 3 * P:4 * P], NOWHERE).then_inc(edges_blank, 1)
            pool.memset(src_i[:, 3 * P:4 * P], NOWHERE).then_inc(edges_blank, 1)
            pool.memset(x_all[:, NT - 1, :], 0.0).then_inc(x_blank, 1)
            pool.memset(ident[:, :], 0.0).then_inc(pool_step, 1)
            pool.wait_ge(pool_step, 1)
            pool.affine_select(out=ident[:, :], in_=ident[:, :], compare_op=ALU.not_equal, fill=1.0, base=0,
                               pattern=[[-1, P]], channel_multiplier=1).then_inc(pool_step, 1)
            pool.wait_ge(pool_step, 2)
            pool.tensor_copy(ident16[:, :], ident[:, :]).then_inc(consts_set, 1)
            pool.iota(win_ids, [[1, NW]], base=0, channel_multiplier=0,
                      allow_small_or_imprecise_dtypes=True).then_inc(consts_set, 1)
            pool.iota(tile_no[:, 0:4], [[P, ETB]], base=1, channel_multiplier=1,
                      allow_small_or_imprecise_dtypes=True).then_inc(consts_set, 1)
            pool.iota(tile_no[:, 4:8], [[-P, ETB]], base=ET, channel_multiplier=-1,
                      allow_small_or_imprecise_dtypes=True).then_inc(consts_set, 1)
            pool.iota(iota16, [[1, WCOL]], base=0, channel_multiplier=0,
                      allow_small_or_imprecise_dtypes=True).then_inc(consts_set, 1)
            pool.iota(win_keys[:, :], [[KEYW, NW]], base=0, channel_multiplier=0,
                      allow_small_or_imprecise_dtypes=True).then_inc(consts_set, 1)
            pool.wait_ge(reach_set, 1)
            pool.partition_all_reduce(reach_all, reach_1, P, RMAX).then_inc(reach_max, 1)
            pool.sem_inc(summed, 1)
            pool.wait_ge(win_out, WPT)
            pool.tensor_copy(row_sums, counts[:, 0, :, :]).then_inc(summed, 1)

            def add(i, half):
                pool.wait_ge(win_out, (i * 2 + half + 2) * WPT)
                pool.wait_ge(summed, i * 2 + half + 2)
                pool.tensor_tensor(row_sums, row_sums, counts[:, 1 - half, :, :], ALU.add).then_inc(summed, 1)

            with pool.Fori(0, NT // 2 - 1) as i:
                for half in range(2):
                    add(i, half)
            add(NT // 2 - 1, 0)

        @block.vector
        def _(dve):
            done = [0]

            def then(ins):
                done[0] += 1
                ins.then_inc(dve_step, 1)
                dve.wait_ge(dve_step, done[0])

            dve.wait_ge(edges_in, 96)
            then(dve.tensor_scalar(key_i, dst_i, 5, 10, ALU.logical_shift_right, ALU.logical_shift_left))
            then(dve.tensor_scalar(tmp_i, src_i, 7, 5, ALU.logical_shift_right, ALU.logical_shift_left))
            then(dve.tensor_tensor(key_i, key_i, tmp_i, ALU.bitwise_or))
            then(dve.tensor_scalar(tmp_i, dst_i, WD - 1, None, ALU.bitwise_and))
            then(dve.tensor_tensor(key_i, key_i, tmp_i, ALU.bitwise_or))
            then(dve.tensor_scalar(low_i, src_i, P - 1, None, ALU.bitwise_and))
            then(dve.tensor_scalar(tmp_i, dst_i, 5, None, ALU.logical_shift_right))
            dve.tensor_copy(key_f, key_i).then_inc(fields_set, 1)
            dve.tensor_copy(low_f, low_i).then_inc(fields_set, 1)
            then(dve.tensor_copy(win_f, tmp_i))
            wins = win_f.rearrange("p (b e) -> p b e", b=ETB)
            then(dve.tensor_reduce(wmin, wins, AX.X, ALU.min))
            then(dve.tensor_reduce(wmax, wins, AX.X, ALU.max))
            dve.wait_ge(consts_set, 6)
            for b in range(ETB):
                dve.tensor_scalar(to_hi[:, :, b], win_ids, wmin[:, b:b + 1], tile_no[:, b:b + 1], ALU.is_ge, ALU.mult)
                then(dve.tensor_scalar(from_lo[:, :, b], win_ids, wmin[:, b:b + 1], tile_no[:, 4 + b:5 + b],
                                       ALU.is_ge, ALU.mult))
                dve.scalar_tensor_tensor(out=reach[:, 0:NW, b], in0=win_ids, scalar=wmax[:, b:b + 1],
                                         in1=to_hi[:, :, b], op0=ALU.is_le, op1=ALU.mult)
                then(dve.scalar_tensor_tensor(out=reach[:, NW:2 * NW, b], in0=win_ids, scalar=wmax[:, b:b + 1],
                                              in1=from_lo[:, :, b], op0=ALU.is_le, op1=ALU.mult))
            dve.tensor_reduce(reach_1, reach, AX.X, ALU.max).then_inc(reach_set, 1)
            dve.wait_ge(x_in, 32)
            for tile in range(NT):
                dve.bn_stats(stats[:, tile, :], x_all[:, tile, :]).then_inc(stats_set, 1)
            for n, (field, kept) in enumerate(((key_f, 0), (low_f, 1))):
                dve.wait_ge(turned, n + 1)
                dve.tensor_copy(edges[:, :, kept], prep_ps[:, :]).then_inc(keys_set, 1)
            dve.wait_ge(reach_max, 1)
            then(dve.tensor_scalar(lo_f, reach_all[:, NW:2 * NW], -1.0, float(ET), ALU.mult, ALU.add))
            then(dve.tensor_tensor(n_f, reach_all[:, 0:NW], lo_f, ALU.subtract))
            then(dve.tensor_scalar(n_f, n_f, 1.0, float(GT - 1), ALU.max, ALU.add))
            then(dve.tensor_copy(n_i, n_f))
            dve.tensor_scalar(ranges[:, :, 0], n_i, GT.bit_length() - 1, None, ALU.logical_shift_right).then_inc(ranges_set, 1)
            then(dve.tensor_scalar(lo_f, lo_f, float(ET - GT), None, ALU.min))
            dve.tensor_copy(ranges[:, :, 1], lo_f).then_inc(ranges_set, 1)
            dve.wait_ge(ranges_set, 2)
            dve.wait_ge(keys_set, 2)
            slot = dve.alloc_register("dve_slot")
            tile = dve.alloc_register("dve_edge_tile")
            range_regs = [dve.alloc_register(f"dve_range_{n}") for n in range(2 * WPT)]
            dve.reg_mov(slot, 0)

            with dve.Fori(0, NT) as d:
                dve.load(range_regs, ranges[0:1, bass.ds(d * WPT, WPT), :].rearrange("p w r -> p (w r)"))
                for q in range(WPT):
                    n = dve.snap(range_regs[2 * q], min_val=1, max_val=MAXGROUPS)
                    dve.reg_mov(tile, range_regs[2 * q + 1])
                    with dve.Fori(0, n):
                        c = dve.snap(slot, min_val=0, max_val=MAXSTEPS)
                        first = dve.snap(tile, min_val=0, max_val=ET - GT)
                        for g in range(GT):
                            if g % HT == 0:
                                dve.wait_ge(oh_free, c + (g // HT + 1))
                            dve.tensor_scalar(one_hots[:, g, 0:WCOL], iota16, win_keys[:, bass.ds(d * WPT + q, 1)],
                                              edges[:, bass.ds(first + g, 1), 0], ALU.add, ALU.is_equal)
                            last = dve.tensor_scalar(one_hots[:, g, WCOL:OHW], iota16[:, 0:P],
                                                     edges[:, bass.ds(first + g, 1), 1], None, ALU.is_equal)
                            if g % HT == HT - 1:
                                last.then_inc(oh_ready, 1)
                        dve.reg_add(slot, slot, GT // HT)
                        dve.reg_add(tile, tile, GT)
            dve.wait_ge(stats_set, NT)
            for tile in range(NT):
                last = dve.bn_aggr(mean_var[:, tile, :], stats[:, tile, :])
            then(last)
            then(dve.tensor_scalar(var[:, :], mean_var[:, :, 1], 1e-5, None, ALU.add))
            dve.wait_ge(summed, NT)
            then(dve.tensor_reduce(deg[:, :], row_sums, AX.X, ALU.add))
            dve.wait_ge(win_out, NT * WPT)
            then(dve.tensor_reduce(newton[:, :], counts[:, 0, :, :], AX.X, ALU.add))
            dve.tensor_tensor(deg[:, :], deg[:, :], newton[:, :], ALU.add).then_inc(roots_set, 1)
            dve.wait_ge(roots_set, 3)
            for value, r in ((var, rstd), (deg, dinv)):
                then(dve.reciprocal(r[:, :], (vroot if r is rstd else root)[:, :]))
                then(dve.tensor_tensor(newton[:, :], r[:, :], r[:, :], ALU.mult))
                then(dve.scalar_tensor_tensor(out=newton[:, :], in0=newton[:, :], scalar=-0.5, in1=value[:, :],
                                              op0=ALU.mult, op1=ALU.mult))
                then(dve.scalar_tensor_tensor(out=r[:, :], in0=newton[:, :], scalar=1.5, in1=r[:, :],
                                              op0=ALU.add, op1=ALU.mult))

        @block.scalar
        def _(act):
            act.sem_inc(turn_out, 1)

            def window_out(d, half, q):
                act.wait_ge(win_ready, d * WPT + q + 1)
                if not isinstance(d, int) and q == 0:
                    act.wait_ge(summed, d)
                act.activation(counts[:, half, :, q * WD:(q + 1) * WD],
                               win_ps[:, q % 2, 0:WCOL].rearrange("p (s d) -> p s d", d=WD),
                               ACT.Copy).then_inc(win_out, 1)

            def turned_out(d, i):
                k = min(TBLK, NT - i * TBLK)
                act.wait_ge(turn_ready, d * TURNS + i + 1)
                into = AT[:, d:d + 1, :] if isinstance(d, int) else AT[:, bass.ds(d, 1), :]
                act.activation(into[:, :, i * TBLK * P:(i * TBLK + k) * P].rearrange("p a n -> p (a n)"),
                               turn_ps[:, i % 2, 0:k * P], ACT.Copy).then_inc(turn_out, 1)

            def destinations(d, half):
                for q in range(WPT):
                    window_out(d, half, q)
                    for i in PIECES[q]:
                        turned_out(d - 1, i)

            for q in range(WPT):
                window_out(0, 0, q)
            with act.Fori(0, NT // 2) as pair:
                for half in range(2):
                    destinations(pair * 2 + (half + 1), 1 - half)
            for i in range(TURNS):
                turned_out(NT - 1, i)
            act.wait_ge(roots_set, 1)
            act.activation(root[:, :], deg[:, :], ACT.Sqrt).then_inc(roots_set, 1)
            act.activation(vroot[:, :], var[:, :], ACT.Sqrt).then_inc(roots_set, 1)

        @block.tensor
        def _(pe):
            pe.wait_ge(consts_set, 6)
            for n, field in enumerate((key_f, low_f)):
                pe.wait_ge(fields_set, n + 1)
                if n:
                    pe.wait_ge(keys_set, n)
                for b in range(ETB):
                    mm = pe.transpose(prep_ps[:, b * P:(b + 1) * P], field[:, b * P:(b + 1) * P], ident[:, :])
                mm.then_inc(turned, 1)
            pe.wait_ge(ranges_set, 2)
            pe.sem_inc(oh_free, GT // HT)
            slot = pe.alloc_register("pe_slot")
            range_regs = [pe.alloc_register(f"pe_range_{n}") for n in range(2 * WPT)]
            pe.reg_mov(slot, 0)

            def group(q, first):
                c = pe.snap(slot, min_val=0, max_val=MAXSTEPS)
                for g in range(GT):
                    if g % HT == 0:
                        pe.wait_ge(oh_ready, c + (g // HT + 1))
                    for a, b in ((0, 512), (512, WCOL)):
                        mm = pe.matmul(win_ps[:, q % 2, a:b], one_hots[:, g, WCOL:OHW], one_hots[:, g, a:b],
                                       start=(first and g == 0), stop=False, skip_group_check=True)
                    if g % HT == HT - 1:
                        mm.then_inc(oh_free, 1)
                pe.reg_add(slot, slot, GT // HT)

            def window(d, q, n):
                if not (isinstance(d, int) and q < 2):
                    pe.wait_ge(win_out, d * WPT + q - 1)
                group(q, True)
                with pe.If(n > 1):
                    with pe.Fori(1, n):
                        group(q, False)
                into = win_ps[:, q % 2, 0:WD] if isinstance(d, int) else win_ps[:, q % 2, bass.ds(d * WD, WD)]
                pe.matmul(into, ident16[:, :], ident16[:, q * WD:(q + 1) * WD], start=False, stop=True,
                          skip_group_check=True).then_inc(win_ready, 1)

            def turn(d, half, i):
                if i == 0:
                    pe.wait_ge(win_out, (d + 1) * WPT)
                pe.wait_ge(turn_out, d * TURNS + max(i - 1, 0) + 1)
                for k in range(min(TBLK, NT - i * TBLK)):
                    mm = pe.matmul(turn_ps[:, i % 2, k * P:(k + 1) * P], counts[:, half, i * TBLK + k, :],
                                   ident16[:, :], start=True, stop=True)
                mm.then_inc(turn_ready, 1)

            def destinations(d, half):
                pe.load(range_regs, ranges[0:1, bass.ds(d * WPT, WPT), :].rearrange("p w r -> p (w r)"))
                n_of = [pe.snap(range_regs[2 * q], min_val=1, max_val=MAXGROUPS) for q in range(WPT)]
                for q in range(WPT):
                    window(d, q, n_of[q])
                    if not isinstance(d, int):
                        for i in PIECES[q]:
                            turn(d - 1, 1 - half, i)

            destinations(0, 0)
            with pe.Fori(0, NT // 2) as pair:
                for half in range(2):
                    destinations(pair * 2 + (half + 1), 1 - half)
            for i in range(TURNS):
                turn(NT - 1, 0, i)


def convolutions(nc, io, t):
    with ExitStack() as ctx:
        def sem(name):
            return ctx.enter_context(nc.semaphore(name))

        AT, work, ident, ident16 = t["AT"], t["work"], t["ident"], t["ident16"]
        mean_var, rstd, dinv, logits = t["mean_var"], t["rstd"], t["dinv"], t["logits"]
        scale, stats2, mean_var2, var2, root2, rstd2, newton2 = (
            t[name] for name in ("scale", "stats2", "mean_var2", "var2", "root2", "rstd2", "newton2"))
        h_dram, agg_dram = t["h_dram"], t["agg_dram"]

        h_in = work[:, 0:3200].rearrange("p (t f) -> p t f", t=NT)
        parts = [work[:, a:a + 3200].bitcast(F16).rearrange("p (c t f) -> p c t f", c=2, t=NT)
                 for a in (3200, 6400)]
        agg_st = work[:, 9600:9600 + N]
        w_hi, w_lo = t["w_parts"]
        agg_parts = t["agg_parts"]
        bias = work[:, 4096:4096 + H]
        w_in = work[:, 4608:4608 + 2 * H].rearrange("p (k n) -> p k n", k=2)
        agg_in = [work[:, a:a + 4 * GN].rearrange("p (k n) -> p k n", k=4) for a in range(5632, 5632 + 3 * 4 * GN, 4 * GN)]
        y_ring = work[:, 9728:9728 + 2 * H].rearrange("p (r n) -> p r n", r=2)
        h_ring = work[:, 9728 + 2 * H:9728 + 5 * H].rearrange("p (r n) -> p r n", r=3)
        z = t["free"]
        x2, xn2, wfc, bfc, gate_w, gate_b = z["x2"], z["xn2"], z["wfc"], z["bfc"], z["gate_w"], z["gate_b"]
        xnt, zeros = z["xnt"], z["zeros"]
        wfc_hi, wfc_lo = t["wfc_parts"]
        h3t_parts = t["h3t_parts"]

        peak, peak_1, peak_all, expo = t["peak"], t["peak_1"], t["peak_all"], t["expo"]

        banks = ctx.enter_context(nc.psum_tensor("banks", [P, 8, 512], F32))

        pads_set, pads_out = sem("pads_set"), sem("pads_out")
        h_landed = [sem(f"h_landed_{i}") for i in range(NPIECE)]
        hi_set, parts_set = sem("hi_set"), sem("parts_set")
        norm_set = sem("norm_set")
        agg_ready, agg_out_act, agg_out_dve = sem("agg_ready"), sem("agg_out_act"), sem("agg_out_dve")
        agg_stored = [sem(f"agg_stored_{c}") for c in range(CH)]
        w_landed, bias_landed = sem("w_landed"), sem("bias_landed")
        w_hi_set, w_lo_set = sem("w_hi_set"), sem("w_lo_set")
        agg_hi_set, agg_lo_set = sem("agg_hi_set"), sem("agg_lo_set")
        group_landed = [sem(f"group_landed_{i}") for i in range(3)]
        z_ready, z_out, relu_out, peak_set = sem("z_ready"), sem("z_out"), sem("relu_out"), sem("peak_set")
        h_stored = [sem(f"h_stored_{i}") for i in range(3)]
        peak_row, peak_found, scale_set = sem("peak_row"), sem("peak_found"), sem("scale_set")
        conv_step = sem("conv_step")
        xb_set, heads_landed = sem("xb_set"), sem("heads_landed")
        wfc_hi_set, wfc_lo_set = sem("wfc_hi_set"), sem("wfc_lo_set")
        h3_turned, h3t_hi_set, h3t_lo_set = sem("h3_turned"), sem("h3t_hi_set"), sem("h3t_lo_set")
        o_ready, x2_set = sem("o_ready"), sem("x2_set")
        var_set, root_set, xn_set = sem("var_set"), sem("root_set"), sem("xn_set")
        xn_turned, xnt_set, logit_ready = sem("xn_turned"), sem("xnt_set"), sem("logit_ready")
        slots_blank = sem("slots_blank")
        zeros_set = sem("zeros_set")

        blocks = [(layer, j) for layer, k in enumerate(KF) for j in range(k)]
        first = [sum(KF[:layer]) for layer in range(4)]
        weights = [(io[f"L0_gnn_W{n}"], io[f"L0_gnn_b{n}"]) for n in (1, 2, 3)]
        nact, ndve = (CH + 1) // 2, CH // 2

        def rows(tile):
            return P if tile < NT - 1 else LAST

        def landed(n, i):
            return 16 * (n + 1 + (min(n + 1, KF[0]) if i == NPIECE - 1 else 0))

        block = ctx.enter_context(nc.Block())

        @block.sync
        def _(sp):
            stored = 0
            for layer, k in enumerate(KF):
                for j in range(k):
                    n = first[layer] + j
                    if n:
                        sp.wait_ge(parts_set, NPIECE * n)
                    if layer == 0:
                        for i, (a, b) in enumerate(zip(CUTS, CUTS[1:])):
                            full = min(b, NT - 1)
                            sp.dma_start(h_in[:, a:full, :], io["x"][a * P:full * P, j * P:(j + 1) * P]
                                         .rearrange("(t p) f -> p t f", p=P)).then_inc(h_landed[i], 16)
                        if j == 0:
                            sp.wait_ge(pads_set, 2)
                            sp.dma_start(h_dram[:, LAST:P, NT - 1, :].rearrange("k p f -> p k f"),
                                         y_ring[LAST:P, 0, :].rearrange("p (k f) -> p k f", k=4)).then_inc(pads_out, 16)
                        sp.dma_start(h_in[0:LAST, NT - 1, :],
                                     io["x"][(NT - 1) * P:N, j * P:(j + 1) * P]).then_inc(h_landed[NPIECE - 1], 16)
                    else:
                        for i, (a, b) in enumerate(zip(CUTS, CUTS[1:])):
                            if j == 0:
                                for place in range(3):
                                    sp.wait_ge(h_stored[place], 16 * len(range(place, (layer - 1) * NT + b, 3)))
                                sp.wait_ge(pads_out, 16)
                            sp.dma_start(h_in[:, a:b, :], h_dram[j, :, a:b, :]).then_inc(h_landed[i], 16)
                chunks_in = 0

                def load_aggregates(g):
                    nonlocal chunks_in
                    a, b = g * GN, min(N, (g + 1) * GN)
                    while chunks_in < CH and CS[chunks_in] < b:
                        sp.wait_ge(agg_stored[chunks_in], 16 * first[layer + 1])
                        chunks_in += 1
                    sp.dma_start(agg_in[g % 3][:, 0:k, 0:b - a],
                                 agg_dram[0:k, :, a:b].rearrange("k p n -> p k n")).then_inc(group_landed[g % 3], 16)

                for j in range(k):
                    n = first[layer] + j
                    if n == first[layer] + k - 1:
                        sp.wait_ge(agg_ready, CH * n)
                        sp.dma_start(bias, weights[layer][1].rearrange("(o n) -> o n", o=1)
                                     .to_broadcast([P, H])).then_inc(bias_landed, 16)
                        for half in range(k // 2):
                            halves = first[layer] // 2 + half
                            if half:
                                sp.wait_ge(w_lo_set, halves)
                            sp.dma_start(w_in, weights[layer][0].rearrange("(k p) n -> p k n", p=P)
                                         [:, 2 * half:2 * half + 2, :]).then_inc(w_landed, 16)
                    for c in range(CH):
                        if c % 2:
                            sp.wait_ge(agg_out_dve, n * ndve + c // 2 + 1)
                        else:
                            sp.wait_ge(agg_out_act, n * nact + c // 2 + 1)
                        sp.dma_start(agg_dram[j, :, CS[c]:CS[c + 1]],
                                     agg_st[:, CS[c]:CS[c + 1]]).then_inc(agg_stored[c], 16)
                        if j == k - 1 and c == CH // 2:
                            load_aggregates(0)
                for g in range(NG + 3):
                    if 0 < g < NG:
                        if g >= 3:
                            sp.wait_ge(agg_lo_set, layer * NT + (g - 2) * LT)
                        load_aggregates(g)
                    if layer == 2 and g < NG:
                        tiles = range(g * LT, min(NT, (g + 1) * LT))
                        if tiles[-1] == NT - 1:
                            assert len(tiles) == 1
                            sp.dma_start(x2[0:LAST, NT - 1, :], io["x"][(NT - 1) * P:N, :]).then_inc(group_landed[g % 3], 16)
                        else:
                            sp.dma_start(x2[:, tiles[0]:tiles[-1] + 1, :], io["x"][tiles[0] * P:(tiles[-1] + 1) * P, :]
                                         .rearrange("(t p) d -> p t d", p=P)).then_inc(group_landed[g % 3], 16)
                    if layer == 2 and g == 0:
                        sp.dma_start(wfc, io["L0_gnn_Wfc"].rearrange("(k p) n -> p k n", p=P)).then_inc(heads_landed, 16)
                        sp.dma_start(bfc, io["L0_gnn_bfc"].rearrange("(o n) -> o n", o=1)
                                     .to_broadcast([P, D])).then_inc(heads_landed, 16)
                        sp.dma_start(gate_w, io["L0_ffn_gate_w"].rearrange("(k p) e -> p k e", p=P)).then_inc(heads_landed, 16)
                        sp.dma_start(gate_b, io["L0_ffn_gate_b"].rearrange("(o e) -> o e", o=1)
                                     .to_broadcast([P, NE])).then_inc(heads_landed, 16)
                    if layer == 2 and 3 <= g < 5:
                        e = g - 3
                        sp.dma_start(z["w1_in"][:, e, :, :],
                                     io["L0_ffn_w1"][e].rearrange("(k p) f -> p k f", p=P)).then_inc(t["w1_landed"][e], 16)
                    if layer == 2 and g == 5:
                        sp.dma_start(z["b2"], io["L0_ffn_b2"].rearrange("(o e) d -> o (e d)", o=1)
                                     .to_broadcast([P, NE * D])).then_inc(t["b_landed"], 16)
                        sp.dma_start(z["b1_rows"],
                                     io["L0_ffn_b1"].rearrange("e (m f) -> (e m) f", f=P)).then_inc(t["b_landed"], 16)
                        sp.dma_start(z["w2_in"], io["L0_ffn_w2"][0].rearrange("(k p) d -> p k d", p=P)
                                     ).then_inc(t["w2_landed"], 16)
                    if layer == 2 and g == 7:
                        sp.wait_ge(zeros_set, 1)
                        full = SLOTS // P * P
                        sp.dma_start(t["slots_in"][0:full, :].rearrange("(a p) d -> p a d", p=P),
                                     zeros.rearrange("p (a d) -> p a d", a=1).to_broadcast([P, SLOTS // P, ROW])
                                     ).then_inc(slots_blank, 16)
                        sp.dma_start(t["slots_in"][full:SLOTS, :], zeros[0:SLOTS - full, :]).then_inc(slots_blank, 16)
                    if g >= 3 and layer < 2:
                        for tile in range((g - 3) * LT, min(NT, (g - 2) * LT)):
                            m = rows(tile)
                            sp.wait_ge(relu_out, layer * NT + tile + 1)
                            sp.dma_start(h_dram[:, 0:m, tile, :].rearrange("k p f -> p k f"),
                                         h_ring[0:m, stored % 3, :].rearrange("p (k f) -> p k f", k=4)
                                         ).then_inc(h_stored[stored % 3], 16)
                            stored += 1
            sp.wait_ge(slots_blank, 32)

        @block.gpsimd
        def _(pool):
            pool.memset(h_in[:, NT - 1, :], 0.0).then_inc(pads_set, 1)
            pool.memset(y_ring[:, 0, :], 0.0).then_inc(pads_set, 1)
            pool.memset(scale[:, 0, 0:1], 1024.0).then_inc(pads_set, 1)
            pool.memset(scale[:, 0, 1:2], 1.0 / 1024.0).then_inc(pads_set, 1)
            pool.memset(peak[:, :], 0.0).then_inc(pads_set, 1)
            for layer, k in enumerate(KF):
                if layer == 2:
                    pool.wait_ge(agg_ready, CH * len(blocks))
                    pool.memset(zeros, 0.0).then_inc(zeros_set, 1)
                    pool.memset(logits[:, :, :], 0.0).then_inc(zeros_set, 1)
                for tile in range(NT if layer < 2 else NT + 3):
                    if tile < NT:
                        m = rows(tile)
                        at = layer * NT + tile
                        a = tile % LT * P
                        pool.wait_ge(agg_hi_set, at + 1)
                        if at >= 3:
                            pool.wait_ge(z_ready, at - 2)
                        hi, lo = agg_parts[at % 3]
                        pool.tensor_tensor(lo[:, 0:k, 0:m], agg_in[tile // LT % 3][:, 0:k, a:a + m],
                                           hi[:, 0:k, 0:m].bitcast(F32), ALU.subtract).then_inc(agg_lo_set, 1)
                    if layer == 2 and tile >= 3:
                        m = rows(tile - 3)
                        if tile == 3:
                            pool.wait_ge(heads_landed, 64)
                        pool.tensor_tensor(x2[0:m, tile - 3, :], x2[0:m, tile - 3, :], bfc[0:m, :],
                                           ALU.add).then_inc(xb_set, 1)
                if layer < 2:
                    pool.wait_ge(peak_row, layer + 1)
                    pool.partition_all_reduce(peak_all[:, :], peak_1[:, :], P, RMAX).then_inc(peak_found, 1)

        @block.vector
        def _(dve):
            done = [0]

            def then(ins):
                done[0] += 1
                ins.then_inc(conv_step, 1)
                dve.wait_ge(conv_step, done[0])

            def aggregate_out(n, layer):
                for c in range(1, CH, 2):
                    dve.wait_ge(agg_ready, CH * n + c + 1)
                    if n:
                        dve.wait_ge(agg_stored[c], 16 * n)
                    dve.tensor_scalar(agg_st[:, CS[c]:CS[c + 1]], banks[:, c, 0:CS[c + 1] - CS[c]],
                                      scale[:, layer, 1:2], None, ALU.mult).then_inc(agg_out_dve, 1)

            def residual(tile):
                m = rows(tile)
                dve.wait_ge(xb_set, tile + 1)
                dve.wait_ge(o_ready, tile + 1)
                dve.tensor_tensor(x2[0:m, tile, :], banks[0:m, 4 + tile % 2, 0:D], x2[0:m, tile, :],
                                  ALU.add).then_inc(x2_set, 1)
                dve.wait_ge(x2_set, tile + 1)
                then(dve.bn_stats(stats2[0:m, tile, :], x2[0:m, tile, :]))
                then(dve.bn_aggr(mean_var2[0:m, tile, :], stats2[0:m, tile, :]))
                dve.tensor_scalar(var2[0:m, tile:tile + 1], mean_var2[0:m, tile, 1:2], 1e-5, None,
                                  ALU.add).then_inc(var_set, 1)

            def normed(tile):
                m = rows(tile)
                v, root, r, a = (arr[0:m, tile:tile + 1] for arr in (var2, root2, rstd2, newton2))
                dve.wait_ge(root_set, tile + 1)
                then(dve.reciprocal(r, root))
                then(dve.tensor_tensor(a, r, r, ALU.mult))
                then(dve.scalar_tensor_tensor(out=a, in0=a, scalar=-0.5, in1=v, op0=ALU.mult, op1=ALU.mult))
                then(dve.scalar_tensor_tensor(out=r, in0=a, scalar=1.5, in1=r, op0=ALU.add, op1=ALU.mult))
                dve.tensor_scalar(xn2[0:m, tile, 0:D], x2[0:m, tile, :], mean_var2[0:m, tile, 0:1], r,
                                  ALU.subtract, ALU.mult).then_inc(xn_set, 1)

            then(dve.tensor_tensor(rstd[:, :], rstd[:, :], dinv[:, :], ALU.mult))
            dve.wait_ge(pads_set, 5)
            for layer, k in enumerate(KF):
                for j in range(k):
                    n = first[layer] + j
                    for i, (a, b) in enumerate(zip(CUTS, CUTS[1:])):
                        dve.wait_ge(h_landed[i], landed(n, i))
                        if layer == 0:
                            for tile in range(a, b):
                                last = dve.tensor_scalar(h_in[:, tile, :], h_in[:, tile, :], mean_var[:, tile, 0:1],
                                                         rstd[:, tile:tile + 1], ALU.subtract, ALU.mult)
                            last.then_inc(norm_set, 1)
                        dve.wait_ge(hi_set, NPIECE * n + i + 1)
                        dve.scalar_tensor_tensor(out=parts[n % 2][:, 1, a:b, :], in0=h_in[:, a:b, :],
                                                 scalar=scale[:, layer, 0:1], in1=parts[n % 2][:, 0, a:b, :],
                                                 op0=ALU.mult, op1=ALU.subtract).then_inc(parts_set, 1)
                    if j:
                        aggregate_out(n - 1, layer)
                for half in range(k // 2):
                    halves = first[layer] // 2 + half + 1
                    dve.wait_ge(w_hi_set, halves)
                    dve.tensor_tensor(w_lo[:, 2 * half:2 * half + 2, :], w_in,
                                      w_hi[:, 2 * half:2 * half + 2, :].bitcast(F32), ALU.subtract).then_inc(w_lo_set, 1)
                aggregate_out(first[layer + 1] - 1, layer)
                dve.wait_ge(bias_landed, 16 * (layer + 1))
                for tile in range(NT + 4):
                    if tile < NT:
                        m = rows(tile)
                        at = layer * NT + tile
                        dve.wait_ge(z_ready, at + 1)
                        if at >= 2:
                            dve.wait_ge(relu_out, at - 1)
                        if tile < 2:
                            for c in range(CH):
                                dve.wait_ge(agg_stored[c], 16 * first[layer + 1])
                        dve.scalar_tensor_tensor(out=y_ring[0:m, at % 2, :], in0=banks[0:m, tile % 2, :],
                                                 scalar=dinv[0:m, tile:tile + 1], in1=bias[0:m, :],
                                                 op0=ALU.mult, op1=ALU.add).then_inc(z_out, 1)
                    if layer < 2 and 1 <= tile <= NT:
                        m = rows(tile - 1)
                        at = layer * NT + tile - 1
                        dve.wait_ge(relu_out, at + 1)
                        dve.tensor_reduce(peak[0:m, tile - 1:tile], h_ring[0:m, at % 3, :], AX.X,
                                          ALU.max).then_inc(peak_set, 1)
                    if layer == 2 and tile == 1:
                        dve.wait_ge(wfc_hi_set, 1)
                        dve.tensor_tensor(wfc_lo[:, :, :], wfc, wfc_hi[:, :, :].bitcast(F32),
                                          ALU.subtract).then_inc(wfc_lo_set, 1)
                    if layer == 2 and 0 <= tile - 1 < NT:
                        m = rows(tile - 1)
                        hi, lo = h3t_parts[(tile - 1) % 2]
                        dve.wait_ge(h3t_hi_set, tile)
                        dve.tensor_tensor(lo[:, :, 0:m],
                                          banks[:, 2 + (tile - 1) % 2, :].rearrange("p (k m) -> p k m", k=4)[:, :, 0:m],
                                          hi[:, :, 0:m].bitcast(F32), ALU.subtract).then_inc(h3t_lo_set, 1)
                    if layer == 2 and 0 <= tile - 2 < NT:
                        residual(tile - 2)
                    if layer == 2 and 0 <= tile - 3 < NT:
                        normed(tile - 3)
                if layer < 2:
                    dve.wait_ge(peak_set, (layer + 1) * NT)
                    dve.tensor_reduce(peak_1[:, :], peak[:, :], AX.X, ALU.max).then_inc(peak_row, 1)
                    dve.wait_ge(peak_found, layer + 1)
                    then(dve.tensor_scalar(expo[:, 0:1], peak_all[:, :].bitcast(I32), 23, None,
                                           ALU.logical_shift_right))
                    then(dve.tensor_scalar(expo[:, 1:2], expo[:, 0:1], -1.0, 268.0, ALU.mult, ALU.add))
                    then(dve.tensor_scalar(expo[:, 1:2], expo[:, 1:2], 253.0, None, ALU.min))
                    then(dve.tensor_scalar(expo[:, 2:3], expo[:, 1:2], -1.0, 254.0, ALU.mult, ALU.add))
                    dve.tensor_scalar(scale[:, layer + 1, :].bitcast(I32), expo[:, 1:3], 23, None,
                                      ALU.logical_shift_left).then_inc(scale_set, 1)
            dve.wait_ge(zeros_set, 2)
            for a, b, m in ((0, NT - 1, P), (NT - 1, NT, LAST)):
                dve.wait_ge(logit_ready, NT)
                dve.tensor_tensor(logits[0:m, a:b, :],
                                  banks[0:m, 7, a * NE:b * NE].rearrange("p (t e) -> p t e", e=NE),
                                  gate_b[0:m, :].rearrange("p (o e) -> p o e", o=1).to_broadcast([m, b - a, NE]),
                                  ALU.add).then_inc(conv_step, 1)

        @block.scalar
        def _(act):
            def aggregate_out(n, layer):
                for c in range(0, CH, 2):
                    act.wait_ge(agg_ready, CH * n + c + 1)
                    if n:
                        act.wait_ge(agg_stored[c], 16 * n)
                    else:
                        act.wait_ge(pads_out, 16)
                    act.activation(agg_st[:, CS[c]:CS[c + 1]], banks[:, c, 0:CS[c + 1] - CS[c]], ACT.Copy,
                                   scale=scale[:, layer, 1:2]).then_inc(agg_out_act, 1)

            def agg_high(layer, tile):
                m = rows(tile)
                at = layer * NT + tile
                g = tile // LT
                a = tile % LT * P
                if tile < 3 and agg_parts[at % 3] is agg_parts[0]:
                    for c in range(CH):
                        act.wait_ge(agg_stored[c], 16 * first[layer + 1])
                act.wait_ge(group_landed[g % 3], 16 * (layer * len(range(g % 3, NG, 3)) + (g // 3 + 1) * (1 + layer // 2)))
                if at >= 3:
                    act.wait_ge(z_ready, at - 2)
                act.activation(agg_parts[at % 3][0][:, 0:KF[layer], 0:m], agg_in[g % 3][:, 0:KF[layer], a:a + m],
                               ACT.Copy).then_inc(agg_hi_set, 1)

            def turned_out(tile):
                m = rows(tile)
                act.wait_ge(h3_turned, tile + 1)
                if tile >= 2:
                    act.wait_ge(o_ready, tile - 1)
                act.activation(h3t_parts[tile % 2][0][:, :, 0:m],
                               banks[:, 2 + tile % 2, :].rearrange("p (k m) -> p k m", k=4)[:, :, 0:m],
                               ACT.Copy).then_inc(h3t_hi_set, 1)

            def root(tile):
                m = rows(tile)
                act.wait_ge(var_set, tile + 1)
                act.activation(root2[0:m, tile:tile + 1], var2[0:m, tile:tile + 1], ACT.Sqrt).then_inc(root_set, 1)

            def xn_out(tile):
                m = rows(tile)
                act.wait_ge(xn_turned, tile + 1)
                if tile >= 2:
                    act.wait_ge(logit_ready, tile - 1)
                act.activation(xnt[:, tile % 2, :, 0:m],
                               banks[:, 6, :].rearrange("p (r k m) -> p r k m", r=2, k=2)[:, tile % 2, :, 0:m],
                               ACT.Copy).then_inc(xnt_set, 1)

            act.wait_ge(pads_set, 5)
            for layer, k in enumerate(KF):
                if layer:
                    act.wait_ge(scale_set, layer)
                for j in range(k):
                    n = first[layer] + j
                    for i, (a, b) in enumerate(zip(CUTS, CUTS[1:])):
                        act.wait_ge(h_landed[i], landed(n, i))
                        if layer == 0:
                            act.wait_ge(norm_set, NPIECE * n + i + 1)
                        if n >= 2:
                            act.wait_ge(agg_ready, CH * (n - 1))
                        act.activation(parts[n % 2][:, 0, a:b, :], h_in[:, a:b, :], ACT.Copy,
                                       scale=scale[:, layer, 0:1]).then_inc(hi_set, 1)
                    if j:
                        aggregate_out(n - 1, layer)
                act.wait_ge(parts_set, NPIECE * first[layer + 1])
                for half in range(k // 2):
                    act.wait_ge(w_landed, 16 * (first[layer] // 2 + half + 1))
                    act.activation(w_hi[:, 2 * half:2 * half + 2, :], w_in, ACT.Copy).then_inc(w_hi_set, 1)
                aggregate_out(first[layer + 1] - 1, layer)
                agg_high(layer, 0)
                agg_high(layer, 1)
                for tile in range(NT + 5):
                    m = rows(tile)
                    at = layer * NT + tile
                    if tile + 2 < NT:
                        agg_high(layer, tile + 2)
                    if tile < NT:
                        act.wait_ge(z_out, at + 1)
                    if tile >= NT:
                        pass
                    elif layer < 2:
                        if at >= 3:
                            act.wait_ge(h_stored[at % 3], 16 * (at // 3))
                            act.wait_ge(peak_set, at - 2)
                        act.activation(h_ring[0:m, at % 3, :], y_ring[0:m, at % 2, :], ACT.Relu,
                                       scale=dinv[0:m, tile:tile + 1]).then_inc(relu_out, 1)
                    else:
                        if tile >= 3:
                            act.wait_ge(h3_turned, tile - 2)
                        else:
                            act.wait_ge(h_stored[at % 3], 16 * (at // 3))
                            act.wait_ge(peak_set, 2 * NT)
                        act.activation(h_ring[0:m, at % 3, :], y_ring[0:m, at % 2, :],
                                       ACT.Relu).then_inc(relu_out, 1)
                    if layer == 2:
                        if tile == 1:
                            act.wait_ge(heads_landed, 64)
                            act.activation(wfc_hi[:, :, :], wfc, ACT.Copy).then_inc(wfc_hi_set, 1)
                        if 0 <= tile - 1 < NT:
                            turned_out(tile - 1)
                        if 0 <= tile - 3 < NT:
                            root(tile - 3)
                        if 0 <= tile - 4 < NT:
                            xn_out(tile - 4)

        @block.tensor
        def _(pe):
            def turn_h3(tile):
                m = rows(tile)
                pe.wait_ge(relu_out, 2 * NT + tile + 1)
                if tile >= 2:
                    pe.wait_ge(h3t_lo_set, tile - 1)
                for kk in range(4):
                    mm = pe.transpose(banks[:, 2 + tile % 2, kk * P:kk * P + m],
                                      h_ring[0:m, (2 * NT + tile) % 3, kk * P:(kk + 1) * P], ident[0:m, 0:m])
                mm.then_inc(h3_turned, 1)

            def head(tile):
                m = rows(tile)
                if tile == 0:
                    pe.wait_ge(wfc_lo_set, 1)
                pe.wait_ge(h3t_lo_set, tile + 1)
                if tile >= 2:
                    pe.wait_ge(x2_set, tile - 1)
                hi, lo = h3t_parts[tile % 2]
                for kk in range(4):
                    for a, b in ((hi, wfc_hi), (hi, wfc_lo), (lo, wfc_hi)):
                        mm = pe.matmul(banks[0:m, 4 + tile % 2, 0:D], a[:, kk, 0:m], b[:, kk, :],
                                       start=(kk == 0 and a is hi and b is wfc_hi), stop=(kk == 3 and a is lo))
                mm.then_inc(o_ready, 1)

            def turn_xn(tile):
                m = rows(tile)
                pe.wait_ge(xn_set, tile + 1)
                if tile:
                    pe.wait_ge(xnt_set, tile)
                for kk in range(2):
                    mm = pe.transpose(banks[:, 6, (tile % 2) * 2 * P + kk * P:(tile % 2) * 2 * P + kk * P + m],
                                      xn2[0:m, tile, kk * P:(kk + 1) * P], ident[0:m, 0:m])
                mm.then_inc(xn_turned, 1)

            def gate(tile):
                m = rows(tile)
                pe.wait_ge(xnt_set, tile + 1)
                for kk in range(2):
                    mm = pe.matmul(banks[0:m, 7, tile * NE:(tile + 1) * NE], xnt[:, tile % 2, kk, 0:m],
                                   gate_w[:, kk, :], start=(kk == 0), stop=(kk == 1))
                mm.then_inc(logit_ready, 1)

            for layer, k in enumerate(KF):
                for j in range(k):
                    n = first[layer] + j
                    pe.wait_ge(parts_set, NPIECE * n + 1)
                    for c in range(CH):
                        if n:
                            pe.wait_ge(agg_out_dve if c % 2 else agg_out_act,
                                       (n - 1) * (ndve if c % 2 else nact) + c // 2 + 1)
                        for part in range(2):
                            pe.matmul(banks[:, c, 0:CS[c + 1] - CS[c]], parts[n % 2][:, part, 0, :],
                                      AT[:, 0, CS[c]:CS[c + 1]], start=(part == 0), stop=False)
                    for i in range(NPIECE):
                        if i:
                            pe.wait_ge(parts_set, NPIECE * n + i + 1)
                        with pe.Fori(max(1, CUTS[i]), min(NT - 1, CUTS[i + 1])) as d:
                            for part in range(2):
                                for c in range(CH):
                                    pe.matmul(banks[:, c, 0:CS[c + 1] - CS[c]],
                                              parts[n % 2][:, part, bass.ds(d, 1), :].rearrange("p a f -> p (a f)"),
                                              AT[:, bass.ds(d, 1), CS[c]:CS[c + 1]].rearrange("p a n -> p (a n)"),
                                              start=False, stop=False)
                    for c in range(CH):
                        for part in range(2):
                            mm = pe.matmul(banks[:, c, 0:CS[c + 1] - CS[c]], parts[n % 2][:, part, NT - 1, :],
                                           AT[:, NT - 1, CS[c]:CS[c + 1]], start=False, stop=(part == 1))
                        mm.then_inc(agg_ready, 1)
                pe.wait_ge(agg_out_act, first[layer + 1] * nact)
                pe.wait_ge(agg_out_dve, first[layer + 1] * ndve)
                pe.wait_ge(w_lo_set, first[layer + 1] // 2)
                for tile in range(NT if layer < 2 else NT + 5):
                    if tile < NT:
                        m = rows(tile)
                        at = layer * NT + tile
                        pe.wait_ge(agg_lo_set, at + 1)
                        if tile >= 2:
                            pe.wait_ge(z_out, at - 1)
                        hi, lo = agg_parts[at % 3]
                        for kk in range(k):
                            for a, b in ((hi, w_hi), (hi, w_lo), (lo, w_hi)):
                                mm = pe.matmul(banks[0:m, tile % 2, :], a[:, kk, 0:m], b[:, kk, :],
                                               start=(kk == 0 and b is w_hi and a is hi),
                                               stop=(kk == k - 1 and a is lo))
                        mm.then_inc(z_ready, 1)
                    if layer == 2:
                        for stage, lag in ((turn_h3, 1), (head, 2), (turn_xn, 4), (gate, 5)):
                            if 0 <= tile - lag < NT:
                                stage(tile - lag)


def experts(nc, io, t):
    with ExitStack() as ctx:
        def sem(name):
            return ctx.enter_context(nc.semaphore(name))

        work, ident, logits, z = t["work"], t["ident"], t["logits"], t["free"]
        slots_in, slots_out = t["slots_in"], t["slots_out"]
        x2, xn2, w1_in, w2_in, b2, b1_rows, b1t = (z[n] for n in ("x2", "xn2", "w1_in", "w2_in", "b2", "b1_rows", "b1t"))
        w1_parts = [[z["w1_hi_0"], z["w1_lo_0"]], [z["w1_hi_1"], z["w1_lo_1"]]]
        w2_hi, w2_lo = z["w2_hi"], z["w2_lo"]
        xst_hi, xst_lo = (t["xst_parts"][:, n] for n in range(2))
        hid_hi, hid_lo = t["hid_parts"]
        hid_full, y_st = z["hid_full"], z["y_st"]
        tri, ones, e_less, e_valid = z["tri"], z["ones"], z["e_less"], z["e_valid"]
        back = xn2[:, :, 0:D]

        a = 2 * FM * CE + 4 * CE
        xs = [work[:, a + n * ST * ROW:a + (n + 1) * ST * ROW].rearrange("p (s d) -> p s d", s=ST) for n in range(2)]
        after_xn = xn2.rearrange("p t d -> p (t d)")[:, 0:4 * ST * D].rearrange("p (n s d) -> p n s d", n=4, s=ST)
        x_rows, out_rows = after_xn[:, 0:2], after_xn[:, 2:4]
        nobody, filled, slot_token, token_idx = t["nobody"], t["filled"], t["slot_token"], t["token_idx"]
        x2_dram = t["x2_dram"]
        gate_words = [0]

        def small(*shape, dt=F32):
            n = int(np.prod(shape))
            lo = gate_words[0]
            gate_words[0] += n
            v = work[:, lo:lo + n]
            v = v if dt is F32 else v.bitcast(dt)
            return v if len(shape) == 1 else v.rearrange("p (t e) -> p t e", e=shape[1])

        less, ex, pr, eq, cand, ranks = (small(NT, NE) for _ in range(6))
        top, total, inv, idx8, pos, kept, place, token, target = (small(NT) for _ in range(9))
        hot16 = small(NT * NE // 2).bitcast(F16)
        hot = hot16.rearrange("p (t e) -> p t e", e=NE)
        scatter_idx, gather_idx = t["scatter_idx"], t["gather_idx"]
        prob, weight, finite, finite_1, bad = (t[n] for n in ("prob", "weight", "finite", "finite_1", "bad"))

        banks = ctx.enter_context(nc.psum_tensor("expert_banks", [P, 8, 512], F32))

        consts_set, pool_step, gate_step = sem("ffn_consts_set"), sem("ffn_pool_step"), sem("gate_step")
        less_set, ex_set, hot_set, counted = sem("less_set"), sem("ex_set"), sem("hot_set"), sem("counted")
        target_set, scattered = sem("target_set"), sem("scattered")
        b1_turned, b1_set = sem("b1_turned"), sem("b1_set")
        xs_landed = [sem("xs_landed_0"), sem("xs_landed_1")]
        xs_turned, xst_pad = sem("xs_turned"), sem("xst_pad")
        xst_hi_set, xst_lo_set = sem("xst_hi_set"), sem("xst_lo_set")
        w1_hi_set, w1_lo_set, w2_hi_set, w2_lo_set = (sem(f"ffn_{n}_set") for n in ("w1_hi", "w1_lo", "w2_hi", "w2_lo"))
        hid_ready, hid_full_set = sem("hid_ready"), sem("hid_full_set")
        hid_hi_set, hid_lo_set = sem("hid_hi_set"), sem("hid_lo_set")
        y_ready, y_out, y_stored = sem("y_ready"), sem("y_out"), sem("y_stored")
        finite_set, bad_row, bad_found, bad_set = sem("finite_set"), sem("bad_row"), sem("bad_found"), sem("bad_set")
        gathered = [sem(f"gathered_{i}") for i in range(NT)]
        x_saved, x_shown = sem("x_saved"), sem("x_shown")
        x_rows_blank, token_idx_set, slot_step = sem("x_rows_blank"), sem("token_idx_set"), sem("slot_step")
        x_rows_in, out_rows_set, out_rows_out = [sem("x_rows_in_0"), sem("x_rows_in_1")], sem("out_rows_set"), sem("out_rows_out")
        sum_set, out_stored, guard_step = sem("sum_set"), sem("out_stored"), sem("guard_step")

        def rows(tile):
            return P if tile < NT - 1 else LAST

        def slot_rows(s):
            return min(P, C - s * P)

        def whole(dram, e, tiles):
            if tiles == "full":
                return dram[e * C:e * C + (ST - 1) * P, :].rearrange("(s p) d -> p s d", p=P)
            return dram[e * C + (ST - 1) * P:(e + 1) * C, :]

        block = ctx.enter_context(nc.Block())

        @block.sync
        def _(sp):
            def load_slots(e):
                if e >= 2:
                    sp.wait_ge(out_rows_set, ST * (e - 1))
                sp.dma_start(xs[e % 2][:, 0:ST - 1, :], whole(slots_in, e, "full")).then_inc(xs_landed[e % 2], 16)
                sp.dma_start(xs[e % 2][0:slot_rows(ST - 1), ST - 1, :],
                             whole(slots_in, e, "rest")).then_inc(xs_landed[e % 2], 16)

            for dram, done in ((x2_dram, x_saved), (io["out"], x_shown)):
                sp.dma_start(dram[0:(NT - 1) * P, :].rearrange("(t p) d -> p t d", p=P),
                             x2[:, 0:NT - 1, :]).then_inc(done, 16)
                sp.dma_start(dram[(NT - 1) * P:N, :], x2[0:LAST, NT - 1, :]).then_inc(done, 16)
            sp.wait_ge(scattered, 16 * NT)
            load_slots(0)
            load_slots(1)
            for e in range(NE):
                if e + 2 < NE:
                    sp.wait_ge(w1_lo_set, 2 * (e + 1))
                    sp.dma_start(w1_in[:, e % 2, :, :], io["L0_ffn_w1"][e + 2].rearrange("(k p) f -> p k f", p=P)
                                 ).then_inc(t["w1_landed"][e % 2], 16)
                if e + 1 < NE:
                    sp.wait_ge(w2_lo_set, 2 * (e + 1))
                    sp.dma_start(w2_in, io["L0_ffn_w2"][e + 1].rearrange("(k p) d -> p k d", p=P)
                                 ).then_inc(t["w2_landed"], 16)
                sp.wait_ge(y_out, ST * (e + 1))
                sp.dma_start(whole(slots_out, e, "full"), y_st[:, 0:ST - 1, :]).then_inc(y_stored, 16)
                sp.dma_start(whole(slots_out, e, "rest"),
                             y_st[0:slot_rows(ST - 1), ST - 1, :]).then_inc(y_stored, 16)
                if e + 2 < NE:
                    load_slots(e + 2)
            sp.wait_ge(y_stored, 32 * NE)
            sp.wait_ge(out_rows_out, 16 * ST * NE)
            sp.wait_ge(bad_set, 1)
            flag = sp.value_load(t["bad_i"][0:1, 0:1], min_val=0, max_val=1)
            with sp.If(flag > 0):
                for tile in range(NT):
                    m = rows(tile)
                    sp.wait_ge(sum_set, tile + 1)
                    sp.dma_start(io["out"][tile * P:tile * P + m, :], x2[0:m, tile, :]).then_inc(out_stored, 16)
                sp.wait_ge(out_stored, 16 * NT)

        @block.gpsimd
        def _(pool):
            if CE > C:
                for part in (xst_hi, xst_lo):
                    pool.memset(part[:, :, C:CE].bitcast(F32), 0.0).then_inc(xst_pad, 1)
            pool.iota(e_less, [[0, NT], [1, NE]], base=-NE, channel_multiplier=0,
                      allow_small_or_imprecise_dtypes=True).then_inc(consts_set, 1)
            pool.iota(token, [[P, NT]], base=SLOTS, channel_multiplier=1,
                      allow_small_or_imprecise_dtypes=True).then_inc(consts_set, 1)
            pool.memset(finite[:, :], 0.0).then_inc(consts_set, 1)
            pool.iota(nobody[:, :], [[P, ST]], base=N, channel_multiplier=1,
                      allow_small_or_imprecise_dtypes=True).then_inc(consts_set, 1)
            pool.iota(e_valid, [[0, NT], [1, NE]], base=-NE, channel_multiplier=0,
                      allow_small_or_imprecise_dtypes=True).then_inc(pool_step, 1)
            pool.memset(tri, 1.0).then_inc(pool_step, 1)
            pool.memset(ones, 1.0).then_inc(consts_set, 1)
            pool.wait_ge(pool_step, 2)
            pool.affine_select(out=e_valid[:, NT - 1, :], in_=e_valid[:, NT - 1, :], compare_op=ALU.is_ge, fill=1.0,
                               base=LAST - 1, pattern=[[0, NE]], channel_multiplier=-1).then_inc(consts_set, 1)
            pool.affine_select(out=tri, in_=tri, compare_op=ALU.is_ge, fill=0.0, base=0, pattern=[[1, P]],
                               channel_multiplier=-1).then_inc(consts_set, 1)
            pool.wait_ge(target_set, 4)
            for tile in range(NT):
                m = rows(tile)
                pool.indirect_dma_start(
                    out=slots_in[:, :], out_offset=bass.IndirectOffsetOnAxis(ap=scatter_idx[0:m, tile:tile + 1], axis=0),
                    in_=xn2[0:m, tile, :], in_offset=None, bounds_check=SLOTS - 1, oob_is_err=False,
                ).then_inc(scattered, 16)
            pool.wait_ge(scattered, 16 * NT)
            pool.memset(x_rows, 0.0).then_inc(x_rows_blank, 1)

            def fetch(e):
                pool.wait_ge(token_idx_set, e + 1)
                if e >= 2:
                    pool.wait_ge(out_rows_set, ST * (e - 1))
                for s in range(ST):
                    m = slot_rows(s)
                    pool.indirect_dma_start(
                        out=x_rows[0:m, e % 2, s, :], out_offset=None, in_=x2_dram[:, :],
                        in_offset=bass.IndirectOffsetOnAxis(ap=token_idx[0:m, e % 2, s:s + 1], axis=0),
                        bounds_check=N - 1, oob_is_err=False,
                    ).then_inc(x_rows_in[e % 2], 16)

            pool.wait_ge(x_rows_blank, 1)
            pool.wait_ge(x_saved, 32)
            fetch(0)
            pool.wait_ge(x_shown, 32)
            for e in range(NE):
                if e + 1 < NE:
                    fetch(e + 1)
                for s in range(ST):
                    m = slot_rows(s)
                    pool.wait_ge(out_rows_set, ST * e + s + 1)
                    pool.indirect_dma_start(
                        out=io["out"][:, :],
                        out_offset=bass.IndirectOffsetOnAxis(ap=token_idx[0:m, e % 2, s:s + 1], axis=0),
                        in_=out_rows[0:m, e % 2, s, :], in_offset=None, bounds_check=N - 1, oob_is_err=False,
                    ).then_inc(out_rows_out, 16)
            pool.wait_ge(bad_row, 1)
            pool.partition_all_reduce(bad[:, 1:2], bad[:, 0:1], P, RMAX).then_inc(bad_found, 1)
            pool.wait_ge(bad_set, 1)
            flag = pool.value_load(t["bad_i"][0:1, 0:1], min_val=0, max_val=1)
            with pool.If(flag > 0):
                pool.wait_ge(y_stored, 32 * NE)
                pool.wait_ge(out_rows_out, 16 * ST * NE)
                for tile in range(NT):
                    m = rows(tile)
                    pool.indirect_dma_start(
                        out=back[0:m, tile, :], out_offset=None, in_=slots_out[:, :],
                        in_offset=bass.IndirectOffsetOnAxis(ap=gather_idx[0:m, tile:tile + 1], axis=0),
                    ).then_inc(gathered[tile], 16)

        @block.vector
        def _(dve):
            done = [0]

            def then(ins):
                done[0] += 1
                ins.then_inc(gate_step, 1)
                dve.wait_ge(gate_step, done[0])

            def by_expert(v):
                return v.rearrange("p (t o) -> p t o", o=1).to_broadcast([P, NT, NE])

            then(dve.tensor_reduce(top, logits[:, :, :], AX.X, ALU.max))
            dve.tensor_tensor(less, logits[:, :, :], by_expert(top), ALU.subtract).then_inc(less_set, 1)
            dve.wait_ge(ex_set, 1)
            then(dve.tensor_reduce(total, ex, AX.X, ALU.add))
            then(dve.reciprocal(inv, total))
            then(dve.tensor_tensor(pr, ex, by_expert(inv), ALU.mult))
            then(dve.tensor_reduce(prob[:, :], pr, AX.X, ALU.max))
            then(dve.tensor_tensor(eq, pr, by_expert(prob[:, :]), ALU.is_equal))
            dve.wait_ge(consts_set, 7)
            then(dve.tensor_tensor(cand, eq, e_less, ALU.mult))
            then(dve.tensor_reduce(idx8, cand, AX.X, ALU.min))
            dve.tensor_tensor(hot, e_valid, by_expert(idx8), ALU.is_equal).then_inc(hot_set, 1)
            dve.wait_ge(counted, 1)
            dve.wait_ge(hot_set, 1)
            then(dve.tensor_tensor(ranks, banks[:, 7, 0:NT * NE].rearrange("p (t e) -> p t e", e=NE), hot, ALU.mult))
            then(dve.tensor_reduce(pos, ranks, AX.X, ALU.add))
            then(dve.tensor_scalar(kept, pos, float(C), None, ALU.is_le))
            dve.tensor_tensor(weight[:, :], prob[:, :], kept, ALU.mult)
            then(dve.tensor_scalar(pos, pos, float(C), 1.0, ALU.min, ALU.max))
            then(dve.tensor_scalar(place, idx8, float(C), float(SLOTS - 1), ALU.mult, ALU.add))
            then(dve.tensor_tensor(place, place, pos, ALU.add))
            then(dve.tensor_tensor(target, place, token, ALU.subtract))
            then(dve.tensor_tensor(target, target, kept, ALU.mult))
            then(dve.tensor_tensor(target, target, token, ALU.add))
            dve.tensor_scalar(xn2[:, :, D], token, float(1 - SLOTS), None, ALU.add).then_inc(target_set, 1)
            dve.tensor_copy(xn2[:, :, D + 1], weight[:, :]).then_inc(target_set, 1)
            dve.tensor_scalar(gather_idx[:, :], place, float(SLOTS - 1), None, ALU.min).then_inc(target_set, 1)
            dve.tensor_copy(scatter_idx[:, :], target).then_inc(target_set, 1)
            dve.wait_ge(b1_turned, 1)
            dve.tensor_copy(b1t, banks[:, 5, 0:NE * FM]).then_inc(b1_set, 1)

            def xst_low(e):
                for k in range(2):
                    dve.wait_ge(xst_hi_set, 2 * e + k + 1)
                    dve.tensor_tensor(xst_lo[:, k, 0:C], banks[:, k, 0:C], xst_hi[:, k, 0:C].bitcast(F32),
                                      ALU.subtract).then_inc(xst_lo_set, 1)

            def w1_low(e, k):
                dve.wait_ge(w1_hi_set, e + 1)
                dve.tensor_tensor(w1_parts[e % 2][1][:, k, :], w1_in[:, e % 2, k, :],
                                  w1_parts[e % 2][0][:, k, :].bitcast(F32), ALU.subtract).then_inc(w1_lo_set, 1)

            slot_steps = [0]

            def tokens_of(e):
                def then_slot(ins):
                    slot_steps[0] += 1
                    ins.then_inc(slot_step, 1)
                    dve.wait_ge(slot_step, slot_steps[0])

                dve.wait_ge(xs_landed[e % 2], 32 * (e // 2 + 1))
                if e >= 2:
                    dve.wait_ge(out_rows_out, 16 * ST * (e - 1))
                then_slot(dve.tensor_scalar(filled[:, :], xs[e % 2][:, :, D], 0.0, None, ALU.is_gt))
                then_slot(dve.scalar_tensor_tensor(out=slot_token[:, :], in0=xs[e % 2][:, :, D], scalar=-1.0,
                                                   in1=nobody[:, :], op0=ALU.add, op1=ALU.subtract))
                then_slot(dve.tensor_tensor(slot_token[:, :], slot_token[:, :], filled[:, :], ALU.mult))
                dve.tensor_tensor(token_idx[:, e % 2, :], slot_token[:, :], nobody[:, :], ALU.add).then_inc(token_idx_set, 1)
                dve.wait_ge(token_idx_set, e + 1)

            w1_low(0, 0)
            w1_low(0, 1)
            tokens_of(0)
            xst_low(0)
            for e in range(NE):
                for m in range(FM):
                    g = e * FM + m
                    dve.wait_ge(hid_hi_set, g + 1)
                    dve.tensor_tensor(hid_lo[:, m, 0:C], hid_full[:, g % 3, 0:C], hid_hi[:, m, 0:C].bitcast(F32),
                                      ALU.subtract).then_inc(hid_lo_set, 1)
                    if m < 4:
                        half = slice(m // 2 * FM // 2, (m // 2 + 1) * FM // 2)
                        if m == 0:
                            dve.wait_ge(t["w2_landed"], 16 * (e + 1))
                        if m % 2 == 0:
                            dve.tensor_copy(w2_hi[:, half, :], w2_in[:, half, :]).then_inc(w2_hi_set, 1)
                        else:
                            dve.wait_ge(w2_hi_set, 2 * e + m // 2 + 1)
                            dve.tensor_tensor(w2_lo[:, half, :], w2_in[:, half, :], w2_hi[:, half, :].bitcast(F32),
                                              ALU.subtract).then_inc(w2_lo_set, 1)
                if e + 1 < NE:
                    xst_low(e + 1)
                    tokens_of(e + 1)
                if e == 0:
                    dve.wait_ge(t["b_landed"], 32)
                if e:
                    dve.wait_ge(y_stored, 32 * e)
                for s in range(ST):
                    m = slot_rows(s)
                    dve.wait_ge(y_ready, e * ST + s + 1)
                    dve.tensor_tensor(y_st[0:m, s, :], banks[0:m, 5 + s % 2, 0:D], b2[0:m, e, :],
                                      ALU.add).then_inc(y_out, 1)
                    dve.wait_ge(y_out, e * ST + s + 1)
                    dve.tensor_tensor_reduce(out=z["junk"][0:m, :], in0=y_st[0:m, s, :], in1=z["zeros"][0:m, 0:D],
                                             scale=1.0, scalar=0.0, op0=ALU.mult, op1=ALU.add,
                                             accum_out=finite[0:m, e * ST + s:e * ST + s + 1]).then_inc(finite_set, 1)
                    if s == 0:
                        dve.wait_ge(x_rows_in[e % 2], 16 * ST * (e // 2 + 1))
                        if e >= 2:
                            dve.wait_ge(out_rows_out, 16 * ST * (e - 1))
                    dve.scalar_tensor_tensor(out=out_rows[0:m, e % 2, s, :], in0=y_st[0:m, s, :],
                                             scalar=xs[e % 2][0:m, s, D + 1:D + 2], in1=x_rows[0:m, e % 2, s, :],
                                             op0=ALU.mult, op1=ALU.add).then_inc(out_rows_set, 1)
                    if s < 2 and e + 1 < NE:
                        w1_low(e + 1, s)
            dve.wait_ge(finite_set, NE * ST)
            then(dve.tensor_scalar(finite[:, :], finite[:, :], 0.0, None, ALU.is_equal))
            then(dve.tensor_reduce(finite_1[:, :], finite[:, :], AX.X, ALU.min))
            dve.tensor_scalar(bad[:, 0:1], finite_1[:, :], -1.0, 1.0, ALU.mult, ALU.add).then_inc(bad_row, 1)
            dve.wait_ge(bad_found, 1)
            dve.tensor_copy(t["bad_i"][:, :], bad[:, 1:2]).then_inc(bad_set, 1)
            dve.wait_ge(bad_set, 1)
            flag = dve.value_load(t["bad_i"][0:1, 0:1], min_val=0, max_val=1)
            with dve.If(flag > 0):
                lim = xs[0][:, 0, 0:D]
                mask = xs[0][:, 1, 0:D].bitcast(I32)
                value = xs[0][:, 2, 0:D]
                steps = [0]

                def after(ins):
                    steps[0] += 1
                    ins.then_inc(guard_step, 1)
                    dve.wait_ge(guard_step, steps[0])

                for tile in range(NT):
                    m = rows(tile)
                    dve.wait_ge(gathered[tile], 16)
                    after(dve.tensor_scalar(lim[0:m, :], back[0:m, tile, :], weight[0:m, tile:tile + 1], None, ALU.mult))
                    for op, bound, fill in ((ALU.is_gt, FMAX, 1e4), (ALU.is_lt, -FMAX, -1e4)):
                        dve.memset(value[0:m, :], fill)
                        after(dve.tensor_scalar(mask[0:m, :], lim[0:m, :], bound, None, op))
                        after(dve.copy_predicated(lim[0:m, :], mask[0:m, :], value[0:m, :]))
                    after(dve.tensor_tensor(value[0:m, :], lim[0:m, :], lim[0:m, :], ALU.is_equal))
                    after(dve.tensor_scalar(mask[0:m, :], value[0:m, :], 0.5, None, ALU.is_lt))
                    after(dve.memset(value[0:m, :], 0.0))
                    after(dve.copy_predicated(lim[0:m, :], mask[0:m, :], value[0:m, :]))
                    after(dve.tensor_tensor(x2[0:m, tile, :], lim[0:m, :], x2[0:m, tile, :], ALU.add))
                    dve.sem_inc(sum_set, 1)

        @block.scalar
        def _(act):
            act.wait_ge(less_set, 1)
            act.activation(ex, less, ACT.Exp).then_inc(ex_set, 1)

            def xst_high(e):
                for k in range(2):
                    act.wait_ge(xs_turned, 2 * e + k + 1)
                    act.activation(xst_hi[:, k, 0:C], banks[:, k, 0:C], ACT.Copy).then_inc(xst_hi_set, 1)

            def w1_high(e):
                act.wait_ge(t["w1_landed"][e % 2], 16 * (e // 2 + 1))
                act.activation(w1_parts[e % 2][0][:, :, :], w1_in[:, e % 2, :, :], ACT.Copy).then_inc(w1_hi_set, 1)

            def hid_high(g):
                act.wait_ge(hid_full_set, g + 1)
                act.activation(hid_hi[:, g % FM, 0:C], hid_full[:, g % 3, 0:C], ACT.Copy).then_inc(hid_hi_set, 1)

            w1_high(0)
            xst_high(0)
            act.wait_ge(b1_set, 1)
            for e in range(NE):
                for m in range(FM):
                    g = e * FM + m
                    act.wait_ge(hid_ready, g + 1)
                    if g >= 3:
                        act.wait_ge(hid_lo_set, g - 2)
                    act.activation(hid_full[:, g % 3, 0:C], banks[:, 2 + g % 3, 0:C], ACT.Relu,
                                   bias=b1t[:, g:g + 1]).then_inc(hid_full_set, 1)
                    if m:
                        hid_high(g - 1)
                hid_high(g)
                if e + 1 < NE:
                    xst_high(e + 1)
                    w1_high(e + 1)

        @block.tensor
        def _(pe):
            pe.wait_ge(t["b_landed"], 32)
            pe.transpose(banks[:, 5, 0:NE * FM], b1_rows, ident[0:NE * FM, 0:NE * FM]).then_inc(b1_turned, 1)
            pe.wait_ge(consts_set, 7)
            pe.wait_ge(hot_set, 1)
            pe.matmul(banks[:, 7, 0:NT * NE], tri, hot16, start=True, stop=False, skip_group_check=True)
            for back_by in range(1, NT):
                mm = pe.matmul(banks[:, 7, back_by * NE:NT * NE], ones, hot16[:, 0:(NT - back_by) * NE],
                               start=False, stop=(back_by == NT - 1), skip_group_check=True)
            mm.then_inc(counted, 1)

            def turn_slots(e):
                pe.wait_ge(xs_landed[e % 2], 32 * (e // 2 + 1))
                for k in range(2):
                    if e:
                        pe.wait_ge(xst_lo_set, 2 * (e - 1) + k + 1)
                    for s in range(ST):
                        m = slot_rows(s)
                        mm = pe.transpose(banks[:, k, s * P:s * P + m], xs[e % 2][0:m, s, k * P:(k + 1) * P],
                                          ident[0:m, 0:m])
                    mm.then_inc(xs_turned, 1)

            turn_slots(0)
            for e in range(NE):
                pe.wait_ge(w1_lo_set, 2 * (e + 1))
                pe.wait_ge(xst_lo_set, 2 * e + 2)
                if e == 0 and CE > C:
                    pe.wait_ge(xst_pad, 2)
                w1_hi, w1_lo = w1_parts[e % 2]
                for m in range(FM):
                    g = e * FM + m
                    if g >= 3:
                        pe.wait_ge(hid_full_set, g - 2)
                    for k in range(2):
                        for a, b in ((w1_hi, xst_hi), (w1_hi, xst_lo), (w1_lo, xst_hi)):
                            mm = pe.matmul(banks[:, 2 + g % 3, 0:CE], a[:, k, m * P:(m + 1) * P], b[:, k, :],
                                           start=(k == 0 and a is w1_hi and b is xst_hi),
                                           stop=(k == 1 and a is w1_lo))
                    mm.then_inc(hid_ready, 1)
                if e + 1 < NE:
                    turn_slots(e + 1)
                pe.wait_ge(w2_lo_set, 2 * (e + 1))
                if e == 0:
                    pe.wait_ge(b1_set, 1)
                for s in range(ST):
                    m = slot_rows(s)
                    g = e * ST + s
                    if g >= 2:
                        pe.wait_ge(y_out, g - 1)
                    for k in range(FM):
                        if s == 0:
                            pe.wait_ge(hid_lo_set, e * FM + k + 1)
                        for a, b in ((hid_hi, w2_hi), (hid_hi, w2_lo), (hid_lo, w2_hi)):
                            mm = pe.matmul(banks[0:m, 5 + s % 2, 0:D], a[:, k, s * P:s * P + m], b[:, k, :],
                                           start=(k == 0 and a is hid_hi and b is w2_hi),
                                           stop=(k == FM - 1 and a is hid_lo))
                    mm.then_inc(y_ready, 1)


_INS = ["x", "src", "dst", "L0_gnn_W1", "L0_gnn_b1", "L0_gnn_W2", "L0_gnn_b2", "L0_gnn_W3", "L0_gnn_b3",
        "L0_gnn_Wfc", "L0_gnn_bfc", "L0_ffn_gate_w", "L0_ffn_gate_b", "L0_ffn_w1", "L0_ffn_b1", "L0_ffn_w2",
        "L0_ffn_b2"]


def kernel(**inputs):
    import concourse.bacc as bacc
    from concourse.bass_utils import run_bass_kernel_spmd

    nc = bacc.Bacc("TRN2", target_bir_lowering=False, num_devices=1, dynamic_dma_scratch_size=4096)
    arrays, io = {}, {}
    for name in _INS:
        a = np.ascontiguousarray(inputs[name])
        arrays[f"in_{name}"] = a
        io[name] = nc.dram_tensor(f"in_{name}", a.shape, mybir.dt.from_np(a.dtype), kind="ExternalInput").ap()
    io["out"] = nc.dram_tensor("out", (N, D), F32, kind="ExternalOutput").ap()
    build(nc, io)
    r = run_bass_kernel_spmd(nc, [arrays], core_ids=[0])
    return r.results[0]["out"]
```
